# Optimizing a Trainium2 kernel written in Bass

```python
import numpy as np
import jax
import jax.numpy as jnp

def _softmax(x, axis=-1):
    return jax.nn.softmax(x, axis=axis)

def _gelu(x):
    return jax.nn.gelu(x, approximate=True)

def _silu(x):
    return jax.nn.silu(x)

def _sigmoid(x):
    return jax.nn.sigmoid(x)

def _layernorm(x, axis=-1, eps=1e-05):
    m = jnp.mean(x, axis=axis, keepdims=True)
    v = jnp.var(x, axis=axis, keepdims=True)
    return (x - m) / jnp.sqrt(v + eps)

def _scatter_add(tgt, idx, src, axis=0):
    return tgt.at[idx].add(src)

def _segment_sum(src, seg, n):
    return jax.ops.segment_sum(src, seg, n)
kernel_name = 'mk_adj_resnorm_d4_adj_r2_5aefa1'

def setup_inputs(seed: int=0):
    np.random.seed(seed)
    _w = jnp.asarray

    def _rec_inputs():
        import jax
        import jax.numpy as jnp
        _gk = jax.random.key(seed)
        x = 7.22e-05 + 1 * jax.random.normal(jax.random.fold_in(_gk, 1), (64, 128, 256), jnp.float32)
        _w = (1.0 + jnp.arange(128, dtype=jnp.float32)) ** (-0.5)
        _w = _w / _w.mean()
        _pij = jnp.clip(0.03125 * _w[:, None] * _w[None, :], 0.0, 1.0)
        _a = jax.random.uniform(jax.random.fold_in(_gk, 2), (64, 128, 128)) < _pij
        _a = jnp.logical_or(_a, jnp.swapaxes(_a, -1, -2))
        _a = jnp.logical_or(_a, jnp.eye(128, dtype=bool))
        _af = _a.astype(jnp.float32)
        _af = _af * jax.random.uniform(jax.random.fold_in(_gk, 3), (64, 128, 128), jnp.float32, 0.05, 1)
        adj = _af
        return (x, adj)
    x, adj = _rec_inputs()

    def _L0_gnn_setup():
        import jax, jax.numpy as jnp
        import numpy as np
        EPS_LN = 1e-05

        def hypergraph_conv(x, adj, W, b):
            N, C, _ = adj.shape
            H = (adj != 0).astype(x.dtype)
            w = adj.reshape(N, -1)[:, :C]
            xw = jnp.einsum('ncd,hd->nch', x, W)
            Dn = jnp.einsum('nce,ne->nc', H, w)
            Dn = jnp.where(Dn > 0, 1.0 / Dn, 0.0)
            Be = H.sum(axis=1)
            Be = jnp.where(Be > 0, 1.0 / Be, 0.0)
            m = Be[:, :, None] * jnp.einsum('nce,nch->neh', H, xw)
            out = Dn[:, :, None] * jnp.einsum('nce,neh->nch', H, m)
            return out + b

        def layer_norm(x, g, b):
            mu = jnp.mean(x, axis=-1, keepdims=True)
            var = jnp.var(x, axis=-1, keepdims=True)
            return (x - mu) * jax.lax.rsqrt(var + EPS_LN) * g + b
        key = jax.random.key(seed)
        ks = jax.random.split(key, 4)
        N, C, Din, Dh, Dout = (16, 512, 256, 512, 256)
        x = jax.random.normal(ks[0], (N, C, Din), dtype=jnp.float32)
        adj = jax.random.uniform(ks[1], (N, C, C), dtype=jnp.float32, minval=0.1, maxval=1.0)
        W1 = jax.random.normal(ks[2], (Dh, Din), dtype=jnp.float32) * (1.0 / np.sqrt(Din))
        b1 = jnp.zeros((Dh,), dtype=jnp.float32)
        gamma = jnp.ones((Dh,), dtype=jnp.float32)
        beta = jnp.zeros((Dh,), dtype=jnp.float32)
        W2 = jax.random.normal(ks[3], (Dout, Dh), dtype=jnp.float32) * (1.0 / np.sqrt(Dh))
        b2 = jnp.zeros((Dout,), dtype=jnp.float32)
        return {'x': x, 'adj': adj, 'W1': W1, 'b1': b1, 'gamma': gamma, 'beta': beta, 'W2': W2, 'b2': b2}
    _L0_gnn_all = _L0_gnn_setup()
    _L0_gnn_in = {k: v for k, v in _L0_gnn_all.items() if k in ('W1', 'b1', 'gamma', 'beta', 'W2', 'b2')}
    del _L0_gnn_all

    def _L1_gnn_setup():
        import jax, jax.numpy as jnp
        import numpy as np
        IN_DIM = 256
        ATT_DIM = 64
        B, N = (4, 2048)
        key = jax.random.key(seed)
        k1, k2, k3, k4 = jax.random.split(key, 4)
        x = jax.random.normal(k1, (B, N, IN_DIM), dtype=jnp.float32)
        adj_matrix = (jax.random.uniform(k2, (B, N, N)) < 0.05).astype(jnp.float32)
        W_qk = jax.random.normal(k3, (2 * ATT_DIM, IN_DIM), dtype=jnp.float32) / np.sqrt(IN_DIM)
        W_v = jax.random.normal(k4, (IN_DIM, IN_DIM), dtype=jnp.float32) / np.sqrt(IN_DIM)
        return {'x': x, 'adj_matrix': adj_matrix, 'W_qk': W_qk, 'W_v': W_v}
    _L1_gnn_all = _L1_gnn_setup()
    _L1_gnn_in = {k: v for k, v in _L1_gnn_all.items() if k in ('W_qk', 'W_v')}
    del _L1_gnn_all

    def _L2_gnn_setup():
        import jax, jax.numpy as jnp
        import numpy as np
        B, N, DIN, DOUT, K = (4, 1024, 256, 256, 3)
        key = jax.random.key(seed)
        ks = jax.random.split(key, 8)
        X = jax.random.normal(ks[0], (B, N, DIN), dtype=jnp.float32)
        A = jax.random.uniform(ks[1], (B, N, N), dtype=jnp.float32)
        Wv = jax.random.normal(ks[2], (DIN, DOUT), dtype=jnp.float32) * 0.02
        bv = jax.random.normal(ks[3], (DOUT,), dtype=jnp.float32) * 0.02
        aw = jax.random.normal(ks[4], (2 * DOUT, 1), dtype=jnp.float32) * 0.05
        ab = jax.random.normal(ks[5], (1,), dtype=jnp.float32) * 0.05
        Wk = jax.random.normal(ks[6], (K, DIN, DOUT), dtype=jnp.float32) * 0.02
        bk = jax.random.normal(ks[7], (K, DOUT), dtype=jnp.float32) * 0.02
        return {'X': X, 'A': A, 'Wv': Wv, 'bv': bv, 'aw': aw, 'ab': ab, 'Wk': Wk, 'bk': bk}
    _L2_gnn_all = _L2_gnn_setup()
    _L2_gnn_in = {k: v for k, v in _L2_gnn_all.items() if k in ('Wv', 'bv', 'aw', 'ab', 'Wk', 'bk')}
    del _L2_gnn_all

    def _L3_gnn_setup():
        import jax, jax.numpy as jnp
        import numpy as np
        B, N, D_IN, D_OUT = (4, 2048, 256, 256)
        key = jax.random.key(seed)
        k1, k2, k3, k4 = jax.random.split(key, 4)
        x = jax.random.normal(k1, (B, N, D_IN), dtype=jnp.float32)
        A_shape = jax.random.uniform(k2, (B, N, N), dtype=jnp.float32)
        w = jax.random.normal(k3, (D_IN, D_OUT), dtype=jnp.float32)
        a = jax.random.normal(k4, (D_OUT,), dtype=jnp.float32)
        return {'x': x, 'A_shape': A_shape, 'w': w, 'a': a}
    _L3_gnn_all = _L3_gnn_setup()
    _L3_gnn_in = {k: v for k, v in _L3_gnn_all.items() if k in ('w', 'a')}
    del _L3_gnn_all
    return {'x': x, 'adj': adj, 'L0_gnn_W1': _L0_gnn_in['W1'], 'L0_gnn_b1': _L0_gnn_in['b1'], 'L0_gnn_gamma': _L0_gnn_in['gamma'], 'L0_gnn_beta': _L0_gnn_in['beta'], 'L0_gnn_W2': _L0_gnn_in['W2'], 'L0_gnn_b2': _L0_gnn_in['b2'], 'L1_gnn_W_qk': _L1_gnn_in['W_qk'], 'L1_gnn_W_v': _L1_gnn_in['W_v'], 'L2_gnn_Wv': _L2_gnn_in['Wv'], 'L2_gnn_bv': _L2_gnn_in['bv'], 'L2_gnn_aw': _L2_gnn_in['aw'], 'L2_gnn_ab': _L2_gnn_in['ab'], 'L2_gnn_Wk': _L2_gnn_in['Wk'], 'L2_gnn_bk': _L2_gnn_in['bk'], 'L3_gnn_w': _L3_gnn_in['w'], 'L3_gnn_a': _L3_gnn_in['a']}

def reference(x, adj, L0_gnn_W1, L0_gnn_b1, L0_gnn_gamma, L0_gnn_beta, L0_gnn_W2, L0_gnn_b2, L1_gnn_W_qk, L1_gnn_W_v, L2_gnn_Wv, L2_gnn_bv, L2_gnn_aw, L2_gnn_ab, L2_gnn_Wk, L2_gnn_bk, L3_gnn_w, L3_gnn_a):
    import jax
    import jax.numpy as jnp

    def _L0_gnn_ref(x, adj, W1, b1, gamma, beta, W2, b2):
        import jax, jax.numpy as jnp
        import numpy as np
        EPS_LN = 1e-05

        def hypergraph_conv(x, adj, W, b):
            N, C, _ = adj.shape
            H = (adj != 0).astype(x.dtype)
            w = adj.reshape(N, -1)[:, :C]
            xw = jnp.einsum('ncd,hd->nch', x, W)
            Dn = jnp.einsum('nce,ne->nc', H, w)
            Dn = jnp.where(Dn > 0, 1.0 / Dn, 0.0)
            Be = H.sum(axis=1)
            Be = jnp.where(Be > 0, 1.0 / Be, 0.0)
            m = Be[:, :, None] * jnp.einsum('nce,nch->neh', H, xw)
            out = Dn[:, :, None] * jnp.einsum('nce,neh->nch', H, m)
            return out + b

        def layer_norm(x, g, b):
            mu = jnp.mean(x, axis=-1, keepdims=True)
            var = jnp.var(x, axis=-1, keepdims=True)
            return (x - mu) * jax.lax.rsqrt(var + EPS_LN) * g + b
        h = jax.nn.relu(hypergraph_conv(x, adj, W1, b1))
        h = layer_norm(h, gamma, beta)
        y = hypergraph_conv(h, adj, W2, b2)
        return y + x

    def _L1_gnn_ref(x, adj_matrix, W_qk, W_v):
        import jax, jax.numpy as jnp
        import numpy as np
        IN_DIM = 256
        ATT_DIM = 64
        B, N = (4, 2048)
        qk = jnp.einsum('bnd,ed->bne', x, W_qk)
        q, k = jnp.split(qk, 2, axis=-1)
        v = jnp.einsum('bnd,ed->bne', x, W_v)
        inv_scale = 1.0 / ATT_DIM ** 0.5
        scores = jnp.einsum('bnd,bmd->bnm', q, k) * inv_scale
        w = jnp.sum(scores * adj_matrix, axis=-1, keepdims=True)
        w = jax.nn.softmax(w, axis=1)
        return w * v

    def _L2_gnn_ref(X, A, Wv, bv, aw, ab, Wk, bk):
        import jax, jax.numpy as jnp
        import numpy as np
        B, N, DIN, DOUT, K = (4, 1024, 256, 256, 3)
        d = Wv.shape[1]
        Xw = X @ Wv + bv
        sj = Xw @ aw[:d, 0]
        si = Xw @ aw[d:, 0]
        e = jax.nn.leaky_relu(sj[:, None, :] + si[:, :, None] + ab[0], negative_slope=0.2)
        alpha_matrix = A * jnp.exp(e)
        transition = alpha_matrix / (jnp.sum(alpha_matrix, axis=-1, keepdims=True) + 1e-12)
        H = jnp.zeros(X.shape[:-1] + (d,), dtype=X.dtype)
        Xk = X
        for k in range(Wk.shape[0]):
            H = H + Xk @ Wk[k] + bk[k]
            Xk = jnp.einsum('bij,bjd->bid', transition, Xk)
        return jax.nn.relu(H)

    def _L3_gnn_ref(x, A_shape, w, a):
        import jax, jax.numpy as jnp
        import numpy as np
        B, N, D_IN, D_OUT = (4, 2048, 256, 256)
        y = x @ w
        s = y @ a
        A = s[..., :, None] + s[..., None, :]
        A = jnp.tanh(A / 8.0) * 8.0
        A = jnp.where(A >= 0, A, 0.1 * A)
        A = jnp.exp(A) * A_shape
        A = A / jnp.sum(A, axis=-1, keepdims=True)
        A = A * jnp.sum(A_shape, axis=-1, keepdims=True)
        out = A @ x @ w
        return out
    x = _layernorm(x + _L0_gnn_ref(x, adj, L0_gnn_W1, L0_gnn_b1, L0_gnn_gamma, L0_gnn_beta, L0_gnn_W2, L0_gnn_b2), axis=-1)
    x = _layernorm(x + _L1_gnn_ref(x, adj, L1_gnn_W_qk, L1_gnn_W_v), axis=-1)
    x = _layernorm(x + _L2_gnn_ref(x, adj, L2_gnn_Wv, L2_gnn_bv, L2_gnn_aw, L2_gnn_ab, L2_gnn_Wk, L2_gnn_bk), axis=-1)
    x = _layernorm(x + _L3_gnn_ref(x, adj, L3_gnn_w, L3_gnn_a), axis=-1)
    return x

_drawn_inputs = setup_inputs


def setup_inputs(seed=0):
    import zlib

    import numpy as np

    out = dict(_drawn_inputs(seed))
    spreads = {'L0_gnn_b1': (0.0, 0.1),
     'L0_gnn_gamma': (1.0, 0.2),
     'L0_gnn_beta': (0.0, 0.1),
     'L0_gnn_b2': (0.0, 0.1)}
    factors = {'L2_gnn_bv': 29.306}
    for name, (base, spread) in spreads.items():
        noise = np.random.default_rng([zlib.crc32(name.encode()), seed]).standard_normal(out[name].shape)
        drawn = base * np.exp(spread * noise) if base else spread * noise
        out[name] = jnp.asarray(drawn.astype(out[name].dtype))
    for name, factor in factors.items():
        out[name] = (out[name] * factor).astype(out[name].dtype)
    return out
```

```python
import numpy as np
import concourse.bass as bass
from concourse import mybir
from contextlib import ExitStack

F32 = mybir.dt.float32
F16 = mybir.dt.float16
ALU = mybir.AluOpType
ACT = mybir.ActivationFunctionType
AX = mybir.AxisListType

GRAPHS, N, D, H = 64, 128, 256, 512
GP = 4
G = GRAPHS // GP
C = GP * N
DT = D // 128
HT = H // 128
QK = 64
EPS = 1e-5
W_SCALE = 64.0
WK_SCALE = 256.0
W3_SCALE = 16.0
CNT_SCALE = 128.0


class Parts:
    pass


def upto(g, per, k):
    return g * per + k


def xcols(g):
    return bass.ds(g * (GP * D), GP * D)


def gcols(g, j):
    return bass.ds(g * (GP * D) + j * D, D)


def acols(g):
    return bass.ds(g * C, C)


def over_groups(eng, step, lead, lag):
    first = 4 if lag else 2
    for g in range(-lead, first):
        step(g, g % 2, lambda k, g=g: 0 <= g + k < G)
    with eng.Fori(first // 2, G // 2 - 1) as pair:
        step(pair * 2, 0, lambda k: True)
        step(pair * 2 + 1, 1, lambda k: True)
    for g in range(G - 2, G + lag):
        step(g, g % 2, lambda k, g=g: 0 <= g + k < G)


def reused(g, back=2):
    return not isinstance(g, int) or g >= back


def triple(nc, out, lhs, rhs, start=True, stop=True, **kw):
    nc.tensor.matmul(out, lhs[0], rhs[1], start=start, stop=False, **kw)
    nc.tensor.matmul(out, lhs[1], rhs[0], start=False, stop=False, **kw)
    return nc.tensor.matmul(out, lhs[0], rhs[0], start=False, stop=stop, **kw)



def build(nc, x, adj, W1, b1, gamma, beta, W2, b2, W_qk, W_v, Wv, bv, aw, ab, Wk, bk, w3, a3, out,
          layers=4):
    ctx = ExitStack()
    with ctx:
        def sb(name, shape, dt=F32):
            return ctx.enter_context(nc.sbuf_tensor(name, shape, dt))

        def halves(name, shape):
            return [sb(f"{name}_{s}", shape, F16) for s in ("hi", "lo")]

        K = Parts()
        K.bank = [ctx.enter_context(nc.psum_tensor(f"bank{i}", [128, 512], F32)) for i in range(8)]
        K.x = sb("x_resident", [128, GRAPHS * D])
        K.at = sb("adjT_resident", [128, GRAPHS * N])
        K.asum = sb("adj_row_sums", [128, GRAPHS])
        K.ident = sb("ident", [128, 128])
        K.ident16 = sb("ident16", [128, 128], F16)
        K.ones = sb("ones", [128, 128])
        K.ones16 = sb("ones16", [128, 128], F16)
        K.minus_half, K.quarter, K.inv_d, K.eps, K.eps_quarter = (
            sb(name, [128, GP]) for name in ("minus_half", "quarter", "inv_d", "eps", "eps_quarter"))
        K.w1 = halves("W1T", [128, DT, H])
        K.w2 = halves("W2T", [128, HT, D + 1])
        K.qkv = halves("qkvT", [128, DT, 2 * QK + D])
        K.wk = halves("Wk", [128, DT, 3 * D + 2])
        K.w3 = halves("w3", [128, DT, D + 1])
        K.b1 = sb("b1_col", [128, HT])
        K.w2beta = sb("W2beta_rows", [128, D])
        K.edge_bias = sb("edge_bias", [128, 1])
        K.b2row = sb("b2_parts", [128, D], F16)
        K.bkrow = sb("bk_parts", [128, D], F16)

        K.xd = x.rearrange("g n d -> n g d")
        K.ad = adj.rearrange("g n e -> n g e")
        K.od = out.rearrange("g n d -> n g d")
        setup(nc, K, W1, b1, gamma, beta, W2, b2, W_qk, W_v, Wv, bv, aw, ab, Wk, bk, w3, a3)
        layer0(nc, K)
        if layers >= 2:
            layer1(nc, K)
        if layers >= 3:
            layer2(nc, K)
        if layers >= 4:
            layer3(nc, K)
        else:
            with nc.semaphore("out_done") as out_done, nc.Block() as block:
                @block.sync
                def _(sp):
                    sp.dma_start(K.od, K.x[:, :].rearrange("p (g d) -> p g d", g=GRAPHS)).then_inc(out_done, 16)
                    sp.wait_ge(out_done, 16)


def setup(nc, K, W1, b1, gamma, beta, W2, b2, W_qk, W_v, Wv, bv, aw, ab, Wk, bk, w3, a3):
    ctx = ExitStack()
    with ctx:
        def sb(name, shape, dt=F32):
            return ctx.enter_context(nc.sbuf_tensor(name, shape, dt))

        def sem(name):
            return ctx.enter_context(nc.semaphore(name))

        w1n, w2n = sb("w1n", [128, HT, D]), sb("w2n", [128, DT, H])
        wqn, wvn = sb("wqn", [128, D]), sb("wvn", [128, DT, D])
        gam, bet = sb("gam", [128, HT]), sb("bet", [128, HT])
        b2n, bkn = sb("b2n", [128, D]), sb("bkn", [128, 3, D])
        l2v, l2k = sb("l2v", [128, DT, D]), sb("l2k", [128, 3, DT, D])
        awb, bvb, abb = sb("awb", [128, 2 * D]), sb("bvb", [128, D]), sb("abb", [128, 1])
        w3n, a3b = sb("w3n", [128, DT, D]), sb("a3b", [128, D])
        w1f, w2f = sb("w1f", [128, DT, H]), sb("w2f", [128, HT, D + 1])
        w2b, qkvf = sb("w2b", [128, HT, D]), sb("qkvf", [128, DT, 2 * QK + D])
        wkf, w3f = sb("wkf", [128, DT, 3 * D + 2]), sb("w3f", [128, DT, D + 1])
        prod, edge = sb("prod", [128, 8, D]), sb("edge", [128, 4])
        gam64, bks = sb("gam64", [128, HT]), sb("bks", [128, 2, D])
        loaded, const, iden = sem("loaded"), sem("const"), sem("iden")
        transposed, gathered, v = sem("transposed"), sem("gathered"), sem("v")
        centre_ps, bias_ps = sem("centre_ps"), sem("bias_ps")
        folded = sem("folded")
        with nc.Block() as block:
            loads = [
                (w1n[:], W1.rearrange("(t p) d -> p t d", p=128)),
                (w2n[:], W2.rearrange("(t p) h -> p t h", p=128)),
                (wqn[:], W_qk), (wvn[:], W_v.rearrange("(t p) d -> p t d", p=128)),
                (l2v[:], Wv.rearrange("(t p) o -> p t o", p=128)),
                (l2k[:], Wk.rearrange("k (t p) o -> p k t o", p=128)),
                (w3n[:], w3.rearrange("(t p) o -> p t o", p=128)),
                (awb[:], aw.rearrange("a b -> b a").to_broadcast([128, 2 * D])),
                (bvb[:], bv.rearrange("(a b) -> a b", a=1).to_broadcast([128, D])),
                (abb[:], ab.rearrange("(a b) -> a b", a=1).to_broadcast([128, 1])),
                (a3b[:], a3.rearrange("(a b) -> a b", a=1).to_broadcast([128, D])),
            ]
            rows = [(b2n[r:r + 1, :], b2.rearrange("(a b) -> a b", a=1)) for r in (0, 32)]
            rows += [(bkn[r:r + 1, :, :], bk.rearrange("(a k) b -> a k b", a=1)) for r in (0, 32)]
            columns = [(K.b1, b1), (gam, gamma), (bet, beta)]
            all_loaded = 16 * (len(loads) + len(rows) + len(columns))

            @block.sync
            def _(sp):
                for dst, src in loads + rows:
                    sp.dma_start(dst, src).then_inc(loaded, 16)
                with nc.allow_non_contiguous_dma(reason="three short vectors, a value per partition"):
                    for dst, src in columns:
                        sp.dma_start(dst[:], src.rearrange("(t p) -> p t", p=128)).then_inc(loaded, 16)

            @block.gpsimd
            def _(pool):
                for m, value in ((K.ident, 0.0), (K.ident16, 0.0), (K.ones, 1.0), (K.ones16, 1.0),
                                 (K.minus_half, -0.5), (K.b2row, 0.0), (K.bkrow, 0.0), (K.quarter, 0.25),
                                 (K.inv_d, 1.0 / D), (K.eps, EPS), (K.eps_quarter, 0.25 * EPS)):
                    pool.memset(m[:], value).then_inc(const, 1)
                pool.wait_ge(const, 11)
                for m in (K.ident, K.ident16):
                    pool.affine_select(out=m[:], in_=m[:], compare_op=ALU.not_equal, fill=1.0, base=0,
                                       pattern=[[-1, 128]], channel_multiplier=1).then_inc(iden, 1)

            @block.tensor
            def _(pe):
                pe.wait_ge(loaded, all_loaded)
                pe.wait_ge(iden, 2)
                for d in range(DT):
                    for h in range(HT):
                        pe.transpose(K.bank[d][:, h * 128:(h + 1) * 128],
                                     w1n[:, h, d * 128:(d + 1) * 128], K.ident[:])
                for h in range(HT):
                    for d in range(DT):
                        c = (h % 2) * D + d * 128
                        pe.transpose(K.bank[2 + h // 2][:, c:c + 128],
                                     w2n[:, d, h * 128:(h + 1) * 128], K.ident[:])
                for d in range(DT):
                    pe.transpose(K.bank[4 + d][:, 0:128], wqn[:, d * 128:(d + 1) * 128], K.ident[:])
                    for e in range(DT):
                        m = pe.transpose(K.bank[4 + d][:, (e + 1) * 128:(e + 2) * 128],
                                         wvn[:, e, d * 128:(d + 1) * 128], K.ident[:])
                m.then_inc(transposed, 1)
                pe.wait_ge(gathered, 1)
                for h in range(HT):
                    m = pe.matmul(K.bank[6][:, 0:D], K.ones[:], w2f[:, h, 0:D],
                                  start=h == 0, stop=h == HT - 1)
                m.then_inc(centre_ps, 1)
                for h in range(HT):
                    m = pe.matmul(K.bank[7][:, 0:D], K.ones[:], w2b[:, h, :],
                                  start=h == 0, stop=h == HT - 1)
                m.then_inc(bias_ps, 1)

            @block.vector
            def _(dve):
                done = [0]

                def then(op):
                    done[0] += 1
                    op.then_inc(v, 1)
                    dve.wait_ge(v, done[0])

                dve.wait_ge(loaded, all_loaded)
                then(dve.tensor_scalar(gam64[:], gam[:], W_SCALE, None, ALU.mult))
                dve.wait_ge(transposed, 1)
                for d in range(DT):
                    dve.tensor_scalar(w1f[:, d, :], K.bank[d][:], W_SCALE, None, ALU.mult)
                    dve.tensor_scalar(qkvf[:, d, :], K.bank[4 + d][:, 0:2 * QK + D], W_SCALE, None, ALU.mult)
                for h in range(HT):
                    src = K.bank[2 + h // 2][:, (h % 2) * D:(h % 2 + 1) * D]
                    dve.tensor_scalar(w2f[:, h, 0:D], src, gam64[:, h:h + 1], None, ALU.mult)
                    dve.tensor_scalar(w2b[:, h, :], src, bet[:, h:h + 1], None, ALU.mult)
                dve.memset(w2f[:, :, D:D + 1], W_SCALE / H)
                op = dve.tensor_scalar(wkf[:, :, 0:D], l2k[:, 2], WK_SCALE, None, ALU.mult)
                then(op)
                dve.sem_inc(gathered, 1)
                dve.tensor_scalar(wkf[:, :, D + 2:2 * D + 2], l2k[:, 1], WK_SCALE, None, ALU.mult)
                dve.tensor_scalar(wkf[:, :, 2 * D + 2:3 * D + 2], l2k[:, 0], WK_SCALE, None, ALU.mult)
                for d in range(DT):
                    for s in range(2):
                        dve.tensor_tensor(prod[:, 2 * d + s, :], l2v[:, d, :], awb[:, s * D:(s + 1) * D], ALU.mult)
                    dve.tensor_tensor(prod[:, 4 + d, :], w3n[:, d, :], a3b[:], ALU.mult)
                for s in range(2):
                    op = dve.tensor_tensor(prod[:, 6 + s, :], bvb[:], awb[:, s * D:(s + 1) * D], ALU.mult)
                then(op)
                for d in range(DT):
                    dve.tensor_reduce(wkf[:, d, D:D + 2], prod[:, 2 * d:2 * d + 2, :], AX.X, ALU.add)
                    dve.tensor_reduce(w3f[:, d, D:D + 1], prod[:, 4 + d, :], AX.X, ALU.add)
                    dve.tensor_scalar(w3f[:, d, 0:D], w3n[:, d, :], W3_SCALE, None, ALU.mult)
                then(dve.tensor_reduce(edge[:, 0:2], prod[:, 6:8, :], AX.X, ALU.add))
                then(dve.tensor_tensor(edge[:, 2:3], edge[:, 0:1], edge[:, 1:2], ALU.add))
                then(dve.tensor_tensor(K.edge_bias[:], edge[:, 2:3], abb[:], ALU.add))
                for d in range(DT):
                    op = dve.tensor_scalar(wkf[:, d, D:D + 2], wkf[:, d, D:D + 2], WK_SCALE, None, ALU.mult)
                then(op)
                dve.wait_ge(centre_ps, 1)
                then(dve.tensor_scalar(prod[:, 0, :], K.bank[6][:, 0:D], 1.0 / H, None, ALU.mult))
                for h in range(HT):
                    op = dve.tensor_tensor(w2f[:, h, 0:D], w2f[:, h, 0:D], prod[:, 0, :], ALU.subtract)
                then(op)
                dve.wait_ge(bias_ps, 1)
                dve.tensor_copy(K.w2beta[:], K.bank[7][:, 0:D])
                for full, (hi, lo) in ((w1f, K.w1), (w2f, K.w2), (qkvf, K.qkv), (wkf, K.wk), (w3f, K.w3)):
                    then(dve.tensor_copy(hi[:], full[:]))
                    then(dve.tensor_tensor(lo[:], full[:], hi[:], ALU.subtract))
                dve.wait_ge(const, 11)
                for r in (0, 32):
                    rr = slice(r, r + 1)
                    then(dve.tensor_tensor(bks[rr, 0, :], bkn[rr, 0, :], bkn[rr, 1, :], ALU.add))
                    then(dve.tensor_tensor(bks[rr, 1, :], bks[rr, 0, :], bkn[rr, 2, :], ALU.add))
                    then(dve.tensor_scalar(bks[rr, 0, :], bks[rr, 1, :], WK_SCALE, None, ALU.mult))
                    for src, row in ((b2n[rr, :], K.b2row[rr, :]), (bks[rr, 0, :], K.bkrow[rr, :])):
                        then(dve.tensor_copy(row, src))
                        if r:
                            then(dve.tensor_tensor(row, src, row, ALU.subtract))


def layer0(nc, K):
    ctx = ExitStack()
    with ctx:
        def sb(name, shape, dt=F32):
            return ctx.enter_context(nc.sbuf_tensor(name, shape, dt))

        def sem(name):
            return ctx.enter_context(nc.semaphore(name))

        def halves(name, shape):
            return [sb(f"{name}_{s}", shape, F16) for s in ("hi", "lo")]

        bank = K.bank
        b_adj, b_gram = bank[0], bank[1]
        b_mix, b_hid, b_z = bank[2:4], bank[4:6], bank[6:8]

        adjn = [sb(f"adj{p}", [128, GP, N]) for p in range(2)]
        inc = [sb(f"incT{p}", [128, C], F16) for p in range(2)]
        wcol = halves("wcol", [128, GP])
        cnt, cnt1, rcnt = sb("cnt", [128, GP]), sb("cnt1", [128, GP]), sb("rcnt", [128, GP])
        rcs = halves("rcs", [128, GP])
        incb = [halves(f"incB{p}", [128, C]) for p in range(2)]
        dcl, drc, dpos, dinv = (sb(f"d{i}", [128, GP]) for i in range(4))
        dis = halves("dis", [128, GP])
        dbc, pf = sb("dbc", [128, C]), sb("pf", [128, C])
        ps = [halves(f"P{p}", [128, C]) for p in range(2)]
        xs = [halves(f"x{p}", [128, GP, D]) for p in range(2)]
        px = [halves(f"px{p}", [128, DT, C]) for p in range(2)]
        hf = sb("hf", [128, HT, C])
        hs = halves("h", [128, HT, C])
        hq, hq2, hqs = sb("hq", [128, HT, C]), sb("hq2", [128, 2, C]), sb("hqs", [128, C])
        zf, zn = sb("zf", [128, GP, D + 2]), sb("zn", [128, GP, D])
        zs = halves("z", [128, GP, D])
        zm2, zvar, zrs = sb("zm2", [128, GP]), sb("zvar", [128, GP]), sb("zrs", [128, GP])
        L = norm(nc, ctx, "l0")

        adj_in = [sem(f"adj_in{p}") for p in range(2)]
        x_in = [sem(f"x_in{p}") for p in range(2)]
        adjT_ps, adjT_sb, inc_ok, wcol_ok, small, incb_ok = map(
            sem, ("adjT_ps", "adjT_sb", "inc_ok", "wcol_ok", "small", "incb_ok"))
        deg_ps, gram_ps, dinv_ok, dbc_ps, dbc_sb, pf_ok, p_hi, p_lo = map(
            sem, ("deg_ps", "gram_ps", "dinv_ok", "dbc_ps", "dbc_sb", "pf_ok", "p_hi", "p_lo"))
        x_hi, x_lo, px_ps, px_hi, px_lo = map(sem, ("x_hi", "x_lo", "px_ps", "px_hi", "px_lo"))
        hid_ps, hf_ok, h_hi, h_sq, h_lo, hqs_ok = map(
            sem, ("hid_ps", "hf_ok", "h_hi", "h_sq", "h_lo", "hqs_ok"))
        z_ps, zf_ok, zvar_ok, zrs_ok, zn_ok, z_hi, z_lo = map(
            sem, ("z_ps", "zf_ok", "zvar_ok", "zrs_ok", "zn_ok", "z_hi", "z_lo"))
        y_ps = sem("y_ps")
        dchain = sem("dchain")

        with nc.Block() as block:
            @block.sync
            def _(sp):
                def load(g, p, has):
                    if has(0):
                        if reused(g):
                            sp.wait_ge(adjT_ps, upto(g - 2, 1, 1))
                        gs = bass.ds(g * GP, GP)
                        sp.dma_start(adjn[p][:], K.ad[:, gs, :]).then_inc(adj_in[p], 16)
                        if reused(g):
                            sp.wait_ge(x_lo, upto(g - 2, 1, 1))
                        sp.dma_start(K.x[:, xcols(g)].rearrange("p (g d) -> p g d", g=GP),
                                     K.xd[:, gs, :]).then_inc(x_in[p], 16)
                over_groups(sp, load, 0, 0)

            @block.tensor
            def _(pe):
                def transpose_adj(g, p):
                    pe.wait_ge(adj_in[p], 8 * (g - p) + 16)
                    if reused(g, 1):
                        pe.wait_ge(dbc_sb, upto(g - 1, 1, 1))
                    for j in range(GP):
                        m = pe.transpose(b_adj[:, j * N:(j + 1) * N], adjn[p][:, j, :], K.ident[:])
                    m.then_inc(adjT_ps, 1)

                def hidden(g, p):
                    for h in range(HT):
                        if h == 0:
                            pe.wait_ge(px_lo, upto(g, 2, 2))
                            pe.wait_ge(px_hi, upto(g, 2, 2))
                        if h >= 2 or reused(g, 1):
                            pe.wait_ge(hf_ok, upto(g, HT, h - 1))
                        for d in range(DT):
                            m = triple(nc, b_hid[h % 2][:], [w[:, d, h * 128:(h + 1) * 128] for w in K.w1],
                                       [s[:, d, :] for s in px[p]], start=d == 0, stop=d == DT - 1)
                        m.then_inc(hid_ps, 1)

                def gram(g, p):
                    pe.wait_ge(incb_ok, upto(g, 8, 8))
                    if reused(g, 1):
                        pe.wait_ge(pf_ok, upto(g - 1, 1, 1))
                    for j in range(GP):
                        c = slice(j * N, (j + 1) * N)
                        pe.matmul(b_gram[:, c], inc[p][:, c], incb[p][1][:, c], start=True, stop=False)
                        m = pe.matmul(b_gram[:, c], inc[p][:, c], incb[p][0][:, c], start=False, stop=True)
                    m.then_inc(gram_ps, 1)
                    pe.wait_ge(adjT_sb, upto(g, 1, 1))
                    for j in range(GP):
                        c = slice(j * N, (j + 1) * N)
                        pe.matmul(b_adj[:, j:j + 1], inc[p][:, c], wcol[1][:, j:j + 1], start=True, stop=False)
                        m = pe.matmul(b_adj[:, j:j + 1], inc[p][:, c], wcol[0][:, j:j + 1], start=False, stop=True)
                    m.then_inc(deg_ps, 1)

                def spread_degrees(g, p):
                    pe.wait_ge(dinv_ok, upto(g, 2, 2))
                    for j in range(GP):
                        for i, s in enumerate((1, 0)):
                            m = pe.matmul(b_adj[:, j * N:(j + 1) * N], dis[s][:, j:j + 1].to_broadcast([128, 128]),
                                          K.ident16[:], start=i == 0, stop=i == 1)
                    m.then_inc(dbc_ps, 1)

                def mix_x(g, p):
                    pe.wait_ge(x_hi, upto(g, 1, 1))
                    pe.wait_ge(x_lo, upto(g, 1, 1))
                    pe.wait_ge(p_hi, upto(g, 1, 1))
                    pe.wait_ge(p_lo, upto(g, 1, 1))
                    for d in range(DT):
                        if reused(g, 2):
                            pe.wait_ge(L.pre_ok, upto(g - 2, 2, d + 1))
                        elif g == 1:
                            pe.wait_ge(px_lo, upto(0, 2, d + 1))
                        for j in range(GP):
                            c = slice(j * N, (j + 1) * N)
                            m = triple(nc, b_mix[d][:, c], [s[:, j, d * 128:(d + 1) * 128] for s in xs[p]],
                                       [s[:, c] for s in ps[p]])
                        m.then_inc(px_ps, 1)

                def project(g, j):
                    if j >= 2 or reused(g, 1):
                        pe.wait_ge(zf_ok, upto(g, GP, j - 1))
                    for h in range(HT):
                        if j == 0:
                            pe.wait_ge(h_lo, upto(g, HT, h + 1))
                        triple(nc, b_z[j % 2][:, 0:D + 1], [s[:, h, j * N:(j + 1) * N] for s in hs],
                               [w[:, h, :] for w in K.w2], start=h == 0, stop=h == HT - 1)

                def square_sums(g, j):
                    if j == 0:
                        pe.wait_ge(hqs_ok, upto(g, 3, 3))
                    pe.matmul(b_z[j % 2][:, D + 1:D + 129], hqs[:, j * N:(j + 1) * N], K.ones[:],
                              start=True, stop=True).then_inc(z_ps, 1)

                def mix_z(g, p, last):
                    for i in range(2):
                        if not last:
                            if i == 0:
                                pe.wait_ge(px_lo, upto(g + 1, 2, 2))
                        else:
                            pe.wait_ge(L.pre_ok, upto(g - 1, 2, i + 1))
                        for jj in range(2):
                            j = 2 * i + jj
                            pe.wait_ge(z_hi, upto(g, GP, j + 1))
                            pe.wait_ge(z_lo, upto(g, GP, j + 1))
                            o = b_mix[i][:, jj * D:(jj + 1) * D]
                            pe.matmul(o, K.ones16[:], K.b2row[:], start=True, stop=False)
                            m = triple(nc, o, [s[:, j * N:(j + 1) * N] for s in ps[p]],
                                       [s[:, j, :] for s in zs], start=False)
                        m.then_inc(y_ps, 1)

                def step(g, p, has):
                    q = 1 - p
                    if has(0):
                        hidden(g, p)
                    if has(1):
                        gram(g + 1, q)
                    if has(-1):
                        mix_z(g - 1, q, isinstance(g, int) and g == G)
                    if has(1):
                        spread_degrees(g + 1, q)
                    if has(0):
                        project(g, 0)
                        project(g, 1)
                        square_sums(g, 0)
                        square_sums(g, 1)
                        project(g, 2)
                        square_sums(g, 2)
                    if has(1):
                        mix_x(g + 1, q)
                    if has(2):
                        transpose_adj(g + 2, p)
                    if has(0):
                        project(g, 3)
                        square_sums(g, 3)
                over_groups(pe, step, 2, 1)

            @block.scalar
            def _(act):
                def hidden(g, h):
                    act.wait_ge(hid_ps, upto(g, HT, h + 1))
                    if reused(g, 1):
                        act.wait_ge(h_lo, upto(g - 1, HT, h + 1))
                        act.wait_ge(h_sq, upto(g - 1, HT, h + 1))
                    act.activation(hf[:, h, :], b_hid[h % 2][:], ACT.Relu, bias=K.b1[:, h:h + 1],
                                   scale=1.0 / W_SCALE).then_inc(hf_ok, 1)
                    act.wait_ge(hf_ok, upto(g, HT, h + 1))
                    if reused(g, 1):
                        act.wait_ge(hqs_ok, upto(g - 1, 3, 3))
                    act.activation(hq[:, h, :], hf[:, h, :], ACT.Square).then_inc(h_sq, 1)

                def copy_z(g, j):
                    act.wait_ge(z_ps, upto(g, GP, j + 1))
                    if reused(g, 1):
                        act.wait_ge(zn_ok, upto(g - 1, GP, GP))
                    act.activation(zf[:, j, :], b_z[j % 2][:, 0:D + 2], ACT.Copy,
                                   scale=1.0 / W_SCALE).then_inc(zf_ok, 1)

                def z_high(g):
                    for j in range(GP):
                        act.wait_ge(zn_ok, upto(g, GP, j + 1))
                        if reused(g, 1):
                            act.wait_ge(y_ps, upto(g - 1, 2, 2))
                        act.activation(zs[0][:, j, :], zn[:, j, :], ACT.Copy).then_inc(z_hi, 1)

                def x_high(g, p):
                    act.wait_ge(x_in[p], 8 * (g - p) + 16)
                    if reused(g):
                        act.wait_ge(px_ps, upto(g - 2, 2, 2))
                    act.activation(xs[p][0][:], K.x[:, xcols(g)].rearrange("p (g d) -> p g d", g=GP),
                                   ACT.Copy).then_inc(x_hi, 1)

                def copy_degrees(g):
                    act.wait_ge(dbc_ps, upto(g, 1, 1))
                    if reused(g, 1):
                        act.wait_ge(pf_ok, upto(g - 1, 1, 1))
                    act.activation(dbc[:], b_adj[:], ACT.Copy).then_inc(dbc_sb, 1)

                def operator_high(g, p):
                    act.wait_ge(pf_ok, upto(g, 1, 1))
                    if reused(g):
                        act.wait_ge(y_ps, upto(g - 2, 2, 2))
                    act.activation(ps[p][0][:], pf[:], ACT.Copy).then_inc(p_hi, 1)

                def mixed_high(g, p):
                    for d in range(DT):
                        act.wait_ge(px_ps, upto(g, 2, d + 1))
                        if reused(g):
                            act.wait_ge(hid_ps, upto(g - 2, HT, HT))
                        act.activation(px[p][0][:, d, :], b_mix[d][:], ACT.Copy).then_inc(px_hi, 1)

                def copy_adj(g):
                    act.wait_ge(adjT_ps, upto(g, 1, 1))
                    act.activation(K.at[:, acols(g)], b_adj[:], ACT.Copy).then_inc(adjT_sb, 1)

                def step(g, p, has):
                    q = 1 - p
                    if has(0):
                        hidden(g, 0)
                    if has(-1):
                        z_high(g - 1)
                    if has(0):
                        hidden(g, 1)
                        hidden(g, 2)
                        hidden(g, 3)
                    if has(-2):
                        norm_apply(K, L, act, g - 2)
                    if has(1):
                        x_high(g + 1, q)
                        copy_degrees(g + 1)
                    if has(0):
                        copy_z(g, 0)
                    if has(1):
                        operator_high(g + 1, q)
                    if has(0):
                        copy_z(g, 1)
                        copy_z(g, 2)
                    if has(1):
                        mixed_high(g + 1, q)
                    if has(2):
                        copy_adj(g + 2)
                    if has(0):
                        copy_z(g, 3)
                over_groups(act, step, 2, 2)

            @block.vector
            def _(dve):
                def incidence(g, p):
                    dve.wait_ge(adjT_sb, upto(g, 1, 1))
                    if reused(g):
                        dve.wait_ge(deg_ps, upto(g - 2, 1, 1))
                    dve.tensor_scalar(inc[p][:], K.at[:, acols(g)], 0.0, None, ALU.not_equal).then_inc(inc_ok, 1)
                    first = K.at[:, acols(g)].rearrange("p (g n) -> p g n", g=GP)[:, :, 0]
                    if reused(g, 1):
                        dve.wait_ge(deg_ps, upto(g - 1, 1, 1))
                    dve.tensor_scalar(wcol[0][:], first, 1.0, None, ALU.mult).then_inc(wcol_ok, 1)
                    dve.wait_ge(wcol_ok, upto(g, 2, 1))
                    dve.tensor_tensor(wcol[1][:], first, wcol[0][:], ALU.subtract).then_inc(wcol_ok, 1)
                    dve.wait_ge(inc_ok, upto(g, 1, 1))
                    dve.tensor_reduce(cnt[:], inc[p][:].rearrange("p (g n) -> p g n", g=GP), AX.X,
                                      ALU.add).then_inc(small, 1)
                    dve.wait_ge(small, upto(g, 5, 1))
                    dve.tensor_scalar(cnt1[:], cnt[:], 1.0, 1.0 / CNT_SCALE, ALU.max, ALU.mult).then_inc(small, 1)
                    dve.wait_ge(small, upto(g, 5, 2))
                    dve.reciprocal(rcnt[:], cnt1[:]).then_inc(small, 1)
                    dve.wait_ge(small, upto(g, 5, 3))
                    dve.tensor_copy(rcs[0][:], rcnt[:]).then_inc(small, 1)
                    dve.wait_ge(small, upto(g, 5, 4))
                    dve.tensor_tensor(rcs[1][:], rcnt[:], rcs[0][:], ALU.subtract).then_inc(small, 1)

                def scale_incidence(g, p):
                    dve.wait_ge(small, upto(g, 5, 5))
                    if reused(g):
                        dve.wait_ge(gram_ps, upto(g - 2, 1, 1))
                    for s in range(2):
                        for j in range(GP):
                            c = slice(j * N, (j + 1) * N)
                            dve.tensor_scalar(incb[p][s][:, c], inc[p][:, c], rcs[s][:, j:j + 1], None,
                                              ALU.mult).then_inc(incb_ok, 1)

                def degrees(g):
                    dve.wait_ge(deg_ps, upto(g, 1, 1))
                    dve.tensor_scalar(dcl[:], b_adj[:, 0:GP], 1e-37, None, ALU.max).then_inc(dchain, 1)
                    dve.tensor_scalar(dpos[:], b_adj[:, 0:GP], 0.0, 1.0 / CNT_SCALE, ALU.is_gt,
                                      ALU.mult).then_inc(dchain, 1)
                    dve.wait_ge(dchain, upto(g, 4, 2))
                    dve.reciprocal(drc[:], dcl[:]).then_inc(dchain, 1)
                    dve.wait_ge(dchain, upto(g, 4, 3))
                    dve.tensor_tensor(dinv[:], drc[:], dpos[:], ALU.mult).then_inc(dchain, 1)
                    dve.wait_ge(dchain, upto(g, 4, 4))
                    if reused(g, 1):
                        dve.wait_ge(dbc_ps, upto(g - 1, 1, 1))
                    dve.tensor_copy(dis[0][:], dinv[:]).then_inc(dinv_ok, 1)
                    dve.wait_ge(dinv_ok, upto(g, 2, 1))
                    dve.tensor_tensor(dis[1][:], dinv[:], dis[0][:], ALU.subtract).then_inc(dinv_ok, 1)

                def hidden_split(g, h):
                    dve.wait_ge(hf_ok, upto(g, HT, h + 1))
                    if reused(g, 1):
                        dve.wait_ge(z_ps, upto(g - 1, GP, GP))
                    dve.tensor_copy(hs[0][:, h, :], hf[:, h, :]).then_inc(h_hi, 1)
                    dve.wait_ge(h_hi, upto(g, HT, h + 1))
                    dve.tensor_tensor(hs[1][:, h, :], hf[:, h, :], hs[0][:, h, :],
                                      ALU.subtract).then_inc(h_lo, 1)

                def operator(g, p):
                    dve.wait_ge(gram_ps, upto(g, 1, 1))
                    dve.wait_ge(dbc_sb, upto(g, 1, 1))
                    if reused(g, 1):
                        dve.wait_ge(p_hi, upto(g - 1, 1, 1))
                        dve.wait_ge(p_lo, upto(g - 1, 1, 1))
                    dve.tensor_tensor(pf[:], b_gram[:], dbc[:], ALU.mult).then_inc(pf_ok, 1)

                def operator_low(g, p):
                    dve.wait_ge(p_hi, upto(g, 1, 1))
                    dve.wait_ge(pf_ok, upto(g, 1, 1))
                    if reused(g):
                        dve.wait_ge(y_ps, upto(g - 2, 2, 2))
                    dve.tensor_tensor(ps[p][1][:], pf[:], ps[p][0][:], ALU.subtract).then_inc(p_lo, 1)

                def mixed_low(g, p):
                    for d in range(DT):
                        dve.wait_ge(px_hi, upto(g, 2, d + 1))
                        if reused(g):
                            dve.wait_ge(hid_ps, upto(g - 2, HT, HT))
                        dve.tensor_tensor(px[p][1][:, d, :], b_mix[d][:], px[p][0][:, d, :],
                                          ALU.subtract).then_inc(px_lo, 1)

                def layer_out(g):
                    for i in range(2):
                        dve.wait_ge(y_ps, upto(g, 2, i + 1))
                        if reused(g, 1):
                            dve.wait_ge(L.x_new, upto(g - 1, GP, GP))
                        dve.scalar_tensor_tensor(L.pre[:, 2 * i:2 * i + 2, :].rearrange("p a b -> p (a b)"),
                                                 b_mix[i][:], 0.5, K.x[:, bass.ds(g * (GP * D) + i * 2 * D, 2 * D)],
                                                 ALU.mult, ALU.add).then_inc(L.pre_ok, 1)
                    norm_rows(L, dve, g, 2)

                def hidden_norm(g):
                    dve.wait_ge(zf_ok, upto(g, GP, GP))
                    dve.tensor_tensor(zm2[:], zf[:, :, D], zf[:, :, D], ALU.mult).then_inc(zvar_ok, 1)
                    dve.wait_ge(zvar_ok, upto(g, 3, 1))
                    dve.scalar_tensor_tensor(zvar[:], zf[:, :, D + 1], W_SCALE / H, zm2[:], ALU.mult,
                                             ALU.subtract).then_inc(zvar_ok, 1)
                    dve.wait_ge(zvar_ok, upto(g, 3, 2))
                    if reused(g, 1):
                        dve.wait_ge(zrs_ok, upto(g - 1, 1, 1))
                    dve.tensor_scalar(zvar[:], zvar[:], 0.0, EPS, ALU.max, ALU.add).then_inc(zvar_ok, 1)

                def normalise(g):
                    dve.wait_ge(zrs_ok, upto(g, 1, 1))
                    for j in range(GP):
                        if reused(g, 1):
                            dve.wait_ge(z_hi, upto(g - 1, GP, j + 1))
                            dve.wait_ge(z_lo, upto(g - 1, GP, j + 1))
                        dve.scalar_tensor_tensor(zn[:, j, :], zf[:, j, 0:D], zrs[:, j:j + 1], K.w2beta[:],
                                                 ALU.mult, ALU.add).then_inc(zn_ok, 1)

                def step(g, p, has):
                    q = 1 - p
                    if has(-1):
                        hidden_norm(g - 1)
                    if has(1):
                        incidence(g + 1, q)
                    if has(-1):
                        normalise(g - 1)
                    if has(0):
                        hidden_split(g, 0)
                    if has(1):
                        scale_incidence(g + 1, q)
                    if has(-2):
                        norm_shift(L, dve, g - 2)
                    if has(0):
                        hidden_split(g, 1)
                        hidden_split(g, 2)
                    if has(1):
                        degrees(g + 1)
                    if has(0):
                        hidden_split(g, 3)
                    if has(1):
                        operator(g + 1, q)
                        operator_low(g + 1, q)
                    if has(-1):
                        layer_out(g - 1)
                    if has(1):
                        mixed_low(g + 1, q)
                over_groups(dve, step, 1, 2)

            @block.gpsimd
            def _(pool):
                def step(g, p, has):
                    q = 1 - p
                    if has(-1):
                        pool.wait_ge(zvar_ok, upto(g - 1, 3, 3))
                        if reused(g - 1, 1):
                            pool.wait_ge(zn_ok, upto(g - 2, GP, GP))
                        pool.tensor_tensor(zrs[:], zvar[:], K.minus_half[:], ALU.pow).then_inc(zrs_ok, 1)
                        for j in range(GP):
                            pool.wait_ge(z_hi, upto(g - 1, GP, j + 1))
                            if reused(g - 1, 1):
                                pool.wait_ge(y_ps, upto(g - 2, 2, 2))
                            pool.tensor_tensor(zs[1][:, j, :], zn[:, j, :], zs[0][:, j, :],
                                               ALU.subtract).then_inc(z_lo, 1)
                    if has(0):
                        for h in range(1, HT):
                            pool.wait_ge(h_sq, upto(g, HT, h + 1))
                            if h > 1:
                                pool.wait_ge(hqs_ok, upto(g, 3, h - 1))
                            elif reused(g, 1):
                                pool.wait_ge(z_ps, upto(g - 1, GP, GP))
                            pool.tensor_tensor((hqs if h == HT - 1 else hq2[:, h - 1, :])[:],
                                               (hq[:, 0, :] if h == 1 else hq2[:, h - 2, :])[:],
                                               hq[:, h, :], ALU.add).then_inc(hqs_ok, 1)
                    if has(1):
                        pool.wait_ge(x_hi, upto(g + 1, 1, 1))
                        if reused(g + 1):
                            pool.wait_ge(px_ps, upto(g - 1, 2, 2))
                        pool.tensor_tensor(xs[q][1][:], K.x[:, xcols(g + 1)].rearrange("p (g d) -> p g d", g=GP),
                                           xs[q][0][:], ALU.subtract).then_inc(x_lo, 1)
                    if has(-1):
                        norm_power(K, L, pool, g - 1, K.eps_quarter)
                over_groups(pool, step, 1, 1)


def norm(nc, ctx, tag):
    L = Parts()
    L.pre, L.st = (ctx.enter_context(nc.sbuf_tensor(f"{tag}_{name}", [128, GP, cols], F32))
                   for name, cols in (("pre", D), ("st", 6)))
    L.msum, L.mdiff, L.m2, L.dd, L.ddn, L.var, L.varn, L.veps, L.rstd, L.nmr = (
        ctx.enter_context(nc.sbuf_tensor(f"{tag}_{name}", [128, GP], F32))
        for name in ("msum", "mdiff", "m2", "dd", "ddn", "var", "varn", "veps", "rstd", "nmr"))
    L.pre_ok, L.st_ok, L.agg, L.rstd_ok, L.nmr_ok, L.x_new = (
        ctx.enter_context(nc.semaphore(f"{tag}_{name}"))
        for name in ("pre_ok", "st_ok", "agg", "rstd_ok", "nmr_ok", "x_new"))
    return L


def norm_rows(L, dve, g, per=GP):
    for j in range(GP):
        if j % (GP // per) == 0:
            dve.wait_ge(L.pre_ok, upto(g, per, j // (GP // per) + 1))
        if j == 0 and reused(g, 1):
            dve.wait_ge(L.agg, upto(g - 1, 8, 8))
        dve.bn_stats(L.st[:, j, :], L.pre[:, j, :]).then_inc(L.st_ok, 1)


def norm_power(K, L, pool, g, eps):
    pool.wait_ge(L.st_ok, upto(g, GP, GP))
    if reused(g, 1):
        pool.wait_ge(L.nmr_ok, upto(g - 1, 1, 1))
    pool.tensor_tensor(L.msum[:], L.st[:, :, 1], L.st[:, :, 4], ALU.add).then_inc(L.agg, 1)
    pool.tensor_tensor(L.mdiff[:], L.st[:, :, 1], L.st[:, :, 4], ALU.subtract).then_inc(L.agg, 1)
    pool.tensor_tensor(L.m2[:], L.st[:, :, 2], L.st[:, :, 5], ALU.add).then_inc(L.agg, 1)
    pool.wait_ge(L.agg, upto(g, 8, 2))
    pool.tensor_tensor(L.dd[:], L.mdiff[:], L.mdiff[:], ALU.mult).then_inc(L.agg, 1)
    pool.wait_ge(L.agg, upto(g, 8, 4))
    pool.tensor_tensor(L.ddn[:], L.dd[:], K.quarter[:], ALU.mult).then_inc(L.agg, 1)
    pool.tensor_tensor(L.var[:], L.m2[:], K.inv_d[:], ALU.mult).then_inc(L.agg, 1)
    pool.wait_ge(L.agg, upto(g, 8, 6))
    pool.tensor_tensor(L.varn[:], L.var[:], L.ddn[:], ALU.add).then_inc(L.agg, 1)
    pool.wait_ge(L.agg, upto(g, 8, 7))
    pool.tensor_tensor(L.veps[:], L.varn[:], eps[:], ALU.add).then_inc(L.agg, 1)
    pool.wait_ge(L.agg, upto(g, 8, 8))
    if reused(g, 1):
        pool.wait_ge(L.x_new, upto(g - 1, GP, GP))
    pool.tensor_tensor(L.rstd[:], L.veps[:], K.minus_half[:], ALU.pow).then_inc(L.rstd_ok, 1)


def norm_shift(L, dve, g):
    dve.wait_ge(L.rstd_ok, upto(g, 1, 1))
    if reused(g, 1):
        dve.wait_ge(L.x_new, upto(g - 1, GP, GP))
    dve.scalar_tensor_tensor(L.nmr[:], L.msum[:], -0.5, L.rstd[:], ALU.mult, ALU.mult).then_inc(L.nmr_ok, 1)


def norm_apply(K, L, act, g):
    act.wait_ge(L.nmr_ok, upto(g, 1, 1))
    for j in range(GP):
        act.activation(K.x[:, gcols(g, j)], L.pre[:, j, :], ACT.Identity,
                       bias=L.nmr[:, j:j + 1], scale=L.rstd[:, j:j + 1]).then_inc(L.x_new, 1)


def front(nc, K, ctx, tag):
    F = Parts()
    F.x_hi, F.x_lo, F.xT_ps, F.xT_sb = (ctx.enter_context(nc.semaphore(f"{tag}_{name}"))
                                        for name in ("x_hi", "x_lo", "xT_ps", "xT_sb"))
    F.xs = [[ctx.enter_context(nc.sbuf_tensor(f"{tag}_x{p}_{s}", [128, GP, D], F16)) for s in ("hi", "lo")]
            for p in range(2)]
    F.xT = [[ctx.enter_context(nc.sbuf_tensor(f"{tag}_xT{p}_{s}", [128, DT, C], F16)) for s in ("hi", "lo")]
            for p in range(2)]
    return F


def x_high(K, F, act, g, p):
    if reused(g):
        act.wait_ge(F.xT_ps, upto(g - 2, 2, 2))
    act.activation(F.xs[p][0][:], K.x[:, xcols(g)].rearrange("p (g d) -> p g d", g=GP),
                   ACT.Copy).then_inc(F.x_hi, 1)


def x_low(K, F, pool, g, p):
    pool.wait_ge(F.x_hi, upto(g, 1, 1))
    if reused(g):
        pool.wait_ge(F.xT_ps, upto(g - 2, 2, 2))
    pool.tensor_tensor(F.xs[p][1][:], K.x[:, xcols(g)].rearrange("p (g d) -> p g d", g=GP),
                       F.xs[p][0][:], ALU.subtract).then_inc(F.x_lo, 1)


def transpose_x(K, F, pe, g, p, banks):
    for s, ready in ((0, F.x_hi), (1, F.x_lo)):
        pe.wait_ge(ready, upto(g, 1, 1))
        if reused(g, 1):
            pe.wait_ge(F.xT_sb, upto(g - 1, 2, s + 1))
        o = banks[s][:].bitcast(F16)
        for d in range(DT):
            for j in range(GP):
                m = pe.transpose(o[:, d * C + j * N:d * C + (j + 1) * N],
                                 F.xs[p][s][:, j, d * 128:(d + 1) * 128], K.ident16[:])
        m.then_inc(F.xT_ps, 1)


def copy_xT(K, F, dve, g, p, banks, s, readers):
    dve.wait_ge(F.xT_ps, upto(g, 2, s + 1))
    if reused(g):
        dve.wait_ge(readers[0], upto(g - 2, readers[1], readers[1]))
    dve.tensor_copy(F.xT[p][s][:].rearrange("p d c -> p (d c)"), banks[s][:].bitcast(F16)).then_inc(F.xT_sb, 1)


def layer1(nc, K):
    ctx = ExitStack()
    with ctx:
        def sb(name, shape, dt=F32):
            return ctx.enter_context(nc.sbuf_tensor(f"l1_{name}", shape, dt))

        def sem(name):
            return ctx.enter_context(nc.semaphore(f"l1_{name}"))

        bank = K.bank
        b_xT, b_qkv, b_ak, b_sm = bank[0:2], bank[2:6], bank[6], bank[7]
        F, L = front(nc, K, ctx, "l1"), norm(nc, ctx, "l1")
        qkv = [sb(f"qkv{p}", [128, GP, 2 * QK + D]) for p in range(2)]
        ks = [sb("k_hi", [128, GP, QK + 1], F16), sb("k_lo", [128, GP, QK + 1], F16)]
        ats = [[sb(f"adjT{p}_{s}", [128, C], F16) for s in ("hi", "lo")] for p in range(2)]
        qa, w = sb("qa", [128, GP, QK]), sb("w", [128, GP])
        wmax, wneg, wexp, wsum = sb("wmax", [GP, 1]), sb("wneg", [GP, 1]), sb("wexp", [GP, N]), sb("wsum", [GP, 1])
        wsc, wrec, wn, wgt = sb("wsc", [GP, 1]), sb("wrec", [GP, 1]), sb("wn", [GP, N]), sb("wgt", [128, GP])
        qkv_ps, qkv_sb, k_hi, k_lo, a_hi, a_lo, k_one, ak_ps = map(
            sem, ("qkv_ps", "qkv_sb", "k_hi", "k_lo", "a_hi", "a_lo", "k_one", "ak_ps"))
        qa_ok, w_ok, asum_ok, wT_ps, wmax_ok, wneg_ok, wexp_ok, wrec_ok, wn_ok, wB_ps, wgt_ok = map(
            sem, ("qa_ok", "w_ok", "asum_ok", "wT_ps", "wmax_ok", "wneg_ok", "wexp_ok", "wrec_ok", "wn_ok",
                  "wB_ps", "wgt_ok"))
        SC = 1.0 / (W_SCALE * W_SCALE * QK ** 0.5)

        with nc.Block() as block:
            @block.tensor
            def _(pe):
                def project(g, p, j):
                    if j == 0:
                        pe.wait_ge(F.xT_sb, upto(g, 2, 2))
                    if reused(g, 1):
                        pe.wait_ge(qkv_sb, upto(g - 1, GP, j + 1))
                    c = slice(j * N, (j + 1) * N)
                    for d in range(DT):
                        m = triple(nc, b_qkv[j][:, 0:2 * QK + D], [s[:, d, c] for s in F.xT[p]],
                                   [w[:, d, :] for w in K.qkv], start=d == 0, stop=d == DT - 1)
                    m.then_inc(qkv_ps, 1)

                def aggregate(g, p):
                    for s in (k_hi, k_lo, a_hi, a_lo):
                        pe.wait_ge(s, upto(g, 1, 1))
                    if isinstance(g, int) and g == 0:
                        pe.wait_ge(k_one, 2)
                    if reused(g, 1):
                        pe.wait_ge(asum_ok, upto(g - 1, 1, 1))
                        pe.wait_ge(qa_ok, upto(g - 1, 1, 1))
                    for j in range(GP):
                        m = triple(nc, b_ak[:, j * (QK + 1):(j + 1) * (QK + 1)],
                                   [s[:, j * N:(j + 1) * N] for s in ats[p]], [s[:, j, :] for s in ks])
                    m.then_inc(ak_ps, 1)

                def score_rows(g):
                    pe.wait_ge(w_ok, upto(g, 1, 1))
                    if reused(g, 1):
                        pe.wait_ge(wgt_ok, upto(g - 1, 1, 1))
                    pe.transpose(b_sm[0:GP, 0:N], w[:], K.ident[:]).then_inc(wT_ps, 1)

                def weight_columns(g):
                    pe.wait_ge(wn_ok, upto(g, 1, 1))
                    pe.matmul(b_sm[:, N:N + GP], wn[:], K.ident[0:GP, 0:GP], start=True,
                              stop=True).then_inc(wB_ps, 1)

                def step(g, p, has):
                    q = 1 - p
                    if has(0):
                        project(g, p, 0)
                    if has(1):
                        transpose_x(K, F, pe, g + 1, q, b_xT)
                    if has(-1):
                        aggregate(g - 1, q)
                    if has(0):
                        project(g, p, 1)
                    if has(-1):
                        score_rows(g - 1)
                    if has(0):
                        project(g, p, 2)
                        project(g, p, 3)
                    if has(-1):
                        weight_columns(g - 1)
                over_groups(pe, step, 1, 2)

            @block.scalar
            def _(act):
                def step(g, p, has):
                    q = 1 - p
                    if has(2):
                        x_high(K, F, act, g + 2, p)
                    if has(0):
                        if reused(g):
                            act.wait_ge(ak_ps, upto(g - 2, 1, 1))
                        act.activation(ats[p][0][:], K.at[:, acols(g)], ACT.Copy).then_inc(a_hi, 1)
                        for j in range(GP):
                            act.wait_ge(qkv_ps, upto(g, GP, j + 1))
                            if reused(g):
                                act.wait_ge(L.pre_ok, upto(g - 2, GP, j + 1))
                            act.activation(qkv[p][:, j, :], b_qkv[j][:, 0:2 * QK + D],
                                           ACT.Copy).then_inc(qkv_sb, 1)
                        act.wait_ge(qkv_sb, upto(g, GP, GP))
                        if reused(g, 1):
                            act.wait_ge(ak_ps, upto(g - 1, 1, 1))
                        act.activation(ks[0][:, :, 0:QK], qkv[p][:, :, QK:2 * QK], ACT.Copy).then_inc(k_hi, 1)
                    if has(-1):
                        act.wait_ge(wneg_ok, upto(g - 1, 1, 1))
                        if reused(g - 1, 1):
                            act.wait_ge(wn_ok, upto(g - 2, 1, 1))
                        act.activation(wexp[:], b_sm[0:GP, 0:N], ACT.Exp, bias=wneg[:], scale=SC,
                                       accum_out=wsum[:]).then_inc(wexp_ok, 1)
                    if has(-2):
                        norm_apply(K, L, act, g - 2)
                over_groups(act, step, 2, 2)

            @block.vector
            def _(dve):
                def residual(g, p):
                    dve.wait_ge(wB_ps, upto(g, 1, 1))
                    if reused(g, 1):
                        dve.wait_ge(L.pre_ok, upto(g - 1, GP, GP))
                        dve.wait_ge(L.x_new, upto(g - 1, GP, GP))
                    dve.tensor_copy(wgt[:], b_sm[:, N:N + GP]).then_inc(wgt_ok, 1)
                    dve.wait_ge(wgt_ok, upto(g, 1, 1))
                    for j in range(GP):
                        dve.scalar_tensor_tensor(L.pre[:, j, :], qkv[p][:, j, 2 * QK:], wgt[:, j:j + 1],
                                                 K.x[:, gcols(g, j)], ALU.mult, ALU.add).then_inc(L.pre_ok, 1)

                def scores(g, p):
                    dve.wait_ge(ak_ps, upto(g, 1, 1))
                    ak = b_ak[:, 0:GP * (QK + 1)].rearrange("p (g k) -> p g k", g=GP)
                    if reused(g, 1):
                        dve.wait_ge(w_ok, upto(g - 1, 1, 1))
                    dve.tensor_tensor(qa[:], ak[:, :, 0:QK], qkv[p][:, :, 0:QK], ALU.mult).then_inc(qa_ok, 1)
                    dve.tensor_scalar(K.asum[:, bass.ds(g * GP, GP)], ak[:, :, QK], 1.0, None,
                                      ALU.mult).then_inc(asum_ok, 1)
                    dve.wait_ge(qa_ok, upto(g, 1, 1))
                    if reused(g, 1):
                        dve.wait_ge(wT_ps, upto(g - 1, 1, 1))
                    dve.tensor_reduce(w[:], qa[:], AX.X, ALU.add).then_inc(w_ok, 1)

                def maximum(g):
                    dve.wait_ge(wT_ps, upto(g, 1, 1))
                    dve.tensor_reduce(wmax[:], b_sm[0:GP, 0:N], AX.X, ALU.max).then_inc(wmax_ok, 1)
                    dve.wait_ge(wmax_ok, upto(g, 1, 1))
                    if reused(g, 1):
                        dve.wait_ge(wexp_ok, upto(g - 1, 1, 1))
                    dve.tensor_scalar(wneg[:], wmax[:], -SC, None, ALU.mult).then_inc(wneg_ok, 1)

                def softmax(g):
                    dve.wait_ge(wexp_ok, upto(g, 1, 1))
                    dve.tensor_scalar(wsc[:], wsum[:], W_SCALE, None, ALU.mult).then_inc(wrec_ok, 1)
                    dve.wait_ge(wrec_ok, upto(g, 2, 1))
                    dve.reciprocal(wrec[:], wsc[:]).then_inc(wrec_ok, 1)
                    dve.wait_ge(wrec_ok, upto(g, 2, 2))
                    if reused(g, 1):
                        dve.wait_ge(wB_ps, upto(g - 1, 1, 1))
                    dve.tensor_scalar(wn[:], wexp[:], wrec[:], None, ALU.mult).then_inc(wn_ok, 1)

                dve.memset(ks[0][:, :, QK:QK + 1], 1.0).then_inc(k_one, 1)
                dve.memset(ks[1][:, :, QK:QK + 1], 0.0).then_inc(k_one, 1)

                def step(g, p, has):
                    q = 1 - p
                    if has(-2):
                        residual(g - 2, p)
                    if has(-1):
                        scores(g - 1, q)
                    if has(1):
                        copy_xT(K, F, dve, g + 1, q, b_xT, 0, (qkv_ps, GP))
                    if has(-1):
                        maximum(g - 1)
                    if has(1):
                        copy_xT(K, F, dve, g + 1, q, b_xT, 1, (qkv_ps, GP))
                    if has(-1):
                        softmax(g - 1)
                    if has(-2):
                        norm_rows(L, dve, g - 2)
                        norm_shift(L, dve, g - 2)
                over_groups(dve, step, 1, 2)

            @block.gpsimd
            def _(pool):
                def step(g, p, has):
                    if has(2):
                        x_low(K, F, pool, g + 2, p)
                    if has(0):
                        pool.wait_ge(a_hi, upto(g, 1, 1))
                        if reused(g):
                            pool.wait_ge(ak_ps, upto(g - 2, 1, 1))
                        pool.tensor_tensor(ats[p][1][:], K.at[:, acols(g)], ats[p][0][:],
                                           ALU.subtract).then_inc(a_lo, 1)
                    if has(-2):
                        norm_power(K, L, pool, g - 2, K.eps)
                    if has(0):
                        pool.wait_ge(k_hi, upto(g, 1, 1))
                        if reused(g, 1):
                            pool.wait_ge(ak_ps, upto(g - 1, 1, 1))
                        pool.tensor_tensor(ks[1][:, :, 0:QK], qkv[p][:, :, QK:2 * QK], ks[0][:, :, 0:QK],
                                           ALU.subtract).then_inc(k_lo, 1)
                over_groups(pool, step, 2, 2)


def attention_front(nc, K, ctx, tag, width):
    S = Parts()
    S.s_ps, S.s_hi, S.s_lo, S.s_bias, S.sj_ps, S.t_ok, S.e_ok, S.u_ok = (
        ctx.enter_context(nc.semaphore(f"{tag}_{name}"))
        for name in ("s_ps", "s_hi", "s_lo", "s_bias", "sj_ps", "t_ok", "e_ok", "u_ok"))
    S.s = [ctx.enter_context(nc.sbuf_tensor(f"{tag}_s_{s}", [128, GP], F16)) for s in ("hi", "lo")]
    S.bias = ctx.enter_context(nc.sbuf_tensor(f"{tag}_bias", [128, GP], F32))
    S.t = ctx.enter_context(nc.sbuf_tensor(f"{tag}_t", [128, C], F32))
    S.lr = ctx.enter_context(nc.sbuf_tensor(f"{tag}_lr", [128, C], F32))
    S.e = ctx.enter_context(nc.sbuf_tensor(f"{tag}_e", [128, C], F32))
    S.u = ctx.enter_context(nc.sbuf_tensor(f"{tag}_u", [128, C], F32))
    S.width = width
    return S


def node_scores(nc, K, F, S, pe, g, p, b, weights, column):
    pe.wait_ge(F.xT_sb, upto(g, 2, 2))
    if reused(g, 1):
        pe.wait_ge(S.s_lo, upto(g - 1, 1, 1))
        pe.wait_ge(S.s_bias, upto(g - 1, 1, 1))
    for j in range(GP):
        for d in range(DT):
            m = triple(nc, b[:, j * S.width:(j + 1) * S.width], [s[:, d, j * N:(j + 1) * N] for s in F.xT[p]],
                       [w[:, d, column:column + S.width] for w in weights], start=d == 0, stop=d == DT - 1)
    m.then_inc(S.s_ps, 1)


def split_scores(S, dve, g, b):
    dve.wait_ge(S.s_ps, upto(g, 1, 1))
    if reused(g, 1):
        dve.wait_ge(S.sj_ps, upto(g - 1, 1, 1))
    sj = b[:, 0:GP * S.width].rearrange("p (g s) -> p g s", g=GP)[:, :, 0]
    dve.tensor_copy(S.s[0][:], sj).then_inc(S.s_hi, 1)
    dve.wait_ge(S.s_hi, upto(g, 1, 1))
    dve.tensor_tensor(S.s[1][:], sj, S.s[0][:], ALU.subtract).then_inc(S.s_lo, 1)


def spread_scores(nc, K, S, pe, g, b, free, per):
    pe.wait_ge(S.s_lo, upto(g, 1, 1))
    if reused(g, 1):
        pe.wait_ge(free, upto(g - 1, per, per))
    for j in range(GP):
        for s in (1, 0):
            m = pe.matmul(b[:, j * N:(j + 1) * N], S.s[s][:, j:j + 1].to_broadcast([128, 128]),
                          K.ident16[:], start=s == 1, stop=s == 0)
    m.then_inc(S.sj_ps, 1)


def layer2(nc, K):
    ctx = ExitStack()
    with ctx:
        def sb(name, shape, dt=F32):
            return ctx.enter_context(nc.sbuf_tensor(f"l2_{name}", shape, dt))

        def sem(name):
            return ctx.enter_context(nc.semaphore(f"l2_{name}"))

        bank = K.bank
        b_xT, b_far, b_near, b_s, b_t = bank[0:2], bank[2], bank[3:6], bank[6], bank[7]
        F, L, S = front(nc, K, ctx, "l2"), norm(nc, ctx, "l2"), attention_front(nc, K, ctx, "l2", 2)
        adjn = [sb(f"adj{p}", [128, GP, N]) for p in range(2)]
        rsum, reps, rinv = sb("rsum", [128, GP]), sb("reps", [128, GP]), sb("rinv", [128, GP])
        tf = sb("tf", [128, C])
        ts = [sb("T_hi", [128, C], F16), sb("T_lo", [128, C], F16)]
        tT = [sb(f"TT{p}", [128, 2, C], F16) for p in range(2)]
        far = [[sb(f"far{j}_{s}", [128, D], F16) for s in ("hi", "lo")] for j in range(GP)]
        mid = [[sb(f"mid{j}_{s}", [128, D], F16) for s in ("hi", "lo")] for j in range(GP)]
        hr = sb("hr", [128, GP, D])
        adj_in = [sem(f"adj_in{p}") for p in range(2)]
        rsum_ok, reps_ok, rinv_ok, tf_ok, t_hi, t_lo, tT_ps, tT_sb = map(
            sem, ("rsum_ok", "reps_ok", "rinv_ok", "tf_ok", "t_hi", "t_lo", "tT_ps", "tT_sb"))
        far_ps, far_hi, far_lo, near_ps, mid_ps, mid_hi, mid_lo, out_ps, hr_ok = map(
            sem, ("far_ps", "far_hi", "far_lo", "near_ps", "mid_ps", "mid_hi", "mid_lo", "out_ps", "hr_ok"))
        lr_ok = sem("lr_ok")
        before = (0, -2, -1, 1)

        with nc.Block() as block:
            @block.sync
            def _(sp):
                def load(g, p, has):
                    if has(0):
                        if reused(g):
                            sp.wait_ge(S.u_ok, upto(g - 2, 1, 1))
                        sp.dma_start(adjn[p][:], K.ad[:, bass.ds(g * GP, GP), :]).then_inc(adj_in[p], 16)
                over_groups(sp, load, 0, 0)

            @block.tensor
            def _(pe):
                def project(g, p, j, n):
                    if j == 0:
                        pe.wait_ge(F.xT_sb, upto(g, 2, 2))
                    if j >= 1 or reused(g, 1):
                        pe.wait_ge(far_lo, upto(g, GP, j))
                    c = slice(j * N, (j + 1) * N)
                    for d in range(DT):
                        m = triple(nc, b_far[:, 0:D], [s[:, d, c] for s in F.xT[p]],
                                   [w[:, d, 0:D] for w in K.wk], start=d == 0, stop=d == DT - 1)
                    m.then_inc(far_ps, 1)
                    if j == 3 or reused(g, 1):
                        pe.wait_ge(hr_ok, upto(g, GP, before[j]))
                    for d in range(DT):
                        m = triple(nc, b_near[n][:], [s[:, d, c] for s in F.xT[p]],
                                   [w[:, d, D + 2:3 * D + 2] for w in K.wk], start=d == 0, stop=d == DT - 1)
                    m.then_inc(near_ps, 1)

                def walk_far(g, p, j, n):
                    pe.wait_ge(tT_sb, upto(g, 1, 1))
                    pe.wait_ge(far_hi, upto(g, GP, j + 1))
                    pe.wait_ge(far_lo, upto(g, GP, j + 1))
                    triple(nc, b_near[n][:, 0:D], [tT[p][:, s, j * N:(j + 1) * N] for s in range(2)],
                           [s[:] for s in far[j]], start=False, skip_group_check=True).then_inc(mid_ps, 1)

                def walk_mid(g, p, j, n):
                    pe.wait_ge(mid_hi, upto(g, GP, j + 1))
                    pe.wait_ge(mid_lo, upto(g, GP, j + 1))
                    o = b_near[n][:, D:2 * D]
                    pe.matmul(o, K.ones16[:], K.bkrow[:], start=False, stop=False, skip_group_check=True)
                    triple(nc, o, [tT[p][:, s, j * N:(j + 1) * N] for s in range(2)], [s[:] for s in mid[j]],
                           start=False, skip_group_check=True).then_inc(out_ps, 1)

                def transpose_T(g):
                    pe.wait_ge(t_hi, upto(g, 1, 1))
                    pe.wait_ge(t_lo, upto(g, 1, 1))
                    pe.wait_ge(S.t_ok, upto(g, GP, GP))
                    o = b_t[:].bitcast(F16)
                    for s in range(2):
                        for j in range(GP):
                            m = pe.transpose(o[:, s * C + j * N:s * C + (j + 1) * N],
                                             ts[s][:, j * N:(j + 1) * N], K.ident16[:])
                    m.then_inc(tT_ps, 1)

                def step(g, p, has):
                    q = 1 - p
                    if has(1):
                        transpose_x(K, F, pe, g + 1, q, b_xT)
                    if has(0):
                        project(g, p, 0, 0)
                    if has(1):
                        node_scores(nc, K, F, S, pe, g + 1, q, b_s, K.wk, D)
                    if has(0):
                        project(g, p, 1, 1)
                    if has(1):
                        spread_scores(nc, K, S, pe, g + 1, b_t, tT_sb, 1)
                    if has(0):
                        walk_far(g, p, 0, 0)
                        project(g, p, 2, 2)
                        walk_far(g, p, 1, 1)
                        walk_mid(g, p, 0, 0)
                        walk_far(g, p, 2, 2)
                        walk_mid(g, p, 1, 1)
                        project(g, p, 3, 0)
                        walk_mid(g, p, 2, 2)
                        walk_far(g, p, 3, 0)
                    if has(1):
                        transpose_T(g + 1)
                    if has(0):
                        walk_mid(g, p, 3, 0)
                over_groups(pe, step, 2, 0)

            @block.scalar
            def _(act):
                def logits(g):
                    act.wait_ge(S.sj_ps, upto(g, 1, 1))
                    act.wait_ge(S.s_bias, upto(g, 1, 1))
                    if reused(g, 1):
                        act.wait_ge(lr_ok, upto(g - 1, 1, 1))
                    for j in range(GP):
                        act.activation(S.t[:, j * N:(j + 1) * N], b_t[:, j * N:(j + 1) * N], ACT.Identity,
                                       bias=S.bias[:, j:j + 1], scale=1.0 / WK_SCALE).then_inc(S.t_ok, 1)

                def far_high(g, j):
                    act.wait_ge(far_ps, upto(g, GP, j + 1))
                    if reused(g, 1):
                        act.wait_ge(mid_ps, upto(g - 1, GP, j + 1))
                    act.activation(far[j][0][:], b_far[:, 0:D], ACT.Copy).then_inc(far_hi, 1)

                def mid_high(g, j, n):
                    act.wait_ge(mid_ps, upto(g, GP, j + 1))
                    if reused(g, 1):
                        act.wait_ge(out_ps, upto(g - 1, GP, j + 1))
                    act.activation(mid[j][0][:], b_near[n][:, 0:D], ACT.Copy).then_inc(mid_hi, 1)

                def relu(g, j, n):
                    act.wait_ge(out_ps, upto(g, GP, j + 1))
                    if reused(g, 1):
                        act.wait_ge(L.pre_ok, upto(g - 1, GP, j + 1))
                    act.activation(hr[:, j, :], b_near[n][:, D:2 * D], ACT.Relu,
                                   scale=1.0 / WK_SCALE).then_inc(hr_ok, 1)

                def step(g, p, has):
                    q = 1 - p
                    if has(2):
                        x_high(K, F, act, g + 2, p)
                    if has(0):
                        far_high(g, 0)
                        far_high(g, 1)
                    if has(1):
                        logits(g + 1)
                    if has(0):
                        mid_high(g, 0, 0)
                        far_high(g, 2)
                    if has(1):
                        act.wait_ge(lr_ok, upto(g + 1, 1, 1))
                        if reused(g + 1, 1):
                            act.wait_ge(S.u_ok, upto(g, 1, 1))
                        act.activation(S.e[:], S.lr[:], ACT.Exp).then_inc(S.e_ok, 1)
                    if has(0):
                        mid_high(g, 1, 1)
                    if has(-1):
                        norm_apply(K, L, act, g - 1)
                    if has(0):
                        relu(g, 0, 0)
                        mid_high(g, 2, 2)
                        relu(g, 1, 1)
                        far_high(g, 3)
                        relu(g, 2, 2)
                    if has(1):
                        act.wait_ge(tf_ok, upto(g + 1, 1, 1))
                        if reused(g + 1, 1):
                            act.wait_ge(tT_ps, upto(g, 1, 1))
                        act.activation(ts[0][:], tf[:], ACT.Copy).then_inc(t_hi, 1)
                    if has(0):
                        mid_high(g, 3, 0)
                        relu(g, 3, 0)
                over_groups(act, step, 2, 1)

            @block.vector
            def _(dve):
                def far_low(g, j):
                    dve.wait_ge(far_hi, upto(g, GP, j + 1))
                    if reused(g, 1):
                        dve.wait_ge(mid_ps, upto(g - 1, GP, j + 1))
                    dve.tensor_tensor(far[j][1][:], b_far[:, 0:D], far[j][0][:], ALU.subtract).then_inc(far_lo, 1)

                def mid_low(g, j, n):
                    dve.wait_ge(mid_hi, upto(g, GP, j + 1))
                    if reused(g, 1):
                        dve.wait_ge(out_ps, upto(g - 1, GP, j + 1))
                    dve.tensor_tensor(mid[j][1][:], b_near[n][:, 0:D], mid[j][0][:],
                                      ALU.subtract).then_inc(mid_lo, 1)

                def residual(g, j):
                    dve.wait_ge(hr_ok, upto(g, GP, j + 1))
                    if reused(g, 1):
                        dve.wait_ge(L.x_new, upto(g - 1, GP, GP))
                    dve.tensor_tensor(L.pre[:, j, :], hr[:, j, :], K.x[:, gcols(g, j)],
                                      ALU.add).then_inc(L.pre_ok, 1)

                def scores(g):
                    split_scores(S, dve, g, b_s)
                    if reused(g, 1):
                        dve.wait_ge(S.t_ok, upto(g - 1, GP, GP))
                    si = b_s[:, 0:2 * GP].rearrange("p (g s) -> p g s", g=GP)[:, :, 1]
                    dve.tensor_scalar(S.bias[:], si, 1.0 / WK_SCALE, K.edge_bias[:], ALU.mult,
                                      ALU.add).then_inc(S.s_bias, 1)

                def leaky(g):
                    dve.wait_ge(S.t_ok, upto(g, GP, GP))
                    if reused(g, 1):
                        dve.wait_ge(S.e_ok, upto(g - 1, 1, 1))
                    dve.scalar_tensor_tensor(S.lr[:], S.t[:], 0.2, S.t[:], ALU.mult, ALU.max).then_inc(lr_ok, 1)

                def transition(g, p):
                    dve.wait_ge(S.e_ok, upto(g, 1, 1))
                    dve.wait_ge(adj_in[p], 8 * (g - p) + 16)
                    if reused(g, 1):
                        dve.wait_ge(tf_ok, upto(g - 1, 1, 1))
                    dve.tensor_tensor(S.u[:], S.e[:], adjn[p][:].rearrange("p g n -> p (g n)"),
                                      ALU.mult).then_inc(S.u_ok, 1)
                    dve.wait_ge(S.u_ok, upto(g, 1, 1))
                    u = S.u[:].rearrange("p (g n) -> p g n", g=GP)
                    dve.tensor_reduce(rsum[:], u, AX.X, ALU.add).then_inc(rsum_ok, 1)
                    dve.wait_ge(rsum_ok, upto(g, 1, 1))
                    dve.tensor_scalar(reps[:], rsum[:], 1e-12, None, ALU.add).then_inc(reps_ok, 1)
                    dve.wait_ge(reps_ok, upto(g, 1, 1))
                    dve.reciprocal(rinv[:], reps[:]).then_inc(rinv_ok, 1)
                    dve.wait_ge(rinv_ok, upto(g, 1, 1))
                    if reused(g, 1):
                        dve.wait_ge(t_hi, upto(g - 1, 1, 1))
                        dve.wait_ge(t_lo, upto(g - 1, 1, 1))
                    dve.tensor_tensor(tf[:].rearrange("p (g n) -> p g n", g=GP), u,
                                      rinv[:, :, None].to_broadcast([128, GP, N]), ALU.mult).then_inc(tf_ok, 1)

                def copy_tT(g, p):
                    dve.wait_ge(tT_ps, upto(g, 1, 1))
                    if reused(g):
                        dve.wait_ge(out_ps, upto(g - 2, GP, GP))
                    dve.tensor_copy(tT[p][:].rearrange("p s c -> p (s c)"), b_t[:].bitcast(F16)).then_inc(tT_sb, 1)

                def step(g, p, has):
                    q = 1 - p
                    if has(1):
                        for s in range(2):
                            copy_xT(K, F, dve, g + 1, q, b_xT, s, (near_ps, GP))
                    if has(0):
                        far_low(g, 0)
                    if has(1):
                        scores(g + 1)
                    if has(0):
                        far_low(g, 1)
                    if has(-1):
                        residual(g - 1, 3)
                        norm_rows(L, dve, g - 1)
                    if has(1):
                        leaky(g + 1)
                    if has(0):
                        mid_low(g, 0, 0)
                        far_low(g, 2)
                    if has(-1):
                        norm_shift(L, dve, g - 1)
                    if has(1):
                        transition(g + 1, q)
                    if has(0):
                        mid_low(g, 1, 1)
                        mid_low(g, 2, 2)
                        far_low(g, 3)
                        residual(g, 0)
                        residual(g, 1)
                        mid_low(g, 3, 0)
                        residual(g, 2)
                    if has(1):
                        copy_tT(g + 1, q)
                over_groups(dve, step, 2, 1)

            @block.gpsimd
            def _(pool):
                def step(g, p, has):
                    if has(2):
                        x_low(K, F, pool, g + 2, p)
                    if has(-1):
                        norm_power(K, L, pool, g - 1, K.eps)
                    if has(1):
                        pool.wait_ge(t_hi, upto(g + 1, 1, 1))
                        if reused(g + 1, 1):
                            pool.wait_ge(tT_ps, upto(g, 1, 1))
                        pool.tensor_tensor(ts[1][:], tf[:], ts[0][:], ALU.subtract).then_inc(t_lo, 1)
                over_groups(pool, step, 2, 1)


def layer3(nc, K):
    ctx = ExitStack()
    with ctx:
        def sb(name, shape, dt=F32):
            return ctx.enter_context(nc.sbuf_tensor(f"l3_{name}", shape, dt))

        def sem(name):
            return ctx.enter_context(nc.semaphore(f"l3_{name}"))

        bank = K.bank
        b_xT, b_s, b_t, b_xw, b_out = bank[0:2], bank[2], bank[3], bank[4:6], bank[6:8]
        F, L, S = front(nc, K, ctx, "l3"), norm(nc, ctx, "l3"), attention_front(nc, K, ctx, "l3", 1)
        us = [[sb(f"U{p}_{s}", [128, C], F16) for s in ("hi", "lo")] for p in range(2)]
        xw = [sb("xw_hi", [128, GP, D + 1], F16), sb("xw_lo", [128, GP, D + 1], F16)]
        rrec, rfac = sb("rrec", [128, GP]), sb("rfac", [128, GP])
        res = [sb(f"result{p}", [128, GP, D]) for p in range(2)]
        lr_ok, u_hi, u_lo, one_ok, xw_ps, xw_hi, xw_lo, out_ps, rrec_ok, rfac_ok = map(
            sem, ("lr_ok", "u_hi", "u_lo", "one_ok", "xw_ps", "xw_hi", "xw_lo", "out_ps", "rrec_ok", "rfac_ok"))
        stored_p = [sem(f"stored{p}") for p in range(2)]

        with nc.Block() as block:
            @block.sync
            def _(sp):
                def store(g, p, has):
                    if has(0):
                        sp.wait_ge(L.x_new, upto(g, GP, GP))
                        sp.dma_start(K.od[:, bass.ds(g * GP, GP), :], res[p][:]).then_inc(stored_p[p], 16)
                over_groups(sp, store, 0, 0)
                for p in range(2):
                    sp.wait_ge(stored_p[p], 16 * (G // 2))

            @block.tensor
            def _(pe):
                def project(g, p, j):
                    if j >= 2 or reused(g, 1):
                        pe.wait_ge(xw_lo, upto(g, GP, j - 1))
                    c = slice(j * N, (j + 1) * N)
                    for d in range(DT):
                        m = triple(nc, b_xw[j % 2][:, 0:D], [s[:, d, c] for s in F.xT[p]],
                                   [w[:, d, 0:D] for w in K.w3], start=d == 0, stop=d == DT - 1)
                    m.then_inc(xw_ps, 1)

                def aggregate(g, p, j):
                    if j == 0:
                        pe.wait_ge(u_hi, upto(g, 1, 1))
                        pe.wait_ge(u_lo, upto(g, 1, 1))
                        if isinstance(g, int) and g == 0:
                            pe.wait_ge(one_ok, 2)
                    pe.wait_ge(xw_hi, upto(g, GP, j + 1))
                    pe.wait_ge(xw_lo, upto(g, GP, j + 1))
                    if j >= 2 or reused(g, 1):
                        pe.wait_ge(L.pre_ok, upto(g, GP, j - 1))
                    triple(nc, b_out[j % 2][:, 0:D + 1], [s[:, j * N:(j + 1) * N] for s in us[p]],
                           [s[:, j, :] for s in xw]).then_inc(out_ps, 1)

                def step(g, p, has):
                    q = 1 - p
                    if has(1):
                        transpose_x(K, F, pe, g + 1, q, b_xT)
                    if has(0):
                        project(g, p, 0)
                        project(g, p, 1)
                    if has(1):
                        node_scores(nc, K, F, S, pe, g + 1, q, b_s, K.w3, D)
                    if has(0):
                        project(g, p, 2)
                        aggregate(g, p, 0)
                        project(g, p, 3)
                    if has(1):
                        spread_scores(nc, K, S, pe, g + 1, b_t, S.t_ok, GP)
                    if has(0):
                        aggregate(g, p, 1)
                        aggregate(g, p, 2)
                        aggregate(g, p, 3)
                over_groups(pe, step, 2, 0)

            @block.scalar
            def _(act):
                def xw_high(g, j):
                    act.wait_ge(xw_ps, upto(g, GP, j + 1))
                    if reused(g, 1):
                        act.wait_ge(out_ps, upto(g - 1, GP, j + 1))
                    act.activation(xw[0][:, j, 0:D], b_xw[j % 2][:, 0:D], ACT.Copy).then_inc(xw_hi, 1)

                def step(g, p, has):
                    q = 1 - p
                    if has(2):
                        x_high(K, F, act, g + 2, p)
                    if has(0):
                        for j in range(GP):
                            xw_high(g, j)
                    if has(-1):
                        act.wait_ge(L.nmr_ok, upto(g - 1, 1, 1))
                        if reused(g - 1):
                            act.wait_ge(stored_p[q], 8 * ((g - 1) - q))
                        for j in range(GP):
                            act.activation(res[q][:, j, :], L.pre[:, j, :], ACT.Identity,
                                           bias=L.nmr[:, j:j + 1], scale=L.rstd[:, j:j + 1]).then_inc(L.x_new, 1)
                    if has(1):
                        act.wait_ge(S.sj_ps, upto(g + 1, 1, 1))
                        act.wait_ge(S.s_bias, upto(g + 1, 1, 1))
                        if reused(g + 1, 1):
                            act.wait_ge(lr_ok, upto(g, 1, 1))
                        for j in range(GP):
                            act.activation(S.t[:, j * N:(j + 1) * N], b_t[:, j * N:(j + 1) * N], ACT.Tanh,
                                           bias=S.bias[:, j:j + 1], scale=0.125).then_inc(S.t_ok, 1)
                        act.wait_ge(lr_ok, upto(g + 1, 1, 1))
                        if reused(g + 1, 1):
                            act.wait_ge(S.u_ok, upto(g, 1, 1))
                        act.activation(S.e[:], S.lr[:], ACT.Exp, scale=8.0).then_inc(S.e_ok, 1)
                        act.wait_ge(S.u_ok, upto(g + 1, 1, 1))
                        if reused(g + 1):
                            act.wait_ge(out_ps, upto(g - 1, GP, GP))
                        act.activation(us[q][0][:], S.u[:], ACT.Copy).then_inc(u_hi, 1)
                over_groups(act, step, 2, 1)

            @block.vector
            def _(dve):
                def xw_low(g, j):
                    dve.wait_ge(xw_hi, upto(g, GP, j + 1))
                    if reused(g, 1):
                        dve.wait_ge(out_ps, upto(g - 1, GP, j + 1))
                    dve.tensor_tensor(xw[1][:, j, 0:D], b_xw[j % 2][:, 0:D], xw[0][:, j, 0:D],
                                      ALU.subtract).then_inc(xw_lo, 1)

                def scores(g):
                    split_scores(S, dve, g, b_s)
                    if reused(g, 1):
                        dve.wait_ge(S.t_ok, upto(g - 1, GP, GP))
                    dve.tensor_scalar(S.bias[:], b_s[:, 0:GP], 0.125, None, ALU.mult).then_inc(S.s_bias, 1)

                def weights(g):
                    dve.wait_ge(S.t_ok, upto(g, GP, GP))
                    if reused(g, 1):
                        dve.wait_ge(S.e_ok, upto(g - 1, 1, 1))
                    dve.scalar_tensor_tensor(S.lr[:], S.t[:], 0.1, S.t[:], ALU.mult, ALU.max).then_inc(lr_ok, 1)
                    dve.wait_ge(S.e_ok, upto(g, 1, 1))
                    if reused(g, 1):
                        dve.wait_ge(u_hi, upto(g - 1, 1, 1))
                        dve.wait_ge(u_lo, upto(g - 1, 1, 1))
                    dve.tensor_tensor(S.u[:], S.e[:], K.at[:, acols(g)], ALU.mult).then_inc(S.u_ok, 1)

                def residual(g, j):
                    dve.wait_ge(out_ps, upto(g, GP, j + 1))
                    b = b_out[j % 2]
                    dve.reciprocal(rrec[:, j:j + 1], b[:, D:D + 1]).then_inc(rrec_ok, 1)
                    dve.wait_ge(rrec_ok, upto(g, GP, j + 1))
                    dve.scalar_tensor_tensor(rfac[:, j:j + 1], rrec[:, j:j + 1], 1.0 / W3_SCALE,
                                             K.asum[:, bass.ds(g * GP + j, 1)], ALU.mult,
                                             ALU.mult).then_inc(rfac_ok, 1)
                    dve.wait_ge(rfac_ok, upto(g, GP, j + 1))
                    if reused(g, 1):
                        dve.wait_ge(L.x_new, upto(g - 1, GP, GP))
                    dve.scalar_tensor_tensor(L.pre[:, j, :], b[:, 0:D], rfac[:, j:j + 1], K.x[:, gcols(g, j)],
                                             ALU.mult, ALU.add).then_inc(L.pre_ok, 1)

                dve.memset(xw[0][:, :, D:D + 1], 1.0).then_inc(one_ok, 1)
                dve.memset(xw[1][:, :, D:D + 1], 0.0).then_inc(one_ok, 1)

                def step(g, p, has):
                    q = 1 - p
                    if has(1):
                        for s in range(2):
                            copy_xT(K, F, dve, g + 1, q, b_xT, s, (xw_ps, GP))
                    if has(-1):
                        residual(g - 1, 3)
                        norm_rows(L, dve, g - 1)
                    if has(0):
                        xw_low(g, 0)
                        xw_low(g, 1)
                    if has(1):
                        scores(g + 1)
                    if has(0):
                        xw_low(g, 2)
                        xw_low(g, 3)
                    if has(-1):
                        norm_shift(L, dve, g - 1)
                    if has(1):
                        weights(g + 1)
                    if has(0):
                        residual(g, 0)
                        residual(g, 1)
                        residual(g, 2)
                over_groups(dve, step, 2, 1)

            @block.gpsimd
            def _(pool):
                def step(g, p, has):
                    q = 1 - p
                    if has(2):
                        x_low(K, F, pool, g + 2, p)
                    if has(-1):
                        norm_power(K, L, pool, g - 1, K.eps)
                    if has(1):
                        pool.wait_ge(u_hi, upto(g + 1, 1, 1))
                        if reused(g + 1):
                            pool.wait_ge(out_ps, upto(g - 1, GP, GP))
                        pool.tensor_tensor(us[q][1][:], S.u[:], us[q][0][:], ALU.subtract).then_inc(u_lo, 1)
                over_groups(pool, step, 2, 1)


_INS = ['x', 'adj', 'L0_gnn_W1', 'L0_gnn_b1', 'L0_gnn_gamma', 'L0_gnn_beta', 'L0_gnn_W2', 'L0_gnn_b2',
        'L1_gnn_W_qk', 'L1_gnn_W_v', 'L2_gnn_Wv', 'L2_gnn_bv', 'L2_gnn_aw', 'L2_gnn_ab', 'L2_gnn_Wk',
        'L2_gnn_bk', 'L3_gnn_w', 'L3_gnn_a']


def kernel(**inputs):
    import concourse.bacc as bacc
    from concourse.bass_utils import run_bass_kernel_spmd

    nc = bacc.Bacc("TRN2", target_bir_lowering=False, num_devices=1)
    arrays, args = {}, []
    for name in _INS:
        a = np.ascontiguousarray(inputs[name])
        arrays[f"in_{name}"] = a
        args.append(nc.dram_tensor(f"in_{name}", a.shape, mybir.dt.from_np(a.dtype), kind="ExternalInput").ap())
    out = nc.dram_tensor("out", (GRAPHS, N, D), F32, kind="ExternalOutput").ap()
    build(nc, *args, out)
    r = run_bass_kernel_spmd(nc, [arrays], core_ids=[0])
    return r.results[0]["out"]
```

```python
import numpy as np
import concourse.bass as bass
from concourse import mybir
from contextlib import ExitStack

F32 = mybir.dt.float32
F16 = mybir.dt.float16
ALU = mybir.AluOpType
ACT = mybir.ActivationFunctionType
AX = mybir.AxisListType

GRAPHS, N, D, H = 64, 128, 256, 512
GP = 4
G = GRAPHS // GP
C = GP * N
DT = D // 128
HT = H // 128
QK = 64
EPS = 1e-5
W_SCALE = 64.0
WK_SCALE = 256.0
W3_SCALE = 16.0
CNT_SCALE = 128.0


class Parts:
    pass


def upto(g, per, k):
    return g * per + k


def xcols(g):
    return bass.ds(g * (GP * D), GP * D)


def gcols(g, j):
    return bass.ds(g * (GP * D) + j * D, D)


def acols(g):
    return bass.ds(g * C, C)


def over_groups(eng, step, lead, lag):
    first = 4 if lag else 2
    for g in range(-lead, first):
        step(g, g % 2, lambda k, g=g: 0 <= g + k < G)
    with eng.Fori(first // 2, G // 2 - 1) as pair:
        step(pair * 2, 0, lambda k: True)
        step(pair * 2 + 1, 1, lambda k: True)
    for g in range(G - 2, G + lag):
        step(g, g % 2, lambda k, g=g: 0 <= g + k < G)


def reused(g, back=2):
    return not isinstance(g, int) or g >= back


def triple(nc, out, lhs, rhs, start=True, stop=True, **kw):
    nc.tensor.matmul(out, lhs[0], rhs[1], start=start, stop=False, **kw)
    nc.tensor.matmul(out, lhs[1], rhs[0], start=False, stop=False, **kw)
    return nc.tensor.matmul(out, lhs[0], rhs[0], start=False, stop=stop, **kw)



def build(nc, x, adj, W1, b1, gamma, beta, W2, b2, W_qk, W_v, Wv, bv, aw, ab, Wk, bk, w3, a3, out,
          layers=4):
    ctx = ExitStack()
    with ctx:
        def sb(name, shape, dt=F32):
            return ctx.enter_context(nc.sbuf_tensor(name, shape, dt))

        def halves(name, shape):
            return [sb(f"{name}_{s}", shape, F16) for s in ("hi", "lo")]

        K = Parts()
        K.bank = [ctx.enter_context(nc.psum_tensor(f"bank{i}", [128, 512], F32)) for i in range(8)]
        K.x = sb("x_resident", [128, GRAPHS * D])
        K.at = sb("adjT_resident", [128, GRAPHS * N])
        K.asum = sb("adj_row_sums", [128, GRAPHS])
        K.ident = sb("ident", [128, 128])
        K.ident16 = sb("ident16", [128, 128], F16)
        K.ones = sb("ones", [128, 128])
        K.ones16 = sb("ones16", [128, 128], F16)
        K.minus_half, K.quarter, K.inv_d, K.eps, K.eps_quarter = (
            sb(name, [128, GP]) for name in ("minus_half", "quarter", "inv_d", "eps", "eps_quarter"))
        K.w1 = halves("W1T", [128, DT, H])
        K.w2 = halves("W2T", [128, HT, D + 1])
        K.qkv = halves("qkvT", [128, DT, 2 * QK + D])
        K.wk = halves("Wk", [128, DT, 3 * D + 2])
        K.w3 = halves("w3", [128, DT, D + 1])
        K.b1 = sb("b1_col", [128, HT])
        K.w2beta = sb("W2beta_rows", [128, D])
        K.edge_bias = sb("edge_bias", [128, 1])
        K.b2row = sb("b2_parts", [128, D], F16)
        K.bkrow = sb("bk_parts", [128, D], F16)

        K.xd = x.rearrange("g n d -> n g d")
        K.ad = adj.rearrange("g n e -> n g e")
        K.od = out.rearrange("g n d -> n g d")
        K.adjn = [sb(f"adj{p}", [128, GP, N]) for p in range(2)]
        K.adj_in, K.x_in = ([ctx.enter_context(nc.semaphore(f"{name}{p}")) for p in range(2)]
                            for name in ("adj_in", "x_in"))
        setup(nc, K, x, adj, W1, b1, gamma, beta, W2, b2, W_qk, W_v, Wv, bv, aw, ab, Wk, bk, w3, a3)
        layer0(nc, K)
        if layers >= 2:
            layer1(nc, K)
        if layers >= 3:
            layer2(nc, K)
        if layers >= 4:
            layer3(nc, K)
        else:
            with nc.semaphore("out_done") as out_done, nc.Block() as block:
                @block.sync
                def _(sp):
                    sp.dma_start(K.od, K.x[:, :].rearrange("p (g d) -> p g d", g=GRAPHS)).then_inc(out_done, 16)
                    sp.wait_ge(out_done, 16)


def setup(nc, K, x, adj, W1, b1, gamma, beta, W2, b2, W_qk, W_v, Wv, bv, aw, ab, Wk, bk, w3, a3):
    ctx = ExitStack()
    with ctx:
        def sb(name, shape, dt=F32):
            return ctx.enter_context(nc.sbuf_tensor(name, shape, dt))

        def sem(name):
            return ctx.enter_context(nc.semaphore(name))

        w1n, w2n = sb("w1n", [128, HT, D]), sb("w2n", [128, DT, H])
        wqn, wvn = sb("wqn", [128, D]), sb("wvn", [128, DT, D])
        gam, bet, gam_s = sb("gam", [128, HT]), sb("bet", [128, HT]), sb("gam_scaled", [128, HT])
        b2n, bkn, bks = sb("b2n", [128, D]), sb("bkn", [128, 3, D]), sb("bk_sums", [128, 3, D])
        l2v, l2k = sb("l2v", [128, DT, D]), sb("l2k", [128, 3, DT, D])
        awb, bvb, abb = sb("awb", [128, 2 * D]), sb("bvb", [128, D]), sb("abb", [128, 1])
        w3n, a3b = sb("w3n", [128, DT, D]), sb("a3b", [128, D])
        w2g, w2b, w2c = sb("w2_gamma", [128, HT, D]), sb("w2_beta", [128, HT, D]), sb("w2_centred", [128, HT, D + 1])
        wkf, w3f = sb("wkf", [128, DT, 3 * D + 2]), sb("w3f", [128, DT, D + 1])
        prod, ssum, edge = sb("prod", [128, 8, D]), sb("ssum", [128, DT, 2]), sb("edge", [128, 4])
        mean = sb("w2_mean", [128, D])
        w12_in, vec_in, rows_in, rest_in = map(sem, ("w12_in", "vec_in", "rows_in", "rest_in"))
        const = sem("const")
        wT_ps, fold_ps = map(sem, ("wT_ps", "fold_ps"))
        folding = sem("folding")
        w2g_ok, w2c_ok, w12_hi, qkv_hi = map(sem, ("w2g_ok", "w2c_ok", "w12_hi", "qkv_hi"))
        prod_ok, wk3_part, wk3_hi, bk_scaled, row_hi = map(
            sem, ("prod_ok", "wk3_part", "wk3_hi", "bk_scaled", "row_hi"))
        with nc.Block() as block:
            rest = [
                (wqn[:], W_qk), (wvn[:], W_v.rearrange("(t p) d -> p t d", p=128)),
                (l2k[:], Wk.rearrange("k (t p) o -> p k t o", p=128)),
                (l2v[:], Wv.rearrange("(t p) o -> p t o", p=128)),
                (w3n[:], w3.rearrange("(t p) o -> p t o", p=128)),
                (awb[:], aw.rearrange("a b -> b a").to_broadcast([128, 2 * D])),
                (bvb[:], bv.rearrange("(a b) -> a b", a=1).to_broadcast([128, D])),
                (abb[:], ab.rearrange("(a b) -> a b", a=1).to_broadcast([128, 1])),
                (a3b[:], a3.rearrange("(a b) -> a b", a=1).to_broadcast([128, D])),
            ]
            rest_loaded = 16 * len(rest)
            rows = [(b2n[r:r + 1, :], b2.rearrange("(a b) -> a b", a=1)) for r in (0, 32)]
            rows += [(bkn[r:r + 1, :, :], bk.rearrange("(a k) b -> a k b", a=1)) for r in (0, 32)]

            @block.sync
            def _(sp):
                sp.dma_start(w2n[:], W2.rearrange("(t p) h -> p t h", p=128)).then_inc(w12_in, 16)
                sp.dma_start(w1n[:], W1.rearrange("(t p) d -> p t d", p=128)).then_inc(w12_in, 16)
                for g in range(2):
                    load_adj(K, sp, g, g)
                for dst, src in rest:
                    sp.dma_start(dst, src).then_inc(rest_in, 16)
                for g in range(2):
                    load_x(K, sp, g, g)

            @block.gpsimd
            def _(pool):
                for m in (K.ident, K.ident16):
                    pool.memset(m[:], 0.0).then_inc(const, 1)
                pool.wait_ge(const, 2)
                for m in (K.ident, K.ident16):
                    pool.affine_select(out=m[:], in_=m[:], compare_op=ALU.not_equal, fill=1.0, base=0,
                                       pattern=[[-1, 128]], channel_multiplier=1).then_inc(const, 1)
                pool.memset(b2n[:], 0.0).then_inc(const, 1)
                pool.memset(bkn[:], 0.0).then_inc(const, 1)
                pool.memset(K.ones[:], 1.0).then_inc(const, 1)
                for m, value in ((K.ones16, 1.0), (K.minus_half, -0.5), (K.quarter, 0.25),
                                 (K.inv_d, 1.0 / D), (K.eps, EPS), (K.eps_quarter, 0.25 * EPS)):
                    pool.memset(m[:], value)
                pool.wait_ge(rows_in, 16 * len(rows))
                pool.tensor_tensor(bks[:, 0, :], bkn[:, 0, :], bkn[:, 1, :], ALU.add).then_inc(const, 1)
                pool.wait_ge(const, 8)
                pool.tensor_tensor(bks[:, 1, :], bks[:, 0, :], bkn[:, 2, :], ALU.add).then_inc(const, 1)
                pool.wait_ge(wk3_hi, 1)
                pool.tensor_tensor(K.w3[1][:], w3f[:], K.w3[0][:], ALU.subtract)
                pool.wait_ge(wk3_hi, 2)
                pool.tensor_tensor(K.wk[1][:], wkf[:], K.wk[0][:], ALU.subtract)

            @block.tensor
            def _(pe):
                pe.wait_ge(const, 4)
                pe.wait_ge(w12_in, 32)
                for h in range(HT):
                    for d in range(DT):
                        c = (h % 2) * D + d * 128
                        m = pe.transpose(K.bank[2 + h // 2][:, c:c + 128],
                                         w2n[:, d, h * 128:(h + 1) * 128], K.ident[:])
                m.then_inc(wT_ps, 1)
                for d in range(DT):
                    for h in range(HT):
                        m = pe.transpose(K.bank[d][:, h * 128:(h + 1) * 128],
                                         w1n[:, h, d * 128:(d + 1) * 128], K.ident[:])
                m.then_inc(wT_ps, 1)
                pe.wait_ge(const, 7)
                pe.wait_ge(w2g_ok, 2)
                for h in range(HT):
                    m = pe.matmul(K.bank[6][:, 0:D], K.ones[:], w2g[:, h, :], start=h == 0, stop=h == HT - 1)
                m.then_inc(fold_ps, 1)
                for h in range(HT):
                    m = pe.matmul(K.bank[7][:, 0:D], K.ones[:], w2b[:, h, :], start=h == 0, stop=h == HT - 1)
                m.then_inc(fold_ps, 1)
                pe.wait_ge(rest_in, rest_loaded)
                for d in range(DT):
                    pe.transpose(K.bank[4 + d][:, 0:128], wqn[:, d * 128:(d + 1) * 128], K.ident[:])
                    for e in range(DT):
                        m = pe.transpose(K.bank[4 + d][:, (e + 1) * 128:(e + 2) * 128],
                                         wvn[:, e, d * 128:(d + 1) * 128], K.ident[:])
                m.then_inc(wT_ps, 1)

            @block.scalar
            def _(act):
                with nc.allow_non_contiguous_dma(reason="three short vectors, a value per partition"):
                    for dst, src in ((gam, gamma), (bet, beta), (K.b1, b1)):
                        act.dma_start(dst[:], src.rearrange("(t p) -> p t", p=128)).then_inc(vec_in, 16)
                act.wait_ge(const, 6)
                for dst, src in rows:
                    act.dma_start(dst, src).then_inc(rows_in, 16)
                act.wait_ge(wT_ps, 2)
                for d in range(DT):
                    act.activation(K.w1[0][:, d, :], K.bank[d][:], ACT.Copy, scale=W_SCALE).then_inc(w12_hi, 1)
                act.wait_ge(w2c_ok, HT + 1)
                act.activation(K.w2[0][:], w2c[:], ACT.Copy).then_inc(w12_hi, 1)
                act.wait_ge(const, 9)
                act.activation(bks[:, 2, :], bks[:, 1, :], ACT.Copy, scale=WK_SCALE).then_inc(bk_scaled, 1)
                act.activation(K.b2row[:], b2n[:], ACT.Copy).then_inc(row_hi, 1)
                act.wait_ge(rest_in, rest_loaded)
                act.activation(w3f[:, :, 0:D], w3n[:], ACT.Copy, scale=W3_SCALE).then_inc(wk3_part, 1)
                for c, k in ((0, 2), (D + 2, 1), (2 * D + 2, 0)):
                    act.activation(wkf[:, :, c:c + D], l2k[:, k], ACT.Copy, scale=WK_SCALE).then_inc(wk3_part, 1)
                act.wait_ge(wk3_part, 7)
                act.activation(K.w3[0][:], w3f[:], ACT.Copy).then_inc(wk3_hi, 1)
                act.wait_ge(wT_ps, 3)
                for d in range(DT):
                    act.activation(K.qkv[0][:, d, :], K.bank[4 + d][:, 0:2 * QK + D], ACT.Copy,
                                   scale=W_SCALE).then_inc(qkv_hi, 1)
                act.activation(K.wk[0][:], wkf[:], ACT.Copy).then_inc(wk3_hi, 1)
                act.wait_ge(bk_scaled, 1)
                act.activation(K.bkrow[:], bks[:, 2, :], ACT.Copy).then_inc(row_hi, 1)

            @block.vector
            def _(dve):
                dve.memset(w2c[:, :, D:D + 1], W_SCALE / H).then_inc(w2c_ok, 1)
                dve.wait_ge(vec_in, 48)
                dve.tensor_scalar(gam_s[:], gam[:], W_SCALE, None, ALU.mult).then_inc(folding, 1)
                dve.wait_ge(folding, 1)
                dve.wait_ge(wT_ps, 1)
                for h in range(HT):
                    src = K.bank[2 + h // 2][:, (h % 2) * D:(h % 2 + 1) * D]
                    m = dve.tensor_scalar(w2g[:, h, :], src, gam_s[:, h:h + 1], None, ALU.mult)
                m.then_inc(w2g_ok, 1)
                for h in range(HT):
                    src = K.bank[2 + h // 2][:, (h % 2) * D:(h % 2 + 1) * D]
                    m = dve.tensor_scalar(w2b[:, h, :], src, bet[:, h:h + 1], None, ALU.mult)
                m.then_inc(w2g_ok, 1)
                dve.wait_ge(w12_hi, DT)
                for d in range(DT):
                    dve.scalar_tensor_tensor(K.w1[1][:, d, :], K.bank[d][:], W_SCALE, K.w1[0][:, d, :],
                                             ALU.mult, ALU.subtract)
                dve.wait_ge(fold_ps, 1)
                dve.tensor_scalar(mean[:], K.bank[6][:, 0:D], 1.0 / H, None, ALU.mult).then_inc(folding, 1)
                dve.wait_ge(folding, 2)
                for h in range(HT):
                    dve.tensor_tensor(w2c[:, h, 0:D], w2g[:, h, :], mean[:], ALU.subtract).then_inc(w2c_ok, 1)
                dve.wait_ge(fold_ps, 2)
                dve.tensor_copy(K.w2beta[:], K.bank[7][:, 0:D])
                dve.wait_ge(rest_in, rest_loaded)
                for d in range(DT):
                    dve.tensor_tensor(prod[:, 4 + d, :], w3n[:, d, :], a3b[:], ALU.mult).then_inc(prod_ok, 1)
                for d in range(DT):
                    for s in range(2):
                        dve.tensor_tensor(prod[:, 2 * d + s, :], l2v[:, d, :], awb[:, s * D:(s + 1) * D],
                                          ALU.mult).then_inc(prod_ok, 1)
                for s in range(2):
                    dve.tensor_tensor(prod[:, 6 + s, :], bvb[:], awb[:, s * D:(s + 1) * D],
                                      ALU.mult).then_inc(prod_ok, 1)
                dve.wait_ge(prod_ok, 8)
                for d in range(DT):
                    dve.tensor_reduce(w3f[:, d, D:D + 1], prod[:, 4 + d, :], AX.X, ALU.add).then_inc(wk3_part, 1)
                for d in range(DT):
                    dve.tensor_reduce(ssum[:, d, :], prod[:, 2 * d:2 * d + 2, :], AX.X, ALU.add).then_inc(folding, 1)
                dve.tensor_reduce(edge[:, 0:2], prod[:, 6:8, :], AX.X, ALU.add).then_inc(folding, 1)
                dve.wait_ge(folding, 4)
                dve.tensor_scalar(wkf[:, :, D:D + 2], ssum[:], WK_SCALE, None, ALU.mult).then_inc(wk3_part, 1)
                dve.wait_ge(w12_hi, DT + 1)
                dve.tensor_tensor(K.w2[1][:], w2c[:], K.w2[0][:], ALU.subtract)
                dve.wait_ge(folding, 5)
                dve.tensor_tensor(edge[:, 2:3], edge[:, 0:1], edge[:, 1:2], ALU.add).then_inc(folding, 1)
                dve.wait_ge(folding, 6)
                dve.tensor_tensor(K.edge_bias[:], edge[:, 2:3], abb[:], ALU.add)
                dve.wait_ge(qkv_hi, DT)
                for d in range(DT):
                    dve.scalar_tensor_tensor(K.qkv[1][:, d, :], K.bank[4 + d][:, 0:2 * QK + D], W_SCALE,
                                             K.qkv[0][:, d, :], ALU.mult, ALU.subtract)
                low = slice(32, 33)
                dve.wait_ge(row_hi, 2)
                dve.tensor_tensor(K.b2row[low, :], b2n[low, :], K.b2row[low, :], ALU.subtract)
                dve.tensor_tensor(K.bkrow[low, :], bks[low, 2, :], K.bkrow[low, :], ALU.subtract)


def load_adj(K, sp, g, p):
    sp.dma_start(K.adjn[p][:], K.ad[:, bass.ds(g * GP, GP), :]).then_inc(K.adj_in[p], 16)


def load_x(K, sp, g, p):
    sp.dma_start(K.x[:, xcols(g)].rearrange("p (g d) -> p g d", g=GP),
                 K.xd[:, bass.ds(g * GP, GP), :]).then_inc(K.x_in[p], 16)


def layer0(nc, K):
    ctx = ExitStack()
    with ctx:
        def sb(name, shape, dt=F32):
            return ctx.enter_context(nc.sbuf_tensor(name, shape, dt))

        def sem(name):
            return ctx.enter_context(nc.semaphore(name))

        def halves(name, shape):
            return [sb(f"{name}_{s}", shape, F16) for s in ("hi", "lo")]

        bank = K.bank
        b_adj, b_gram = bank[0], bank[1]
        b_mix, b_hid, b_z = bank[2:4], bank[4:6], bank[6:8]

        adjn = K.adjn
        inc = [sb(f"incT{p}", [128, C], F16) for p in range(2)]
        wcol = halves("wcol", [128, GP])
        cnt, cnt1, rcnt = sb("cnt", [128, GP]), sb("cnt1", [128, GP]), sb("rcnt", [128, GP])
        rcs = halves("rcs", [128, GP])
        incb = [halves(f"incB{p}", [128, C]) for p in range(2)]
        dcl, drc, dpos, dinv = (sb(f"d{i}", [128, GP]) for i in range(4))
        dis = halves("dis", [128, GP])
        dbc, pf = sb("dbc", [128, C]), sb("pf", [128, C])
        ps = [halves(f"P{p}", [128, C]) for p in range(2)]
        xs = [halves(f"x{p}", [128, GP, D]) for p in range(2)]
        px = [halves(f"px{p}", [128, DT, C]) for p in range(2)]
        hf = sb("hf", [128, HT, C])
        hs = halves("h", [128, HT, C])
        hq, hqp, hqs = sb("hq", [128, HT, C]), sb("hq_partial", [128, 2, C]), sb("hqs", [128, C])
        zf, zn = sb("zf", [128, GP, D + 2]), sb("zn", [128, GP, D])
        zs = halves("z", [128, GP, D])
        zm2, zvar, zrs = sb("zm2", [128, GP]), sb("zvar", [128, GP]), sb("zrs", [128, GP])
        L = norm(nc, ctx, "l0")

        adj_in, x_in = K.adj_in, K.x_in
        adjT_ps, adjT_sb, inc_ok, wcol_ok, small, incb_ok = map(
            sem, ("adjT_ps", "adjT_sb", "inc_ok", "wcol_ok", "small", "incb_ok"))
        deg_ps, gram_ps, dinv_ok, dbc_ps, dbc_sb, pf_ok, p_hi, p_lo = map(
            sem, ("deg_ps", "gram_ps", "dinv_ok", "dbc_ps", "dbc_sb", "pf_ok", "p_hi", "p_lo"))
        x_hi, x_lo, px_ps, px_hi, px_lo = map(sem, ("x_hi", "x_lo", "px_ps", "px_hi", "px_lo"))
        hid_ps, hf_ok, h_hi, h_sq, h_lo, hqs_ok = map(
            sem, ("hid_ps", "hf_ok", "h_hi", "h_sq", "h_lo", "hqs_ok"))
        z_ps, zf_ok, zvar_ok, zrs_ok, zn_ok, z_hi, z_lo = map(
            sem, ("z_ps", "zf_ok", "zvar_ok", "zrs_ok", "zn_ok", "z_hi", "z_lo"))
        y_ps = sem("y_ps")
        dchain = sem("dchain")

        with nc.Block() as block:
            @block.sync
            def _(sp):
                def load(g, p, has):
                    if has(0) and reused(g):
                        sp.wait_ge(adjT_ps, upto(g - 2, 1, 1))
                        load_adj(K, sp, g, p)
                        sp.wait_ge(x_lo, upto(g - 2, 1, 1))
                        load_x(K, sp, g, p)
                over_groups(sp, load, 0, 0)

            @block.tensor
            def _(pe):
                def transpose_adj(g, p):
                    pe.wait_ge(adj_in[p], 8 * (g - p) + 16)
                    if reused(g, 1):
                        pe.wait_ge(dbc_sb, upto(g - 1, 1, 1))
                    for j in range(GP):
                        m = pe.transpose(b_adj[:, j * N:(j + 1) * N], adjn[p][:, j, :], K.ident[:])
                    m.then_inc(adjT_ps, 1)

                def hidden(g, p, h):
                    if h == 0:
                        pe.wait_ge(px_lo, upto(g, 2, 2))
                        pe.wait_ge(px_hi, upto(g, 2, 2))
                    if h >= 2 or reused(g, 1):
                        pe.wait_ge(hf_ok, upto(g, HT, h - 1))
                    for d in range(DT):
                        m = triple(nc, b_hid[h % 2][:], [w[:, d, h * 128:(h + 1) * 128] for w in K.w1],
                                   [s[:, d, :] for s in px[p]], start=d == 0, stop=d == DT - 1)
                    m.then_inc(hid_ps, 1)

                def gram(g, p):
                    pe.wait_ge(incb_ok, upto(g, 8, 8))
                    if reused(g, 1):
                        pe.wait_ge(pf_ok, upto(g - 1, 1, 1))
                    for j in range(GP):
                        c = slice(j * N, (j + 1) * N)
                        pe.matmul(b_gram[:, c], inc[p][:, c], incb[p][1][:, c], start=True, stop=False)
                        m = pe.matmul(b_gram[:, c], inc[p][:, c], incb[p][0][:, c], start=False, stop=True)
                    m.then_inc(gram_ps, 1)

                def degree(g, p):
                    pe.wait_ge(wcol_ok, upto(g, 2, 2))
                    pe.wait_ge(inc_ok, upto(g, 1, 1))
                    pe.wait_ge(adjT_sb, upto(g, 1, 1))
                    for j in range(GP):
                        c = slice(j * N, (j + 1) * N)
                        pe.matmul(b_adj[:, j:j + 1], inc[p][:, c], wcol[1][:, j:j + 1], start=True, stop=False)
                        m = pe.matmul(b_adj[:, j:j + 1], inc[p][:, c], wcol[0][:, j:j + 1], start=False, stop=True)
                    m.then_inc(deg_ps, 1)

                def spread_degrees(g, p):
                    pe.wait_ge(dinv_ok, upto(g, 2, 2))
                    for j in range(GP):
                        for i, s in enumerate((1, 0)):
                            m = pe.matmul(b_adj[:, j * N:(j + 1) * N], dis[s][:, j:j + 1].to_broadcast([128, 128]),
                                          K.ident16[:], start=i == 0, stop=i == 1)
                    m.then_inc(dbc_ps, 1)

                def mix_x(g, p, d):
                    if d == 0:
                        pe.wait_ge(x_hi, upto(g, 1, 1))
                        pe.wait_ge(x_lo, upto(g, 1, 1))
                        pe.wait_ge(p_hi, upto(g, 1, 1))
                        pe.wait_ge(p_lo, upto(g, 1, 1))
                    if reused(g, 2):
                        pe.wait_ge(L.pre_ok, upto(g - 2, 2, d + 1))
                    elif g == 1:
                        pe.wait_ge(px_lo, upto(0, 2, d + 1))
                    for j in range(GP):
                        c = slice(j * N, (j + 1) * N)
                        m = triple(nc, b_mix[d][:, c], [s[:, j, d * 128:(d + 1) * 128] for s in xs[p]],
                                   [s[:, c] for s in ps[p]])
                    m.then_inc(px_ps, 1)

                def project(g, j):
                    if j >= 2 or reused(g, 1):
                        pe.wait_ge(zf_ok, upto(g, GP, j - 1))
                    for h in range(HT):
                        if j == 0:
                            pe.wait_ge(h_lo, upto(g, HT, h + 1))
                        triple(nc, b_z[j % 2][:, 0:D + 1], [s[:, h, j * N:(j + 1) * N] for s in hs],
                               [w[:, h, :] for w in K.w2], start=h == 0, stop=h == HT - 1)

                def square_sums(g, j):
                    if j == 0:
                        pe.wait_ge(hqs_ok, upto(g, 3, 3))
                    pe.matmul(b_z[j % 2][:, D + 1:D + 2], hqs[:, j * N:(j + 1) * N], K.ones[:, 0:1],
                              start=True, stop=True).then_inc(z_ps, 1)

                def mix_z(g, p, i):
                    if isinstance(g, int) and g == G - 1:
                        pe.wait_ge(L.pre_ok, upto(g - 1, 2, i + 1))
                    elif i == 0:
                        pe.wait_ge(px_lo, upto(g + 1, 2, 2))
                    for jj in range(2):
                        j = 2 * i + jj
                        pe.wait_ge(z_hi, upto(g, GP, j + 1))
                        pe.wait_ge(z_lo, upto(g, GP, j + 1))
                        o = b_mix[i][:, jj * D:(jj + 1) * D]
                        pe.matmul(o, K.ones16[:], K.b2row[:], start=True, stop=False)
                        m = triple(nc, o, [s[:, j * N:(j + 1) * N] for s in ps[p]],
                                   [s[:, j, :] for s in zs], start=False)
                    m.then_inc(y_ps, 1)

                def step(g, p, has):
                    q = 1 - p
                    if has(-1):
                        project(g - 1, 3)
                        square_sums(g - 1, 3)
                    if has(0):
                        hidden(g, p, 0)
                        hidden(g, p, 1)
                        hidden(g, p, 2)
                        hidden(g, p, 3)
                    if has(1):
                        degree(g + 1, q)
                    if has(-1):
                        mix_z(g - 1, q, 0)
                        mix_z(g - 1, q, 1)
                    if has(1):
                        gram(g + 1, q)
                        spread_degrees(g + 1, q)
                    if has(0):
                        project(g, 0)
                        project(g, 1)
                        square_sums(g, 0)
                        square_sums(g, 1)
                    if has(2):
                        transpose_adj(g + 2, p)
                    if has(0):
                        project(g, 2)
                        square_sums(g, 2)
                    if has(1):
                        mix_x(g + 1, q, 0)
                        mix_x(g + 1, q, 1)
                over_groups(pe, step, 2, 1)

            @block.scalar
            def _(act):
                def hidden(g, h):
                    act.wait_ge(hid_ps, upto(g, HT, h + 1))
                    if reused(g, 1):
                        act.wait_ge(h_lo, upto(g - 1, HT, h + 1))
                        act.wait_ge(h_sq, upto(g - 1, HT, h + 1))
                    act.activation(hf[:, h, :], b_hid[h % 2][:], ACT.Relu, bias=K.b1[:, h:h + 1],
                                   scale=1.0 / W_SCALE).then_inc(hf_ok, 1)

                def square(g, h):
                    act.wait_ge(hf_ok, upto(g, HT, h + 1))
                    if reused(g, 1):
                        act.wait_ge(hqs_ok, upto(g - 1, 3, 3))
                    act.activation(hq[:, h, :], hf[:, h, :], ACT.Square).then_inc(h_sq, 1)

                def copy_z(g, j):
                    act.wait_ge(z_ps, upto(g, GP, j + 1))
                    if reused(g, 1):
                        act.wait_ge(zn_ok, upto(g - 1, GP, GP))
                    act.activation(zf[:, j, :], b_z[j % 2][:, 0:D + 2], ACT.Copy,
                                   scale=1.0 / W_SCALE).then_inc(zf_ok, 1)

                def z_high(g, j):
                    act.wait_ge(zn_ok, upto(g, GP, j + 1))
                    if reused(g, 1):
                        act.wait_ge(y_ps, upto(g - 1, 2, 2))
                    act.activation(zs[0][:, j, :], zn[:, j, :], ACT.Copy).then_inc(z_hi, 1)

                def x_high(g, p):
                    act.wait_ge(x_in[p], 8 * (g - p) + 16)
                    if reused(g):
                        act.wait_ge(px_ps, upto(g - 2, 2, 2))
                    act.activation(xs[p][0][:], K.x[:, xcols(g)].rearrange("p (g d) -> p g d", g=GP),
                                   ACT.Copy).then_inc(x_hi, 1)

                def copy_degrees(g):
                    act.wait_ge(dbc_ps, upto(g, 1, 1))
                    if reused(g, 1):
                        act.wait_ge(pf_ok, upto(g - 1, 1, 1))
                    act.activation(dbc[:], b_adj[:], ACT.Copy).then_inc(dbc_sb, 1)

                def operator_high(g, p):
                    act.wait_ge(pf_ok, upto(g, 1, 1))
                    if reused(g):
                        act.wait_ge(y_ps, upto(g - 2, 2, 2))
                    act.activation(ps[p][0][:], pf[:], ACT.Copy).then_inc(p_hi, 1)

                def mixed_high(g, p, d):
                    act.wait_ge(px_ps, upto(g, 2, d + 1))
                    if reused(g):
                        act.wait_ge(hid_ps, upto(g - 2, HT, HT))
                    act.activation(px[p][0][:, d, :], b_mix[d][:], ACT.Copy).then_inc(px_hi, 1)

                def copy_adj(g):
                    act.wait_ge(adjT_ps, upto(g, 1, 1))
                    act.activation(K.at[:, acols(g)], b_adj[:], ACT.Copy).then_inc(adjT_sb, 1)

                def step(g, p, has):
                    q = 1 - p
                    if has(0):
                        hidden(g, 0)
                    if has(-1):
                        z_high(g - 1, 0)
                    if has(0):
                        square(g, 0)
                    if has(-1):
                        z_high(g - 1, 1)
                    if has(0):
                        hidden(g, 1)
                    if has(-1):
                        z_high(g - 1, 2)
                    if has(0):
                        square(g, 1)
                    if has(-1):
                        z_high(g - 1, 3)
                    if has(0):
                        hidden(g, 2)
                        square(g, 2)
                        hidden(g, 3)
                    if has(1):
                        x_high(g + 1, q)
                    if has(-2):
                        norm_apply(K, L, act, g - 2, 0)
                    if has(0):
                        square(g, 3)
                    if has(-2):
                        norm_apply(K, L, act, g - 2, 1)
                        norm_apply(K, L, act, g - 2, 2)
                        norm_apply(K, L, act, g - 2, 3)
                    if has(1):
                        copy_degrees(g + 1)
                    if has(0):
                        copy_z(g, 0)
                    if has(1):
                        operator_high(g + 1, q)
                    if has(0):
                        copy_z(g, 1)
                        copy_z(g, 2)
                    if has(1):
                        mixed_high(g + 1, q, 0)
                        mixed_high(g + 1, q, 1)
                    if has(2):
                        copy_adj(g + 2)
                    if has(0):
                        copy_z(g, 3)
                over_groups(act, step, 2, 2)

            @block.vector
            def _(dve):
                def incidence(g, p):
                    dve.wait_ge(adjT_sb, upto(g, 1, 1))
                    if reused(g):
                        dve.wait_ge(deg_ps, upto(g - 2, 1, 1))
                    dve.tensor_scalar(inc[p][:], K.at[:, acols(g)], 0.0, None, ALU.not_equal).then_inc(inc_ok, 1)

                def edge_weights(g):
                    first = K.at[:, acols(g)].rearrange("p (g n) -> p g n", g=GP)[:, :, 0]
                    if reused(g, 1):
                        dve.wait_ge(deg_ps, upto(g - 1, 1, 1))
                    dve.tensor_scalar(wcol[0][:], first, 1.0, None, ALU.mult).then_inc(wcol_ok, 1)
                    dve.wait_ge(wcol_ok, upto(g, 2, 1))
                    dve.tensor_tensor(wcol[1][:], first, wcol[0][:], ALU.subtract).then_inc(wcol_ok, 1)

                def counts(g, p):
                    dve.wait_ge(inc_ok, upto(g, 1, 1))
                    dve.tensor_reduce(cnt[:], inc[p][:].rearrange("p (g n) -> p g n", g=GP), AX.X,
                                      ALU.add).then_inc(small, 1)
                    dve.wait_ge(small, upto(g, 5, 1))
                    dve.tensor_scalar(cnt1[:], cnt[:], 1.0, 1.0 / CNT_SCALE, ALU.max, ALU.mult).then_inc(small, 1)
                    dve.wait_ge(small, upto(g, 5, 2))
                    dve.reciprocal(rcnt[:], cnt1[:]).then_inc(small, 1)
                    dve.wait_ge(small, upto(g, 5, 3))
                    dve.tensor_copy(rcs[0][:], rcnt[:]).then_inc(small, 1)
                    dve.wait_ge(small, upto(g, 5, 4))
                    dve.tensor_tensor(rcs[1][:], rcnt[:], rcs[0][:], ALU.subtract).then_inc(small, 1)

                def scale_incidence(g, p, s):
                    dve.wait_ge(small, upto(g, 5, 5))
                    if reused(g):
                        dve.wait_ge(gram_ps, upto(g - 2, 1, 1))
                    for j in range(GP):
                        c = slice(j * N, (j + 1) * N)
                        dve.tensor_scalar(incb[p][s][:, c], inc[p][:, c], rcs[s][:, j:j + 1], None,
                                          ALU.mult).then_inc(incb_ok, 1)

                def degrees(g):
                    dve.wait_ge(deg_ps, upto(g, 1, 1))
                    dve.tensor_scalar(dcl[:], b_adj[:, 0:GP], 1e-37, None, ALU.max).then_inc(dchain, 1)
                    dve.tensor_scalar(dpos[:], b_adj[:, 0:GP], 0.0, 1.0 / CNT_SCALE, ALU.is_gt,
                                      ALU.mult).then_inc(dchain, 1)
                    dve.wait_ge(dchain, upto(g, 4, 2))
                    dve.reciprocal(drc[:], dcl[:]).then_inc(dchain, 1)
                    dve.wait_ge(dchain, upto(g, 4, 3))
                    dve.tensor_tensor(dinv[:], drc[:], dpos[:], ALU.mult).then_inc(dchain, 1)
                    dve.wait_ge(dchain, upto(g, 4, 4))
                    if reused(g, 1):
                        dve.wait_ge(dbc_ps, upto(g - 1, 1, 1))
                    dve.tensor_copy(dis[0][:], dinv[:]).then_inc(dinv_ok, 1)
                    dve.wait_ge(dinv_ok, upto(g, 2, 1))
                    dve.tensor_tensor(dis[1][:], dinv[:], dis[0][:], ALU.subtract).then_inc(dinv_ok, 1)

                def hidden_high(g, h):
                    dve.wait_ge(hf_ok, upto(g, HT, h + 1))
                    if reused(g, 1):
                        dve.wait_ge(z_ps, upto(g - 1, GP, GP))
                    dve.tensor_copy(hs[0][:, h, :], hf[:, h, :]).then_inc(h_hi, 1)

                def hidden_low(g, h):
                    dve.wait_ge(h_hi, upto(g, HT, h + 1))
                    dve.tensor_tensor(hs[1][:, h, :], hf[:, h, :], hs[0][:, h, :],
                                      ALU.subtract).then_inc(h_lo, 1)

                def operator(g, p):
                    dve.wait_ge(gram_ps, upto(g, 1, 1))
                    dve.wait_ge(dbc_sb, upto(g, 1, 1))
                    if reused(g, 1):
                        dve.wait_ge(p_hi, upto(g - 1, 1, 1))
                        dve.wait_ge(p_lo, upto(g - 1, 1, 1))
                    dve.tensor_tensor(pf[:], b_gram[:], dbc[:], ALU.mult).then_inc(pf_ok, 1)

                def operator_low(g, p):
                    dve.wait_ge(p_hi, upto(g, 1, 1))
                    dve.wait_ge(pf_ok, upto(g, 1, 1))
                    if reused(g):
                        dve.wait_ge(y_ps, upto(g - 2, 2, 2))
                    dve.tensor_tensor(ps[p][1][:], pf[:], ps[p][0][:], ALU.subtract).then_inc(p_lo, 1)

                def mixed_low(g, p, d):
                    dve.wait_ge(px_hi, upto(g, 2, d + 1))
                    if reused(g):
                        dve.wait_ge(hid_ps, upto(g - 2, HT, HT))
                    dve.tensor_tensor(px[p][1][:, d, :], b_mix[d][:], px[p][0][:, d, :],
                                      ALU.subtract).then_inc(px_lo, 1)

                def layer_out(g, i):
                    dve.wait_ge(y_ps, upto(g, 2, i + 1))
                    if reused(g, 1):
                        dve.wait_ge(L.x_new, upto(g - 1, GP, GP))
                    dve.scalar_tensor_tensor(L.pre[:, 2 * i:2 * i + 2, :].rearrange("p a b -> p (a b)"),
                                             b_mix[i][:], 0.5, K.x[:, bass.ds(g * (GP * D) + i * 2 * D, 2 * D)],
                                             ALU.mult, ALU.add).then_inc(L.pre_ok, 1)

                def hidden_norm(g):
                    dve.wait_ge(zf_ok, upto(g, GP, GP))
                    dve.tensor_tensor(zm2[:], zf[:, :, D], zf[:, :, D], ALU.mult).then_inc(zvar_ok, 1)
                    dve.wait_ge(zvar_ok, upto(g, 3, 1))
                    dve.scalar_tensor_tensor(zvar[:], zf[:, :, D + 1], W_SCALE / H, zm2[:], ALU.mult,
                                             ALU.subtract).then_inc(zvar_ok, 1)
                    dve.wait_ge(zvar_ok, upto(g, 3, 2))
                    if reused(g, 1):
                        dve.wait_ge(zrs_ok, upto(g - 1, 1, 1))
                    dve.tensor_scalar(zvar[:], zvar[:], 0.0, EPS, ALU.max, ALU.add).then_inc(zvar_ok, 1)

                def normalise(g, j):
                    if j == 0:
                        dve.wait_ge(zrs_ok, upto(g, 1, 1))
                    if reused(g, 1):
                        dve.wait_ge(z_hi, upto(g - 1, GP, j + 1))
                        dve.wait_ge(z_lo, upto(g - 1, GP, j + 1))
                    dve.scalar_tensor_tensor(zn[:, j, :], zf[:, j, 0:D], zrs[:, j:j + 1], K.w2beta[:],
                                             ALU.mult, ALU.add).then_inc(zn_ok, 1)

                def step(g, p, has):
                    q = 1 - p
                    if has(0):
                        mixed_low(g, p, 1)
                    if has(-1):
                        hidden_norm(g - 1)
                    if has(1):
                        incidence(g + 1, q)
                        edge_weights(g + 1)
                        counts(g + 1, q)
                    if has(-1):
                        normalise(g - 1, 0)
                        normalise(g - 1, 1)
                        normalise(g - 1, 2)
                        normalise(g - 1, 3)
                    if has(0):
                        hidden_high(g, 0)
                        hidden_low(g, 0)
                    if has(1):
                        scale_incidence(g + 1, q, 0)
                    if has(-2):
                        norm_shift(L, dve, g - 2)
                    if has(0):
                        hidden_high(g, 1)
                        hidden_low(g, 1)
                        hidden_high(g, 2)
                    if has(1):
                        scale_incidence(g + 1, q, 1)
                    if has(0):
                        hidden_low(g, 2)
                    if has(1):
                        degrees(g + 1)
                    if has(0):
                        hidden_high(g, 3)
                        hidden_low(g, 3)
                    if has(-1):
                        layer_out(g - 1, 0)
                        layer_out(g - 1, 1)
                        norm_row(L, dve, g - 1, 0, 2)
                    if has(1):
                        operator(g + 1, q)
                        operator_low(g + 1, q)
                    if has(-1):
                        norm_row(L, dve, g - 1, 1, 2)
                        norm_row(L, dve, g - 1, 2, 2)
                        norm_row(L, dve, g - 1, 3, 2)
                    if has(1):
                        mixed_low(g + 1, q, 0)
                over_groups(dve, step, 1, 2)

            @block.gpsimd
            def _(pool):
                def hidden_power(g):
                    pool.wait_ge(zvar_ok, upto(g, 3, 3))
                    if reused(g, 1):
                        pool.wait_ge(zn_ok, upto(g - 1, GP, GP))
                    pool.tensor_tensor(zrs[:], zvar[:], K.minus_half[:], ALU.pow).then_inc(zrs_ok, 1)

                def z_low(g, j):
                    pool.wait_ge(z_hi, upto(g, GP, j + 1))
                    if reused(g, 1):
                        pool.wait_ge(y_ps, upto(g - 1, 2, 2))
                    pool.tensor_tensor(zs[1][:, j, :], zn[:, j, :], zs[0][:, j, :], ALU.subtract).then_inc(z_lo, 1)

                def sum_squares(g, h):
                    pool.wait_ge(h_sq, upto(g, HT, h + 1))
                    if h > 1:
                        pool.wait_ge(hqs_ok, upto(g, 3, h - 1))
                    elif reused(g, 1):
                        pool.wait_ge(z_ps, upto(g - 1, GP, GP))
                    pool.tensor_tensor((hqs if h == HT - 1 else hqp[:, h - 1, :])[:],
                                       (hq[:, 0, :] if h == 1 else hqp[:, h - 2, :])[:],
                                       hq[:, h, :], ALU.add).then_inc(hqs_ok, 1)

                def x_low0(g, p):
                    pool.wait_ge(x_hi, upto(g, 1, 1))
                    if reused(g):
                        pool.wait_ge(px_ps, upto(g - 2, 2, 2))
                    pool.tensor_tensor(xs[p][1][:], K.x[:, xcols(g)].rearrange("p (g d) -> p g d", g=GP),
                                       xs[p][0][:], ALU.subtract).then_inc(x_lo, 1)

                def step(g, p, has):
                    q = 1 - p
                    if has(-1):
                        hidden_power(g - 1)
                        z_low(g - 1, 0)
                        z_low(g - 1, 1)
                        z_low(g - 1, 2)
                    if has(0):
                        sum_squares(g, 1)
                    if has(-1):
                        z_low(g - 1, 3)
                    if has(0):
                        sum_squares(g, 2)
                    if has(1):
                        x_low0(g + 1, q)
                    if has(0):
                        sum_squares(g, 3)
                    if has(-1):
                        norm_power(K, L, pool, g - 1, K.eps_quarter)
                over_groups(pool, step, 1, 1)


def norm(nc, ctx, tag):
    L = Parts()
    L.pre, L.st = (ctx.enter_context(nc.sbuf_tensor(f"{tag}_{name}", [128, GP, cols], F32))
                   for name, cols in (("pre", D), ("st", 6)))
    L.msum, L.mdiff, L.m2, L.dd, L.ddn, L.var, L.varn, L.veps, L.rstd, L.nmr = (
        ctx.enter_context(nc.sbuf_tensor(f"{tag}_{name}", [128, GP], F32))
        for name in ("msum", "mdiff", "m2", "dd", "ddn", "var", "varn", "veps", "rstd", "nmr"))
    L.pre_ok, L.st_ok, L.agg, L.rstd_ok, L.nmr_ok, L.x_new = (
        ctx.enter_context(nc.semaphore(f"{tag}_{name}"))
        for name in ("pre_ok", "st_ok", "agg", "rstd_ok", "nmr_ok", "x_new"))
    return L


def norm_row(L, dve, g, j, per=GP):
    if j % (GP // per) == 0:
        dve.wait_ge(L.pre_ok, upto(g, per, j // (GP // per) + 1))
    if j == 0 and reused(g, 1):
        dve.wait_ge(L.agg, upto(g - 1, 8, 8))
    dve.bn_stats(L.st[:, j, :], L.pre[:, j, :]).then_inc(L.st_ok, 1)


def norm_power(K, L, pool, g, eps):
    pool.wait_ge(L.st_ok, upto(g, GP, GP))
    if reused(g, 1):
        pool.wait_ge(L.nmr_ok, upto(g - 1, 1, 1))
    pool.tensor_tensor(L.msum[:], L.st[:, :, 1], L.st[:, :, 4], ALU.add).then_inc(L.agg, 1)
    pool.tensor_tensor(L.mdiff[:], L.st[:, :, 1], L.st[:, :, 4], ALU.subtract).then_inc(L.agg, 1)
    pool.tensor_tensor(L.m2[:], L.st[:, :, 2], L.st[:, :, 5], ALU.add).then_inc(L.agg, 1)
    pool.wait_ge(L.agg, upto(g, 8, 2))
    pool.tensor_tensor(L.dd[:], L.mdiff[:], L.mdiff[:], ALU.mult).then_inc(L.agg, 1)
    pool.wait_ge(L.agg, upto(g, 8, 4))
    pool.tensor_tensor(L.ddn[:], L.dd[:], K.quarter[:], ALU.mult).then_inc(L.agg, 1)
    pool.tensor_tensor(L.var[:], L.m2[:], K.inv_d[:], ALU.mult).then_inc(L.agg, 1)
    pool.wait_ge(L.agg, upto(g, 8, 6))
    pool.tensor_tensor(L.varn[:], L.var[:], L.ddn[:], ALU.add).then_inc(L.agg, 1)
    pool.wait_ge(L.agg, upto(g, 8, 7))
    pool.tensor_tensor(L.veps[:], L.varn[:], eps[:], ALU.add).then_inc(L.agg, 1)
    pool.wait_ge(L.agg, upto(g, 8, 8))
    if reused(g, 1):
        pool.wait_ge(L.x_new, upto(g - 1, GP, GP))
    pool.tensor_tensor(L.rstd[:], L.veps[:], K.minus_half[:], ALU.pow).then_inc(L.rstd_ok, 1)


def norm_shift(L, dve, g):
    dve.wait_ge(L.rstd_ok, upto(g, 1, 1))
    if reused(g, 1):
        dve.wait_ge(L.x_new, upto(g - 1, GP, GP))
    dve.scalar_tensor_tensor(L.nmr[:], L.msum[:], -0.5, L.rstd[:], ALU.mult, ALU.mult).then_inc(L.nmr_ok, 1)


def norm_apply(K, L, act, g, j):
    if j == 0:
        act.wait_ge(L.nmr_ok, upto(g, 1, 1))
    act.activation(K.x[:, gcols(g, j)], L.pre[:, j, :], ACT.Identity,
                   bias=L.nmr[:, j:j + 1], scale=L.rstd[:, j:j + 1]).then_inc(L.x_new, 1)


def front(nc, K, ctx, tag):
    F = Parts()
    F.x_hi, F.x_lo, F.xT_ps, F.xT_sb = (ctx.enter_context(nc.semaphore(f"{tag}_{name}"))
                                        for name in ("x_hi", "x_lo", "xT_ps", "xT_sb"))
    F.xs = [[ctx.enter_context(nc.sbuf_tensor(f"{tag}_x{p}_{s}", [128, GP, D], F16)) for s in ("hi", "lo")]
            for p in range(2)]
    F.xT = [[ctx.enter_context(nc.sbuf_tensor(f"{tag}_xT{p}_{s}", [128, DT, C], F16)) for s in ("hi", "lo")]
            for p in range(2)]
    return F


def x_high(K, F, act, g, p):
    if reused(g):
        act.wait_ge(F.xT_ps, upto(g - 2, 2, 2))
    act.activation(F.xs[p][0][:], K.x[:, xcols(g)].rearrange("p (g d) -> p g d", g=GP),
                   ACT.Copy).then_inc(F.x_hi, 1)


def x_low(K, F, pool, g, p):
    pool.wait_ge(F.x_hi, upto(g, 1, 1))
    if reused(g):
        pool.wait_ge(F.xT_ps, upto(g - 2, 2, 2))
    pool.tensor_tensor(F.xs[p][1][:], K.x[:, xcols(g)].rearrange("p (g d) -> p g d", g=GP),
                       F.xs[p][0][:], ALU.subtract).then_inc(F.x_lo, 1)


def transpose_x(K, F, pe, g, p, banks, s):
    pe.wait_ge((F.x_hi, F.x_lo)[s], upto(g, 1, 1))
    if reused(g, 1):
        pe.wait_ge(F.xT_sb, upto(g - 1, 2, s + 1))
    o = banks[s][:].bitcast(F16)
    for d in range(DT):
        for j in range(GP):
            m = pe.transpose(o[:, d * C + j * N:d * C + (j + 1) * N],
                             F.xs[p][s][:, j, d * 128:(d + 1) * 128], K.ident16[:])
    m.then_inc(F.xT_ps, 1)


def copy_xT(K, F, dve, g, p, banks, s, readers):
    dve.wait_ge(F.xT_ps, upto(g, 2, s + 1))
    if reused(g):
        dve.wait_ge(readers[0], upto(g - 2, readers[1], readers[1]))
    dve.tensor_copy(F.xT[p][s][:].rearrange("p d c -> p (d c)"), banks[s][:].bitcast(F16)).then_inc(F.xT_sb, 1)


def layer1(nc, K):
    ctx = ExitStack()
    with ctx:
        def sb(name, shape, dt=F32):
            return ctx.enter_context(nc.sbuf_tensor(f"l1_{name}", shape, dt))

        def sem(name):
            return ctx.enter_context(nc.semaphore(f"l1_{name}"))

        bank = K.bank
        b_xT, b_qkv, b_ak, b_sm = bank[0:2], bank[2:6], bank[6], bank[7]
        F, L = front(nc, K, ctx, "l1"), norm(nc, ctx, "l1")
        qkv = [sb(f"qkv{p}", [128, GP, 2 * QK + D]) for p in range(2)]
        ks = [sb("k_hi", [128, GP, QK + 1], F16), sb("k_lo", [128, GP, QK + 1], F16)]
        ats = [[sb(f"adjT{p}_{s}", [128, C], F16) for s in ("hi", "lo")] for p in range(2)]
        qa, w = sb("qa", [128, GP, QK]), sb("w", [128, GP])
        wmax, wneg, wexp, wsum = sb("wmax", [GP, 1]), sb("wneg", [GP, 1]), sb("wexp", [GP, N]), sb("wsum", [GP, 1])
        wsc, wrec, wn, wgt = sb("wsc", [GP, 1]), sb("wrec", [GP, 1]), sb("wn", [GP, N]), sb("wgt", [128, GP])
        qkv_ps, qkv_sb, k_hi, k_lo, a_hi, a_lo, k_one, ak_ps = map(
            sem, ("qkv_ps", "qkv_sb", "k_hi", "k_lo", "a_hi", "a_lo", "k_one", "ak_ps"))
        qa_ok, w_ok, asum_ok, wT_ps, wmax_ok, wneg_ok, wexp_ok, wrec_ok, wn_ok, wB_ps, wgt_ok = map(
            sem, ("qa_ok", "w_ok", "asum_ok", "wT_ps", "wmax_ok", "wneg_ok", "wexp_ok", "wrec_ok", "wn_ok",
                  "wB_ps", "wgt_ok"))
        SC = 1.0 / (W_SCALE * W_SCALE * QK ** 0.5)

        with nc.Block() as block:
            @block.sync
            def _(sp):
                for g in range(2):
                    load_adj(K, sp, g, g)

            @block.tensor
            def _(pe):
                def project(g, p, j):
                    if j == 0:
                        pe.wait_ge(F.xT_sb, upto(g, 2, 2))
                    if reused(g, 1):
                        pe.wait_ge(qkv_sb, upto(g - 1, GP, j + 1))
                    c = slice(j * N, (j + 1) * N)
                    for d in range(DT):
                        m = triple(nc, b_qkv[j][:, 0:2 * QK + D], [s[:, d, c] for s in F.xT[p]],
                                   [w[:, d, :] for w in K.qkv], start=d == 0, stop=d == DT - 1)
                    m.then_inc(qkv_ps, 1)

                def aggregate(g, p):
                    for s in (k_hi, k_lo, a_hi, a_lo):
                        pe.wait_ge(s, upto(g, 1, 1))
                    if isinstance(g, int) and g == 0:
                        pe.wait_ge(k_one, 2)
                    if reused(g, 1):
                        pe.wait_ge(asum_ok, upto(g - 1, 1, 1))
                        pe.wait_ge(qa_ok, upto(g - 1, 1, 1))
                    for j in range(GP):
                        m = triple(nc, b_ak[:, j * (QK + 1):(j + 1) * (QK + 1)],
                                   [s[:, j * N:(j + 1) * N] for s in ats[p]], [s[:, j, :] for s in ks])
                    m.then_inc(ak_ps, 1)

                def score_rows(g):
                    pe.wait_ge(w_ok, upto(g, 1, 1))
                    if reused(g, 1):
                        pe.wait_ge(wgt_ok, upto(g - 1, 1, 1))
                    pe.transpose(b_sm[0:GP, 0:N], w[:], K.ident[:]).then_inc(wT_ps, 1)

                def weight_columns(g):
                    pe.wait_ge(wn_ok, upto(g, 1, 1))
                    pe.matmul(b_sm[:, N:N + GP], wn[:], K.ident[0:GP, 0:GP], start=True,
                              stop=True).then_inc(wB_ps, 1)

                def step(g, p, has):
                    if has(-2):
                        weight_columns(g - 2)
                    if has(0):
                        project(g, p, 0)
                        project(g, p, 1)
                        project(g, p, 2)
                    if has(-1):
                        score_rows(g - 1)
                    if has(0):
                        project(g, p, 3)
                    if has(2):
                        transpose_x(K, F, pe, g + 2, p, b_xT, 0)
                        transpose_x(K, F, pe, g + 2, p, b_xT, 1)
                    if has(0):
                        aggregate(g, p)
                over_groups(pe, step, 2, 2)

            @block.scalar
            def _(act):
                def adj_high(g, p):
                    if reused(g):
                        act.wait_ge(ak_ps, upto(g - 2, 1, 1))
                    act.activation(ats[p][0][:], K.at[:, acols(g)], ACT.Copy).then_inc(a_hi, 1)

                def copy_qkv(g, p, j):
                    act.wait_ge(qkv_ps, upto(g, GP, j + 1))
                    if reused(g):
                        act.wait_ge(L.pre_ok, upto(g - 2, GP, j + 1))
                    act.activation(qkv[p][:, j, :], b_qkv[j][:, 0:2 * QK + D], ACT.Copy).then_inc(qkv_sb, 1)

                def key_high(g, p):
                    act.wait_ge(qkv_sb, upto(g, GP, GP))
                    if reused(g, 1):
                        act.wait_ge(ak_ps, upto(g - 1, 1, 1))
                    act.activation(ks[0][:, :, 0:QK], qkv[p][:, :, QK:2 * QK], ACT.Copy).then_inc(k_hi, 1)

                def exponentials(g):
                    act.wait_ge(wneg_ok, upto(g, 1, 1))
                    if reused(g, 1):
                        act.wait_ge(wn_ok, upto(g - 1, 1, 1))
                    act.activation(wexp[:], b_sm[0:GP, 0:N], ACT.Exp, bias=wneg[:], scale=SC,
                                   accum_out=wsum[:]).then_inc(wexp_ok, 1)

                def step(g, p, has):
                    q = 1 - p
                    if has(2):
                        x_high(K, F, act, g + 2, p)
                    if has(0):
                        copy_qkv(g, p, 1)
                        copy_qkv(g, p, 2)
                        copy_qkv(g, p, 3)
                        key_high(g, p)
                    if has(-1):
                        exponentials(g - 1)
                    if has(-2):
                        norm_apply(K, L, act, g - 2, 0)
                        norm_apply(K, L, act, g - 2, 1)
                        norm_apply(K, L, act, g - 2, 2)
                        norm_apply(K, L, act, g - 2, 3)
                    if has(2):
                        adj_high(g + 2, p)
                    if has(1):
                        copy_qkv(g + 1, q, 0)
                over_groups(act, step, 2, 2)

            @block.vector
            def _(dve):
                def weights(g):
                    dve.wait_ge(wB_ps, upto(g, 1, 1))
                    if reused(g, 1):
                        dve.wait_ge(L.pre_ok, upto(g - 1, GP, GP))
                    dve.tensor_copy(wgt[:], b_sm[:, N:N + GP]).then_inc(wgt_ok, 1)

                def residual(g, p, j):
                    if j == 0:
                        dve.wait_ge(wgt_ok, upto(g, 1, 1))
                        if reused(g, 1):
                            dve.wait_ge(L.x_new, upto(g - 1, GP, GP))
                    dve.scalar_tensor_tensor(L.pre[:, j, :], qkv[p][:, j, 2 * QK:], wgt[:, j:j + 1],
                                             K.x[:, gcols(g, j)], ALU.mult, ALU.add).then_inc(L.pre_ok, 1)

                def scores(g, p):
                    dve.wait_ge(ak_ps, upto(g, 1, 1))
                    ak = b_ak[:, 0:GP * (QK + 1)].rearrange("p (g k) -> p g k", g=GP)
                    if reused(g, 1):
                        dve.wait_ge(w_ok, upto(g - 1, 1, 1))
                    dve.tensor_tensor(qa[:], ak[:, :, 0:QK], qkv[p][:, :, 0:QK], ALU.mult).then_inc(qa_ok, 1)
                    dve.tensor_scalar(K.asum[:, bass.ds(g * GP, GP)], ak[:, :, QK], 1.0, None,
                                      ALU.mult).then_inc(asum_ok, 1)
                    dve.wait_ge(qa_ok, upto(g, 1, 1))
                    if reused(g, 1):
                        dve.wait_ge(wT_ps, upto(g - 1, 1, 1))
                    dve.tensor_reduce(w[:], qa[:], AX.X, ALU.add).then_inc(w_ok, 1)

                def maximum(g):
                    dve.wait_ge(wT_ps, upto(g, 1, 1))
                    dve.tensor_reduce(wmax[:], b_sm[0:GP, 0:N], AX.X, ALU.max).then_inc(wmax_ok, 1)
                    dve.wait_ge(wmax_ok, upto(g, 1, 1))
                    if reused(g, 1):
                        dve.wait_ge(wexp_ok, upto(g - 1, 1, 1))
                    dve.tensor_scalar(wneg[:], wmax[:], -SC, None, ALU.mult).then_inc(wneg_ok, 1)

                def softmax(g):
                    dve.wait_ge(wexp_ok, upto(g, 1, 1))
                    dve.tensor_scalar(wsc[:], wsum[:], W_SCALE, None, ALU.mult).then_inc(wrec_ok, 1)
                    dve.wait_ge(wrec_ok, upto(g, 2, 1))
                    dve.reciprocal(wrec[:], wsc[:]).then_inc(wrec_ok, 1)
                    dve.wait_ge(wrec_ok, upto(g, 2, 2))
                    if reused(g, 1):
                        dve.wait_ge(wB_ps, upto(g - 1, 1, 1))
                    dve.tensor_scalar(wn[:], wexp[:], wrec[:], None, ALU.mult).then_inc(wn_ok, 1)

                dve.memset(ks[0][:, :, QK:QK + 1], 1.0).then_inc(k_one, 1)
                dve.memset(ks[1][:, :, QK:QK + 1], 0.0).then_inc(k_one, 1)

                def step(g, p, has):
                    q = 1 - p
                    if has(-1):
                        maximum(g - 1)
                    if has(-2):
                        norm_row(L, dve, g - 2, 1)
                        norm_row(L, dve, g - 2, 2)
                    if has(-1):
                        softmax(g - 1)
                    if has(-2):
                        norm_row(L, dve, g - 2, 3)
                    if has(2):
                        copy_xT(K, F, dve, g + 2, p, b_xT, 0, (qkv_ps, GP))
                    if has(-2):
                        norm_shift(L, dve, g - 2)
                    if has(-1):
                        weights(g - 1)
                    if has(0):
                        scores(g, p)
                    if has(-1):
                        residual(g - 1, q, 0)
                    if has(2):
                        copy_xT(K, F, dve, g + 2, p, b_xT, 1, (qkv_ps, GP))
                    if has(-1):
                        residual(g - 1, q, 1)
                        residual(g - 1, q, 2)
                        residual(g - 1, q, 3)
                        norm_row(L, dve, g - 1, 0)
                over_groups(dve, step, 2, 2)

            @block.gpsimd
            def _(pool):
                def adj_low(g, p):
                    pool.wait_ge(a_hi, upto(g, 1, 1))
                    if reused(g):
                        pool.wait_ge(ak_ps, upto(g - 2, 1, 1))
                    pool.tensor_tensor(ats[p][1][:], K.at[:, acols(g)], ats[p][0][:], ALU.subtract).then_inc(a_lo, 1)

                def key_low(g, p):
                    pool.wait_ge(k_hi, upto(g, 1, 1))
                    if reused(g, 1):
                        pool.wait_ge(ak_ps, upto(g - 1, 1, 1))
                    pool.tensor_tensor(ks[1][:, :, 0:QK], qkv[p][:, :, QK:2 * QK], ks[0][:, :, 0:QK],
                                       ALU.subtract).then_inc(k_lo, 1)

                def step(g, p, has):
                    if has(0):
                        adj_low(g, p)
                    if has(2):
                        x_low(K, F, pool, g + 2, p)
                    if has(0):
                        key_low(g, p)
                    if has(-2):
                        norm_power(K, L, pool, g - 2, K.eps)
                over_groups(pool, step, 2, 2)


def attention_front(nc, K, ctx, tag, width):
    S = Parts()
    S.s_ps, S.s_hi, S.s_lo, S.s_bias, S.sj_ps, S.t_ok, S.e_ok, S.u_ok = (
        ctx.enter_context(nc.semaphore(f"{tag}_{name}"))
        for name in ("s_ps", "s_hi", "s_lo", "s_bias", "sj_ps", "t_ok", "e_ok", "u_ok"))
    S.s = [ctx.enter_context(nc.sbuf_tensor(f"{tag}_s_{s}", [128, GP], F16)) for s in ("hi", "lo")]
    S.bias = ctx.enter_context(nc.sbuf_tensor(f"{tag}_bias", [128, GP], F32))
    S.t = ctx.enter_context(nc.sbuf_tensor(f"{tag}_t", [128, C], F32))
    S.lr = ctx.enter_context(nc.sbuf_tensor(f"{tag}_lr", [128, C], F32))
    S.e = ctx.enter_context(nc.sbuf_tensor(f"{tag}_e", [128, C], F32))
    S.u = ctx.enter_context(nc.sbuf_tensor(f"{tag}_u", [128, C], F32))
    S.width = width
    return S


def node_scores(nc, K, F, S, pe, g, p, b, weights, column):
    pe.wait_ge(F.xT_sb, upto(g, 2, 2))
    if reused(g, 1):
        pe.wait_ge(S.s_lo, upto(g - 1, 1, 1))
        pe.wait_ge(S.s_bias, upto(g - 1, 1, 1))
    for j in range(GP):
        for d in range(DT):
            m = triple(nc, b[:, j * S.width:(j + 1) * S.width], [s[:, d, j * N:(j + 1) * N] for s in F.xT[p]],
                       [w[:, d, column:column + S.width] for w in weights], start=d == 0, stop=d == DT - 1)
    m.then_inc(S.s_ps, 1)


def split_scores(S, dve, g, b):
    dve.wait_ge(S.s_ps, upto(g, 1, 1))
    if reused(g, 1):
        dve.wait_ge(S.sj_ps, upto(g - 1, 1, 1))
    sj = b[:, 0:GP * S.width].rearrange("p (g s) -> p g s", g=GP)[:, :, 0]
    dve.tensor_copy(S.s[0][:], sj).then_inc(S.s_hi, 1)
    dve.wait_ge(S.s_hi, upto(g, 1, 1))
    dve.tensor_tensor(S.s[1][:], sj, S.s[0][:], ALU.subtract).then_inc(S.s_lo, 1)


def spread_scores(nc, K, S, pe, g, b, free, per):
    pe.wait_ge(S.s_lo, upto(g, 1, 1))
    if reused(g, 1):
        pe.wait_ge(free, upto(g - 1, per, per))
    for j in range(GP):
        for s in (1, 0):
            m = pe.matmul(b[:, j * N:(j + 1) * N], S.s[s][:, j:j + 1].to_broadcast([128, 128]),
                          K.ident16[:], start=s == 1, stop=s == 0)
    m.then_inc(S.sj_ps, 1)


def layer2(nc, K):
    ctx = ExitStack()
    with ctx:
        def sb(name, shape, dt=F32):
            return ctx.enter_context(nc.sbuf_tensor(f"l2_{name}", shape, dt))

        def sem(name):
            return ctx.enter_context(nc.semaphore(f"l2_{name}"))

        bank = K.bank
        b_xT, b_far, b_near, b_s, b_t = bank[0:2], bank[2], bank[3:6], bank[6], bank[7]
        F, L, S = front(nc, K, ctx, "l2"), norm(nc, ctx, "l2"), attention_front(nc, K, ctx, "l2", 2)
        adjn, adj_in = K.adjn, K.adj_in
        before_l2 = 8 * G
        rsum, reps, rinv = sb("rsum", [128, GP]), sb("reps", [128, GP]), sb("rinv", [128, GP])
        tf = sb("tf", [128, C])
        ts = [sb("T_hi", [128, C], F16), sb("T_lo", [128, C], F16)]
        tT = [sb(f"TT{p}", [128, 2, C], F16) for p in range(2)]
        far = [[sb(f"far{j}_{s}", [128, D], F16) for s in ("hi", "lo")] for j in range(GP)]
        mid = [[sb(f"mid{j}_{s}", [128, D], F16) for s in ("hi", "lo")] for j in range(GP)]
        hr = sb("hr", [128, GP, D])
        rsum_ok, reps_ok, rinv_ok, tf_ok, t_hi, t_lo, tT_ps, tT_sb = map(
            sem, ("rsum_ok", "reps_ok", "rinv_ok", "tf_ok", "t_hi", "t_lo", "tT_ps", "tT_sb"))
        far_ps, far_hi, far_lo, near_ps, mid_ps, mid_hi, mid_lo, out_ps, hr_ok = map(
            sem, ("far_ps", "far_hi", "far_lo", "near_ps", "mid_ps", "mid_hi", "mid_lo", "out_ps", "hr_ok"))
        lr_ok = sem("lr_ok")
        before = (0, -2, -1, 1)

        with nc.Block() as block:
            @block.sync
            def _(sp):
                def load(g, p, has):
                    if has(0) and reused(g):
                        sp.wait_ge(S.u_ok, upto(g - 2, 1, 1))
                        load_adj(K, sp, g, p)
                over_groups(sp, load, 0, 0)

            @block.tensor
            def _(pe):
                def project_far(g, p, j):
                    if j == 0:
                        pe.wait_ge(F.xT_sb, upto(g, 2, 2))
                    if j >= 1 or reused(g, 1):
                        pe.wait_ge(far_lo, upto(g, GP, j))
                    c = slice(j * N, (j + 1) * N)
                    for d in range(DT):
                        m = triple(nc, b_far[:, 0:D], [s[:, d, c] for s in F.xT[p]],
                                   [w[:, d, 0:D] for w in K.wk], start=d == 0, stop=d == DT - 1)
                    m.then_inc(far_ps, 1)

                def project_near(g, p, j, n):
                    if j == 0:
                        pe.wait_ge(F.xT_sb, upto(g, 2, 2))
                    c = slice(j * N, (j + 1) * N)
                    if j == 3 or reused(g, 1):
                        pe.wait_ge(hr_ok, upto(g, GP, before[j]))
                    for d in range(DT):
                        m = triple(nc, b_near[n][:], [s[:, d, c] for s in F.xT[p]],
                                   [w[:, d, D + 2:3 * D + 2] for w in K.wk], start=d == 0, stop=d == DT - 1)
                    m.then_inc(near_ps, 1)

                def walk_far(g, p, j, n):
                    pe.wait_ge(tT_sb, upto(g, 1, 1))
                    pe.wait_ge(far_hi, upto(g, GP, j + 1))
                    pe.wait_ge(far_lo, upto(g, GP, j + 1))
                    triple(nc, b_near[n][:, 0:D], [tT[p][:, s, j * N:(j + 1) * N] for s in range(2)],
                           [s[:] for s in far[j]], start=False, skip_group_check=True).then_inc(mid_ps, 1)

                def walk_mid(g, p, j, n):
                    pe.wait_ge(mid_hi, upto(g, GP, j + 1))
                    pe.wait_ge(mid_lo, upto(g, GP, j + 1))
                    o = b_near[n][:, D:2 * D]
                    pe.matmul(o, K.ones16[:], K.bkrow[:], start=False, stop=False, skip_group_check=True)
                    triple(nc, o, [tT[p][:, s, j * N:(j + 1) * N] for s in range(2)], [s[:] for s in mid[j]],
                           start=False, skip_group_check=True).then_inc(out_ps, 1)

                def transpose_T(g):
                    pe.wait_ge(t_hi, upto(g, 1, 1))
                    pe.wait_ge(t_lo, upto(g, 1, 1))
                    pe.wait_ge(S.t_ok, upto(g, GP, GP))
                    o = b_t[:].bitcast(F16)
                    for s in range(2):
                        for j in range(GP):
                            m = pe.transpose(o[:, s * C + j * N:s * C + (j + 1) * N],
                                             ts[s][:, j * N:(j + 1) * N], K.ident16[:])
                    m.then_inc(tT_ps, 1)

                def step(g, p, has):
                    q = 1 - p
                    if has(-1):
                        walk_mid(g - 1, q, 2, 2)
                        walk_far(g - 1, q, 3, 0)
                    if has(0):
                        transpose_T(g)
                    if has(-1):
                        walk_mid(g - 1, q, 3, 0)
                    if has(1):
                        transpose_x(K, F, pe, g + 1, q, b_xT, 0)
                        transpose_x(K, F, pe, g + 1, q, b_xT, 1)
                    if has(0):
                        project_far(g, p, 0)
                        project_near(g, p, 0, 0)
                    if has(1):
                        node_scores(nc, K, F, S, pe, g + 1, q, b_s, K.wk, D)
                    if has(0):
                        project_far(g, p, 1)
                    if has(1):
                        spread_scores(nc, K, S, pe, g + 1, b_t, tT_sb, 1)
                    if has(0):
                        walk_far(g, p, 0, 0)
                        project_near(g, p, 1, 1)
                        project_far(g, p, 2)
                        project_near(g, p, 2, 2)
                        walk_far(g, p, 1, 1)
                        walk_far(g, p, 2, 2)
                        walk_mid(g, p, 0, 0)
                        walk_mid(g, p, 1, 1)
                        project_far(g, p, 3)
                        project_near(g, p, 3, 0)
                over_groups(pe, step, 1, 1)

            @block.scalar
            def _(act):
                def logits(g, j):
                    if j == 0:
                        act.wait_ge(S.sj_ps, upto(g, 1, 1))
                        act.wait_ge(S.s_bias, upto(g, 1, 1))
                        if reused(g, 1):
                            act.wait_ge(lr_ok, upto(g - 1, 1, 1))
                    act.activation(S.t[:, j * N:(j + 1) * N], b_t[:, j * N:(j + 1) * N], ACT.Identity,
                                   bias=S.bias[:, j:j + 1], scale=1.0 / WK_SCALE).then_inc(S.t_ok, 1)

                def far_high(g, j):
                    act.wait_ge(far_ps, upto(g, GP, j + 1))
                    if reused(g, 1):
                        act.wait_ge(mid_ps, upto(g - 1, GP, j + 1))
                    act.activation(far[j][0][:], b_far[:, 0:D], ACT.Copy).then_inc(far_hi, 1)

                def mid_high(g, j, n):
                    act.wait_ge(mid_ps, upto(g, GP, j + 1))
                    if reused(g, 1):
                        act.wait_ge(out_ps, upto(g - 1, GP, j + 1))
                    act.activation(mid[j][0][:], b_near[n][:, 0:D], ACT.Copy).then_inc(mid_hi, 1)

                def relu(g, j, n):
                    act.wait_ge(out_ps, upto(g, GP, j + 1))
                    if reused(g, 1):
                        act.wait_ge(L.pre_ok, upto(g - 1, GP, j + 1))
                    act.activation(hr[:, j, :], b_near[n][:, D:2 * D], ACT.Relu,
                                   scale=1.0 / WK_SCALE).then_inc(hr_ok, 1)

                def exponentials(g):
                    act.wait_ge(lr_ok, upto(g, 1, 1))
                    if reused(g, 1):
                        act.wait_ge(S.u_ok, upto(g - 1, 1, 1))
                    act.activation(S.e[:], S.lr[:], ACT.Exp).then_inc(S.e_ok, 1)

                def transition_high(g):
                    act.wait_ge(tf_ok, upto(g, 1, 1))
                    if reused(g, 1):
                        act.wait_ge(tT_ps, upto(g - 1, 1, 1))
                    act.activation(ts[0][:], tf[:], ACT.Copy).then_inc(t_hi, 1)

                def step(g, p, has):
                    if has(0):
                        transition_high(g)
                    if has(-2):
                        norm_apply(K, L, act, g - 2, 3)
                    if has(-1):
                        relu(g - 1, 2, 2)
                        mid_high(g - 1, 3, 0)
                    if has(2):
                        x_high(K, F, act, g + 2, p)
                    if has(-1):
                        relu(g - 1, 3, 0)
                    if has(0):
                        far_high(g, 0)
                    if has(1):
                        logits(g + 1, 0)
                    if has(0):
                        far_high(g, 1)
                    if has(1):
                        logits(g + 1, 1)
                        logits(g + 1, 2)
                        logits(g + 1, 3)
                    if has(0):
                        mid_high(g, 0, 0)
                        far_high(g, 2)
                    if has(1):
                        exponentials(g + 1)
                    if has(0):
                        mid_high(g, 1, 1)
                    if has(-1):
                        norm_apply(K, L, act, g - 1, 0)
                    if has(0):
                        mid_high(g, 2, 2)
                    if has(-1):
                        norm_apply(K, L, act, g - 1, 1)
                    if has(0):
                        relu(g, 0, 0)
                        relu(g, 1, 1)
                    if has(-1):
                        norm_apply(K, L, act, g - 1, 2)
                    if has(0):
                        far_high(g, 3)
                over_groups(act, step, 2, 2)

            @block.vector
            def _(dve):
                def far_low(g, j):
                    dve.wait_ge(far_hi, upto(g, GP, j + 1))
                    if reused(g, 1):
                        dve.wait_ge(mid_ps, upto(g - 1, GP, j + 1))
                    dve.tensor_tensor(far[j][1][:], b_far[:, 0:D], far[j][0][:], ALU.subtract).then_inc(far_lo, 1)

                def mid_low(g, j, n):
                    dve.wait_ge(mid_hi, upto(g, GP, j + 1))
                    if reused(g, 1):
                        dve.wait_ge(out_ps, upto(g - 1, GP, j + 1))
                    dve.tensor_tensor(mid[j][1][:], b_near[n][:, 0:D], mid[j][0][:],
                                      ALU.subtract).then_inc(mid_lo, 1)

                def residual(g, j):
                    dve.wait_ge(hr_ok, upto(g, GP, j + 1))
                    if reused(g, 1):
                        dve.wait_ge(L.x_new, upto(g - 1, GP, GP))
                    dve.tensor_tensor(L.pre[:, j, :], hr[:, j, :], K.x[:, gcols(g, j)],
                                      ALU.add).then_inc(L.pre_ok, 1)

                def scores(g):
                    split_scores(S, dve, g, b_s)
                    if reused(g, 1):
                        dve.wait_ge(S.t_ok, upto(g - 1, GP, GP))
                    si = b_s[:, 0:2 * GP].rearrange("p (g s) -> p g s", g=GP)[:, :, 1]
                    dve.tensor_scalar(S.bias[:], si, 1.0 / WK_SCALE, K.edge_bias[:], ALU.mult,
                                      ALU.add).then_inc(S.s_bias, 1)

                def leaky(g):
                    dve.wait_ge(S.t_ok, upto(g, GP, GP))
                    if reused(g, 1):
                        dve.wait_ge(S.e_ok, upto(g - 1, 1, 1))
                    dve.scalar_tensor_tensor(S.lr[:], S.t[:], 0.2, S.t[:], ALU.mult, ALU.max).then_inc(lr_ok, 1)

                def transition(g, p):
                    dve.wait_ge(S.e_ok, upto(g, 1, 1))
                    dve.wait_ge(adj_in[p], before_l2 + 8 * (g - p) + 16)
                    if reused(g, 1):
                        dve.wait_ge(tf_ok, upto(g - 1, 1, 1))
                    dve.tensor_tensor(S.u[:], S.e[:], adjn[p][:].rearrange("p g n -> p (g n)"),
                                      ALU.mult).then_inc(S.u_ok, 1)

                def row_sums(g):
                    dve.wait_ge(S.u_ok, upto(g, 1, 1))
                    u = S.u[:].rearrange("p (g n) -> p g n", g=GP)
                    dve.tensor_reduce(rsum[:], u, AX.X, ALU.add).then_inc(rsum_ok, 1)
                    dve.wait_ge(rsum_ok, upto(g, 1, 1))
                    dve.tensor_scalar(reps[:], rsum[:], 1e-12, None, ALU.add).then_inc(reps_ok, 1)
                    dve.wait_ge(reps_ok, upto(g, 1, 1))
                    dve.reciprocal(rinv[:], reps[:]).then_inc(rinv_ok, 1)

                def normalised(g):
                    u = S.u[:].rearrange("p (g n) -> p g n", g=GP)
                    dve.wait_ge(rinv_ok, upto(g, 1, 1))
                    if reused(g, 1):
                        dve.wait_ge(t_hi, upto(g - 1, 1, 1))
                        dve.wait_ge(t_lo, upto(g - 1, 1, 1))
                    dve.tensor_tensor(tf[:].rearrange("p (g n) -> p g n", g=GP), u,
                                      rinv[:, :, None].to_broadcast([128, GP, N]), ALU.mult).then_inc(tf_ok, 1)

                def copy_tT(g, p):
                    dve.wait_ge(tT_ps, upto(g, 1, 1))
                    if reused(g):
                        dve.wait_ge(out_ps, upto(g - 2, GP, GP))
                    dve.tensor_copy(tT[p][:].rearrange("p s c -> p (s c)"), b_t[:].bitcast(F16)).then_inc(tT_sb, 1)

                def step(g, p, has):
                    q = 1 - p
                    if has(-1):
                        norm_row(L, dve, g - 1, 1)
                    if has(1):
                        scores(g + 1)
                    if has(-1):
                        residual(g - 1, 3)
                        norm_row(L, dve, g - 1, 2)
                        norm_row(L, dve, g - 1, 3)
                    if has(0):
                        far_low(g, 1)
                    if has(1):
                        leaky(g + 1)
                    if has(0):
                        mid_low(g, 0, 0)
                        far_low(g, 2)
                    if has(-1):
                        norm_shift(L, dve, g - 1)
                    if has(1):
                        transition(g + 1, q)
                    if has(0):
                        mid_low(g, 1, 1)
                    if has(1):
                        row_sums(g + 1)
                        normalised(g + 1)
                    if has(0):
                        mid_low(g, 2, 2)
                        far_low(g, 3)
                        residual(g, 0)
                        residual(g, 1)
                        mid_low(g, 3, 0)
                        residual(g, 2)
                    if has(1):
                        copy_tT(g + 1, q)
                    if has(2):
                        copy_xT(K, F, dve, g + 2, p, b_xT, 0, (near_ps, GP))
                        copy_xT(K, F, dve, g + 2, p, b_xT, 1, (near_ps, GP))
                    if has(1):
                        far_low(g + 1, 0)
                    if has(0):
                        norm_row(L, dve, g, 0)
                over_groups(dve, step, 2, 1)

            @block.gpsimd
            def _(pool):
                def transition_low(g):
                    pool.wait_ge(t_hi, upto(g, 1, 1))
                    if reused(g, 1):
                        pool.wait_ge(tT_ps, upto(g - 1, 1, 1))
                    pool.tensor_tensor(ts[1][:], tf[:], ts[0][:], ALU.subtract).then_inc(t_lo, 1)

                def step(g, p, has):
                    if has(-1):
                        norm_power(K, L, pool, g - 1, K.eps)
                    if has(2):
                        x_low(K, F, pool, g + 2, p)
                    if has(1):
                        transition_low(g + 1)
                over_groups(pool, step, 2, 1)


def layer3(nc, K):
    ctx = ExitStack()
    with ctx:
        def sb(name, shape, dt=F32):
            return ctx.enter_context(nc.sbuf_tensor(f"l3_{name}", shape, dt))

        def sem(name):
            return ctx.enter_context(nc.semaphore(f"l3_{name}"))

        bank = K.bank
        b_xT, b_s, b_t, b_xw, b_out = bank[0:2], bank[2], bank[3], bank[4:6], bank[6:8]
        F, L, S = front(nc, K, ctx, "l3"), norm(nc, ctx, "l3"), attention_front(nc, K, ctx, "l3", 1)
        us = [[sb(f"U{p}_{s}", [128, C], F16) for s in ("hi", "lo")] for p in range(2)]
        xw = [sb("xw_hi", [128, GP, D + 1], F16), sb("xw_lo", [128, GP, D + 1], F16)]
        rrec, rfac = sb("rrec", [128, GP]), sb("rfac", [128, GP])
        res = [sb(f"result{p}", [128, GP, D]) for p in range(2)]
        lr_ok, u_hi, u_lo, one_ok, xw_ps, xw_hi, xw_lo, out_ps, rrec_ok, rfac_ok = map(
            sem, ("lr_ok", "u_hi", "u_lo", "one_ok", "xw_ps", "xw_hi", "xw_lo", "out_ps", "rrec_ok", "rfac_ok"))
        stored_p = [sem(f"stored{p}") for p in range(2)]

        with nc.Block() as block:
            @block.sync
            def _(sp):
                def store(g, p, has):
                    if has(0):
                        sp.wait_ge(L.x_new, upto(g, GP, GP))
                        sp.dma_start(K.od[:, bass.ds(g * GP, GP), :], res[p][:]).then_inc(stored_p[p], 16)
                over_groups(sp, store, 0, 0)
                for p in range(2):
                    sp.wait_ge(stored_p[p], 16 * (G // 2))

            @block.tensor
            def _(pe):
                def project(g, p, j):
                    if j >= 2 or reused(g, 1):
                        pe.wait_ge(xw_lo, upto(g, GP, j - 1))
                    c = slice(j * N, (j + 1) * N)
                    for d in range(DT):
                        m = triple(nc, b_xw[j % 2][:, 0:D], [s[:, d, c] for s in F.xT[p]],
                                   [w[:, d, 0:D] for w in K.w3], start=d == 0, stop=d == DT - 1)
                    m.then_inc(xw_ps, 1)

                def aggregate(g, p, j):
                    if j == 0:
                        pe.wait_ge(u_hi, upto(g, 1, 1))
                        pe.wait_ge(u_lo, upto(g, 1, 1))
                        if isinstance(g, int) and g == 0:
                            pe.wait_ge(one_ok, 2)
                    pe.wait_ge(xw_hi, upto(g, GP, j + 1))
                    pe.wait_ge(xw_lo, upto(g, GP, j + 1))
                    if j >= 2 or reused(g, 1):
                        pe.wait_ge(L.pre_ok, upto(g, GP, j - 1))
                    triple(nc, b_out[j % 2][:, 0:D + 1], [s[:, j * N:(j + 1) * N] for s in us[p]],
                           [s[:, j, :] for s in xw]).then_inc(out_ps, 1)

                def step(g, p, has):
                    q = 1 - p
                    if has(0):
                        spread_scores(nc, K, S, pe, g, b_t, S.t_ok, GP)
                    if has(1):
                        transpose_x(K, F, pe, g + 1, q, b_xT, 0)
                    if has(-1):
                        aggregate(g - 1, q, 1)
                        aggregate(g - 1, q, 2)
                    if has(1):
                        transpose_x(K, F, pe, g + 1, q, b_xT, 1)
                    if has(-1):
                        aggregate(g - 1, q, 3)
                    if has(0):
                        project(g, p, 0)
                        project(g, p, 1)
                    if has(1):
                        node_scores(nc, K, F, S, pe, g + 1, q, b_s, K.w3, D)
                    if has(0):
                        project(g, p, 2)
                        project(g, p, 3)
                        aggregate(g, p, 0)
                over_groups(pe, step, 1, 1)

            @block.scalar
            def _(act):
                def xw_high(g, j):
                    act.wait_ge(xw_ps, upto(g, GP, j + 1))
                    if reused(g, 1):
                        act.wait_ge(out_ps, upto(g - 1, GP, j + 1))
                    act.activation(xw[0][:, j, 0:D], b_xw[j % 2][:, 0:D], ACT.Copy).then_inc(xw_hi, 1)

                def result(g, p, j):
                    if j == 0:
                        act.wait_ge(L.nmr_ok, upto(g, 1, 1))
                        if reused(g):
                            act.wait_ge(stored_p[p], 8 * (g - p))
                    act.activation(res[p][:, j, :], L.pre[:, j, :], ACT.Identity,
                                   bias=L.nmr[:, j:j + 1], scale=L.rstd[:, j:j + 1]).then_inc(L.x_new, 1)

                def tanh(g, j):
                    if j == 0:
                        act.wait_ge(S.sj_ps, upto(g, 1, 1))
                        act.wait_ge(S.s_bias, upto(g, 1, 1))
                        if reused(g, 1):
                            act.wait_ge(lr_ok, upto(g - 1, 1, 1))
                    act.activation(S.t[:, j * N:(j + 1) * N], b_t[:, j * N:(j + 1) * N], ACT.Tanh,
                                   bias=S.bias[:, j:j + 1], scale=0.125).then_inc(S.t_ok, 1)

                def exponentials(g):
                    act.wait_ge(lr_ok, upto(g, 1, 1))
                    if reused(g, 1):
                        act.wait_ge(S.u_ok, upto(g - 1, 1, 1))
                    act.activation(S.e[:], S.lr[:], ACT.Exp, scale=8.0).then_inc(S.e_ok, 1)

                def attention_high(g, p):
                    act.wait_ge(S.u_ok, upto(g, 1, 1))
                    if reused(g):
                        act.wait_ge(out_ps, upto(g - 2, GP, GP))
                    act.activation(us[p][0][:], S.u[:], ACT.Copy).then_inc(u_hi, 1)

                def step(g, p, has):
                    if has(-2):
                        result(g - 2, p, 0)
                        result(g - 2, p, 1)
                        result(g - 2, p, 2)
                    if has(0):
                        tanh(g, 0)
                        tanh(g, 1)
                        tanh(g, 2)
                        tanh(g, 3)
                    if has(-2):
                        result(g - 2, p, 3)
                    if has(2):
                        x_high(K, F, act, g + 2, p)
                    if has(0):
                        exponentials(g)
                        attention_high(g, p)
                        xw_high(g, 0)
                        xw_high(g, 1)
                        xw_high(g, 2)
                        xw_high(g, 3)
                over_groups(act, step, 2, 2)

            @block.vector
            def _(dve):
                def xw_low(g, j):
                    dve.wait_ge(xw_hi, upto(g, GP, j + 1))
                    if reused(g, 1):
                        dve.wait_ge(out_ps, upto(g - 1, GP, j + 1))
                    dve.tensor_tensor(xw[1][:, j, 0:D], b_xw[j % 2][:, 0:D], xw[0][:, j, 0:D],
                                      ALU.subtract).then_inc(xw_lo, 1)

                def scores(g):
                    split_scores(S, dve, g, b_s)
                    if reused(g, 1):
                        dve.wait_ge(S.t_ok, upto(g - 1, GP, GP))
                    dve.tensor_scalar(S.bias[:], b_s[:, 0:GP], 0.125, None, ALU.mult).then_inc(S.s_bias, 1)

                def leaky(g):
                    dve.wait_ge(S.t_ok, upto(g, GP, GP))
                    if reused(g, 1):
                        dve.wait_ge(S.e_ok, upto(g - 1, 1, 1))
                    dve.scalar_tensor_tensor(S.lr[:], S.t[:], 0.1, S.t[:], ALU.mult, ALU.max).then_inc(lr_ok, 1)

                def attention(g):
                    dve.wait_ge(S.e_ok, upto(g, 1, 1))
                    if reused(g, 1):
                        dve.wait_ge(u_hi, upto(g - 1, 1, 1))
                        dve.wait_ge(u_lo, upto(g - 1, 1, 1))
                    dve.tensor_tensor(S.u[:], S.e[:], K.at[:, acols(g)], ALU.mult).then_inc(S.u_ok, 1)

                def residual(g, j):
                    dve.wait_ge(out_ps, upto(g, GP, j + 1))
                    b = b_out[j % 2]
                    dve.reciprocal(rrec[:, j:j + 1], b[:, D:D + 1]).then_inc(rrec_ok, 1)
                    dve.wait_ge(rrec_ok, upto(g, GP, j + 1))
                    dve.scalar_tensor_tensor(rfac[:, j:j + 1], rrec[:, j:j + 1], 1.0 / W3_SCALE,
                                             K.asum[:, bass.ds(g * GP + j, 1)], ALU.mult,
                                             ALU.mult).then_inc(rfac_ok, 1)
                    dve.wait_ge(rfac_ok, upto(g, GP, j + 1))
                    if reused(g, 1):
                        dve.wait_ge(L.x_new, upto(g - 1, GP, GP))
                    dve.scalar_tensor_tensor(L.pre[:, j, :], b[:, 0:D], rfac[:, j:j + 1], K.x[:, gcols(g, j)],
                                             ALU.mult, ALU.add).then_inc(L.pre_ok, 1)

                dve.memset(xw[0][:, :, D:D + 1], 1.0).then_inc(one_ok, 1)
                dve.memset(xw[1][:, :, D:D + 1], 0.0).then_inc(one_ok, 1)

                def step(g, p, has):
                    q = 1 - p
                    if has(1):
                        copy_xT(K, F, dve, g + 1, q, b_xT, 1, (xw_ps, GP))
                    if has(-1):
                        norm_row(L, dve, g - 1, 2)
                        norm_row(L, dve, g - 1, 3)
                    if has(0):
                        xw_low(g, 0)
                        xw_low(g, 1)
                    if has(-1):
                        norm_shift(L, dve, g - 1)
                    if has(1):
                        scores(g + 1)
                    if has(0):
                        xw_low(g, 2)
                        xw_low(g, 3)
                    if has(1):
                        leaky(g + 1)
                    if has(0):
                        residual(g, 0)
                        residual(g, 1)
                    if has(2):
                        copy_xT(K, F, dve, g + 2, p, b_xT, 0, (xw_ps, GP))
                    if has(1):
                        attention(g + 1)
                    if has(0):
                        norm_row(L, dve, g, 0)
                        residual(g, 2)
                        norm_row(L, dve, g, 1)
                        residual(g, 3)
                over_groups(dve, step, 2, 1)

            @block.gpsimd
            def _(pool):
                def attention_low(g, p):
                    pool.wait_ge(u_hi, upto(g, 1, 1))
                    if reused(g):
                        pool.wait_ge(out_ps, upto(g - 2, GP, GP))
                    pool.tensor_tensor(us[p][1][:], S.u[:], us[p][0][:], ALU.subtract).then_inc(u_lo, 1)

                def step(g, p, has):
                    if has(0):
                        attention_low(g, p)
                    if has(-1):
                        norm_power(K, L, pool, g - 1, K.eps)
                    if has(2):
                        x_low(K, F, pool, g + 2, p)
                over_groups(pool, step, 2, 1)


_INS = ['x', 'adj', 'L0_gnn_W1', 'L0_gnn_b1', 'L0_gnn_gamma', 'L0_gnn_beta', 'L0_gnn_W2', 'L0_gnn_b2',
        'L1_gnn_W_qk', 'L1_gnn_W_v', 'L2_gnn_Wv', 'L2_gnn_bv', 'L2_gnn_aw', 'L2_gnn_ab', 'L2_gnn_Wk',
        'L2_gnn_bk', 'L3_gnn_w', 'L3_gnn_a']


def kernel(**inputs):
    import concourse.bacc as bacc
    from concourse.bass_utils import run_bass_kernel_spmd

    nc = bacc.Bacc("TRN2", target_bir_lowering=False, num_devices=1)
    arrays, args = {}, []
    for name in _INS:
        a = np.ascontiguousarray(inputs[name])
        arrays[f"in_{name}"] = a
        args.append(nc.dram_tensor(f"in_{name}", a.shape, mybir.dt.from_np(a.dtype), kind="ExternalInput").ap())
    out = nc.dram_tensor("out", (GRAPHS, N, D), F32, kind="ExternalOutput").ap()
    build(nc, *args, out)
    r = run_bass_kernel_spmd(nc, [arrays], core_ids=[0])
    return r.results[0]["out"]
```

```python
import numpy as np
import concourse.bass as bass
from concourse import mybir
from contextlib import ExitStack

F32 = mybir.dt.float32
F16 = mybir.dt.float16
ALU = mybir.AluOpType
ACT = mybir.ActivationFunctionType
AX = mybir.AxisListType

GRAPHS, N, D, H = 64, 128, 256, 512
GP = 4
AFTER = 2
G = GRAPHS // GP
C = GP * N
DT = D // 128
HT = H // 128
QK = 64
EPS = 1e-5
W_SCALE = 64.0
WK_SCALE = 256.0
W3_SCALE = 16.0
CNT_SCALE = 128.0


class Parts:
    pass


def upto(g, per, k):
    return g * per + k


def xcols(g):
    return bass.ds(g * (GP * D), GP * D)


def gcols(g, j):
    return bass.ds(g * (GP * D) + j * D, D)


def acols(g):
    return bass.ds(g * C, C)


def over_groups(eng, step, lead, lag):
    first = 4 if lag else 2
    for g in range(-lead, first):
        step(g, g % 2, lambda k, g=g: 0 <= g + k < G)
    with eng.Fori(first // 2, G // 2 - 1) as pair:
        step(pair * 2, 0, lambda k: True)
        step(pair * 2 + 1, 1, lambda k: True)
    for g in range(G - 2, G + lag):
        step(g, g % 2, lambda k, g=g: 0 <= g + k < G)


def is_first(g):
    return isinstance(g, int) and g == 0


def over_layers(eng, programs):
    before, drain = None, 0
    for step, lead, lag in programs:
        first = 4 if lag else 2
        for g in range(-2, first):
            if g >= -lead:
                step(g, g % 2, lambda k, g=g: 0 <= g + k < G)
            if 0 <= g + AFTER < drain:
                before(G + g + AFTER, (g + AFTER) % 2, lambda k, g=g: g + AFTER + k < 0)
        with eng.Fori(first // 2, G // 2 - 1) as pair:
            step(pair * 2, 0, lambda k: True)
            step(pair * 2 + 1, 1, lambda k: True)
        for g in range(G - 2, G):
            step(g, g % 2, lambda k, g=g: 0 <= g + k < G)
        before, drain = step, lag
    for g in range(G, G + drain):
        before(g, g % 2, lambda k, g=g: g + k < G)


def reused(g, back=2):
    return not isinstance(g, int) or g >= back


def triple(nc, out, lhs, rhs, start=True, stop=True, **kw):
    nc.tensor.matmul(out, lhs[0], rhs[1], start=start, stop=False, **kw)
    nc.tensor.matmul(out, lhs[1], rhs[0], start=False, stop=False, **kw)
    return nc.tensor.matmul(out, lhs[0], rhs[0], start=False, stop=stop, **kw)


def build(nc, x, adj, W1, b1, gamma, beta, W2, b2, W_qk, W_v, Wv, bv, aw, ab, Wk, bk, w3, a3, out):
    ctx = ExitStack()
    with ctx:
        def sb(name, shape, dt=F32):
            return ctx.enter_context(nc.sbuf_tensor(name, shape, dt))

        def halves(name, shape):
            return [sb(f"{name}_{s}", shape, F16) for s in ("hi", "lo")]

        K = Parts()
        K.bank = [ctx.enter_context(nc.psum_tensor(f"bank{i}", [128, 512], F32)) for i in range(8)]
        K.x = sb("x_resident", [128, GRAPHS * D])
        K.at = sb("adjT_resident", [128, GRAPHS * N])
        K.asum = sb("adj_row_sums", [128, GRAPHS])
        K.ident = sb("ident", [128, 128])
        K.ident16 = sb("ident16", [128, 128], F16)
        K.ones = sb("ones", [128, 128])
        K.ones16 = sb("ones16", [128, 128], F16)
        K.minus_half = sb("minus_half", [128, GP])
        K.w1 = halves("W1T", [128, DT, H])
        K.w2 = halves("W2T", [128, HT, D + 1])
        K.qkv = halves("qkvT", [128, DT, 2 * QK + D])
        K.wk = halves("Wk", [128, DT, 3 * D + 2])
        K.w3 = halves("w3", [128, DT, D + 1])
        K.b1 = sb("b1_col", [128, HT])
        K.w2beta = sb("W2beta_rows", [128, D])
        K.edge_bias = sb("edge_bias", [128, 1])
        K.b2row = sb("b2_parts", [128, D], F16)
        K.bkrow = sb("bk_parts", [128, D], F16)

        K.xd = x.rearrange("g n d -> n g d")
        K.ad = adj.rearrange("g n e -> n g e")
        K.od = out.rearrange("g n d -> n g d")
        K.adjn = [sb(f"adj{p}", [128, GP, N]) for p in range(2)]
        K.adj_in, K.x_in = ([ctx.enter_context(nc.semaphore(f"{name}{p}")) for p in range(2)]
                            for name in ("adj_in", "x_in"))
        setup(nc, K, W1, b1, gamma, beta, W2, b2, W_qk, W_v, Wv, bv, aw, ab, Wk, bk, w3, a3)
        layer0(nc, K)
        graph_layers(nc, K)


def graph_layers(nc, K):
    with ExitStack() as ctx:
        K.F = front(nc, ctx)
        K.x_new, K.scores_after = {}, {}
        second = layer2(nc, K, ctx)
        with ExitStack() as tiles:
            layers = [layer1(nc, K, ctx, tiles), second]
        layers.append(layer3(nc, K, ctx))
        with nc.Block() as block:
            @block.sync
            def _(sp):
                for sync, _, _, _, _ in layers:
                    sync(sp)

            @block.tensor
            def _(pe):
                over_layers(pe, [tensor(pe) for _, tensor, _, _, _ in layers])

            @block.scalar
            def _(act):
                over_layers(act, [scalar(act) for _, _, scalar, _, _ in layers])

            @block.vector
            def _(dve):
                over_layers(dve, [vector(dve) for _, _, _, vector, _ in layers])

            @block.gpsimd
            def _(pool):
                over_layers(pool, [gpsimd(pool) for _, _, _, _, gpsimd in layers])


def setup(nc, K, W1, b1, gamma, beta, W2, b2, W_qk, W_v, Wv, bv, aw, ab, Wk, bk, w3, a3):
    ctx = ExitStack()
    with ctx:
        def sb(name, shape, dt=F32):
            return ctx.enter_context(nc.sbuf_tensor(name, shape, dt))

        def sem(name):
            return ctx.enter_context(nc.semaphore(name))

        w1n, w2n = sb("w1n", [128, HT, D]), sb("w2n", [128, DT, H])
        wqn, wvn = sb("wqn", [128, D]), sb("wvn", [128, DT, D])
        gam, bet, gam_s = sb("gam", [128, HT]), sb("bet", [128, HT]), sb("gam_scaled", [128, HT])
        b2n, bkn, bks = sb("b2n", [128, D]), sb("bkn", [128, 3, D]), sb("bk_sums", [128, 3, D])
        l2v, l2k = sb("l2v", [128, DT, D]), sb("l2k", [128, 3, DT, D])
        awb, bvb, abb = sb("awb", [128, 2 * D]), sb("bvb", [128, D]), sb("abb", [128, 1])
        w3n, a3b = sb("w3n", [128, DT, D]), sb("a3b", [128, D])
        w2g, w2b, w2c = sb("w2_gamma", [128, HT, D]), sb("w2_beta", [128, HT, D]), sb("w2_centred", [128, HT, D + 1])
        wkf, w3f = sb("wkf", [128, DT, 3 * D + 2]), sb("w3f", [128, DT, D + 1])
        prod, ssum, edge = sb("prod", [128, 8, D]), sb("ssum", [128, DT, 2]), sb("edge", [128, 4])
        mean = sb("w2_mean", [128, D])
        w12_in, vec_in, rows_in, rest_in = map(sem, ("w12_in", "vec_in", "rows_in", "rest_in"))
        const = sem("const")
        wT_ps, fold_ps = map(sem, ("wT_ps", "fold_ps"))
        folding = sem("folding")
        w2g_ok, w2c_ok, w12_hi, qkv_hi = map(sem, ("w2g_ok", "w2c_ok", "w12_hi", "qkv_hi"))
        prod_ok, wk3_part, wk3_hi, bk_scaled, row_hi = map(
            sem, ("prod_ok", "wk3_part", "wk3_hi", "bk_scaled", "row_hi"))
        with nc.Block() as block:
            rest = [
                (wqn[:], W_qk), (wvn[:], W_v.rearrange("(t p) d -> p t d", p=128)),
                (l2k[:], Wk.rearrange("k (t p) o -> p k t o", p=128)),
                (l2v[:], Wv.rearrange("(t p) o -> p t o", p=128)),
                (w3n[:], w3.rearrange("(t p) o -> p t o", p=128)),
                (awb[:], aw.rearrange("a b -> b a").to_broadcast([128, 2 * D])),
                (bvb[:], bv.rearrange("(a b) -> a b", a=1).to_broadcast([128, D])),
                (abb[:], ab.rearrange("(a b) -> a b", a=1).to_broadcast([128, 1])),
                (a3b[:], a3.rearrange("(a b) -> a b", a=1).to_broadcast([128, D])),
            ]
            rest_loaded = 16 * len(rest)
            rows = [(b2n[r:r + 1, :], b2.rearrange("(a b) -> a b", a=1)) for r in (0, 32)]
            rows += [(bkn[r:r + 1, :, :], bk.rearrange("(a k) b -> a k b", a=1)) for r in (0, 32)]

            @block.sync
            def _(sp):
                sp.dma_start(w2n[:], W2.rearrange("(t p) h -> p t h", p=128)).then_inc(w12_in, 16)
                sp.dma_start(w1n[:], W1.rearrange("(t p) d -> p t d", p=128)).then_inc(w12_in, 16)
                for g in range(2):
                    load_adj(K, sp, g, g)
                for dst, src in rest:
                    sp.dma_start(dst, src).then_inc(rest_in, 16)
                for g in range(2):
                    load_x(K, sp, g, g)

            @block.gpsimd
            def _(pool):
                for m in (K.ident, K.ident16):
                    pool.memset(m[:], 0.0).then_inc(const, 1)
                pool.wait_ge(const, 2)
                for m in (K.ident, K.ident16):
                    pool.affine_select(out=m[:], in_=m[:], compare_op=ALU.not_equal, fill=1.0, base=0,
                                       pattern=[[-1, 128]], channel_multiplier=1).then_inc(const, 1)
                pool.memset(b2n[:], 0.0).then_inc(const, 1)
                pool.memset(bkn[:], 0.0).then_inc(const, 1)
                pool.memset(K.ones[:], 1.0).then_inc(const, 1)
                pool.memset(K.ones16[:], 1.0)
                pool.memset(K.minus_half[:], -0.5)
                pool.wait_ge(rows_in, 16 * len(rows))
                pool.tensor_tensor(bks[:, 0, :], bkn[:, 0, :], bkn[:, 1, :], ALU.add).then_inc(const, 1)
                pool.wait_ge(const, 8)
                pool.tensor_tensor(bks[:, 1, :], bks[:, 0, :], bkn[:, 2, :], ALU.add).then_inc(const, 1)
                pool.wait_ge(wk3_hi, 1)
                pool.tensor_tensor(K.w3[1][:], w3f[:], K.w3[0][:], ALU.subtract)
                pool.wait_ge(wk3_hi, 2)
                pool.tensor_tensor(K.wk[1][:], wkf[:], K.wk[0][:], ALU.subtract)

            @block.tensor
            def _(pe):
                pe.wait_ge(const, 4)
                pe.wait_ge(w12_in, 32)
                for h in range(HT):
                    for d in range(DT):
                        c = (h % 2) * D + d * 128
                        m = pe.transpose(K.bank[2 + h // 2][:, c:c + 128],
                                         w2n[:, d, h * 128:(h + 1) * 128], K.ident[:])
                m.then_inc(wT_ps, 1)
                for d in range(DT):
                    for h in range(HT):
                        m = pe.transpose(K.bank[d][:, h * 128:(h + 1) * 128],
                                         w1n[:, h, d * 128:(d + 1) * 128], K.ident[:])
                m.then_inc(wT_ps, 1)
                pe.wait_ge(const, 7)
                pe.wait_ge(w2g_ok, 2)
                for h in range(HT):
                    m = pe.matmul(K.bank[6][:, 0:D], K.ones[:], w2g[:, h, :], start=h == 0, stop=h == HT - 1)
                m.then_inc(fold_ps, 1)
                for h in range(HT):
                    m = pe.matmul(K.bank[7][:, 0:D], K.ones[:], w2b[:, h, :], start=h == 0, stop=h == HT - 1)
                m.then_inc(fold_ps, 1)
                pe.wait_ge(rest_in, rest_loaded)
                for d in range(DT):
                    pe.transpose(K.bank[4 + d][:, 0:128], wqn[:, d * 128:(d + 1) * 128], K.ident[:])
                    for e in range(DT):
                        m = pe.transpose(K.bank[4 + d][:, (e + 1) * 128:(e + 2) * 128],
                                         wvn[:, e, d * 128:(d + 1) * 128], K.ident[:])
                m.then_inc(wT_ps, 1)

            @block.scalar
            def _(act):
                with nc.allow_non_contiguous_dma(reason="three short vectors, a value per partition"):
                    for dst, src in ((gam, gamma), (bet, beta), (K.b1, b1)):
                        act.dma_start(dst[:], src.rearrange("(t p) -> p t", p=128)).then_inc(vec_in, 16)
                act.wait_ge(const, 6)
                for dst, src in rows:
                    act.dma_start(dst, src).then_inc(rows_in, 16)
                act.wait_ge(wT_ps, 2)
                for d in range(DT):
                    act.activation(K.w1[0][:, d, :], K.bank[d][:], ACT.Copy, scale=W_SCALE).then_inc(w12_hi, 1)
                act.wait_ge(w2c_ok, HT + 1)
                act.activation(K.w2[0][:], w2c[:], ACT.Copy).then_inc(w12_hi, 1)
                act.wait_ge(const, 9)
                act.activation(bks[:, 2, :], bks[:, 1, :], ACT.Copy, scale=WK_SCALE).then_inc(bk_scaled, 1)
                act.activation(K.b2row[:], b2n[:], ACT.Copy).then_inc(row_hi, 1)
                act.wait_ge(rest_in, rest_loaded)
                act.activation(w3f[:, :, 0:D], w3n[:], ACT.Copy, scale=W3_SCALE).then_inc(wk3_part, 1)
                for c, k in ((0, 2), (D + 2, 1), (2 * D + 2, 0)):
                    act.activation(wkf[:, :, c:c + D], l2k[:, k], ACT.Copy, scale=WK_SCALE).then_inc(wk3_part, 1)
                act.wait_ge(wk3_part, 7)
                act.activation(K.w3[0][:], w3f[:], ACT.Copy).then_inc(wk3_hi, 1)
                act.wait_ge(wT_ps, 3)
                for d in range(DT):
                    act.activation(K.qkv[0][:, d, :], K.bank[4 + d][:, 0:2 * QK + D], ACT.Copy,
                                   scale=W_SCALE).then_inc(qkv_hi, 1)
                act.activation(K.wk[0][:], wkf[:], ACT.Copy).then_inc(wk3_hi, 1)
                act.wait_ge(bk_scaled, 1)
                act.activation(K.bkrow[:], bks[:, 2, :], ACT.Copy).then_inc(row_hi, 1)

            @block.vector
            def _(dve):
                dve.memset(w2c[:, :, D:D + 1], W_SCALE / H).then_inc(w2c_ok, 1)
                dve.wait_ge(vec_in, 48)
                dve.tensor_scalar(gam_s[:], gam[:], W_SCALE, None, ALU.mult).then_inc(folding, 1)
                dve.wait_ge(folding, 1)
                dve.wait_ge(wT_ps, 1)
                for h in range(HT):
                    src = K.bank[2 + h // 2][:, (h % 2) * D:(h % 2 + 1) * D]
                    m = dve.tensor_scalar(w2g[:, h, :], src, gam_s[:, h:h + 1], None, ALU.mult)
                m.then_inc(w2g_ok, 1)
                for h in range(HT):
                    src = K.bank[2 + h // 2][:, (h % 2) * D:(h % 2 + 1) * D]
                    m = dve.tensor_scalar(w2b[:, h, :], src, bet[:, h:h + 1], None, ALU.mult)
                m.then_inc(w2g_ok, 1)
                dve.wait_ge(w12_hi, DT)
                for d in range(DT):
                    dve.scalar_tensor_tensor(K.w1[1][:, d, :], K.bank[d][:], W_SCALE, K.w1[0][:, d, :],
                                             ALU.mult, ALU.subtract)
                dve.wait_ge(fold_ps, 1)
                dve.tensor_scalar(mean[:], K.bank[6][:, 0:D], 1.0 / H, None, ALU.mult).then_inc(folding, 1)
                dve.wait_ge(folding, 2)
                for h in range(HT):
                    dve.tensor_tensor(w2c[:, h, 0:D], w2g[:, h, :], mean[:], ALU.subtract).then_inc(w2c_ok, 1)
                dve.wait_ge(fold_ps, 2)
                dve.tensor_copy(K.w2beta[:], K.bank[7][:, 0:D])
                dve.wait_ge(rest_in, rest_loaded)
                for d in range(DT):
                    dve.tensor_tensor(prod[:, 4 + d, :], w3n[:, d, :], a3b[:], ALU.mult).then_inc(prod_ok, 1)
                for d in range(DT):
                    for s in range(2):
                        dve.tensor_tensor(prod[:, 2 * d + s, :], l2v[:, d, :], awb[:, s * D:(s + 1) * D],
                                          ALU.mult).then_inc(prod_ok, 1)
                for s in range(2):
                    dve.tensor_tensor(prod[:, 6 + s, :], bvb[:], awb[:, s * D:(s + 1) * D],
                                      ALU.mult).then_inc(prod_ok, 1)
                dve.wait_ge(prod_ok, 8)
                for d in range(DT):
                    dve.tensor_reduce(w3f[:, d, D:D + 1], prod[:, 4 + d, :], AX.X, ALU.add).then_inc(wk3_part, 1)
                for d in range(DT):
                    dve.tensor_reduce(ssum[:, d, :], prod[:, 2 * d:2 * d + 2, :], AX.X, ALU.add).then_inc(folding, 1)
                dve.tensor_reduce(edge[:, 0:2], prod[:, 6:8, :], AX.X, ALU.add).then_inc(folding, 1)
                dve.wait_ge(folding, 4)
                dve.tensor_scalar(wkf[:, :, D:D + 2], ssum[:], WK_SCALE, None, ALU.mult).then_inc(wk3_part, 1)
                dve.wait_ge(w12_hi, DT + 1)
                dve.tensor_tensor(K.w2[1][:], w2c[:], K.w2[0][:], ALU.subtract)
                dve.wait_ge(folding, 5)
                dve.tensor_tensor(edge[:, 2:3], edge[:, 0:1], edge[:, 1:2], ALU.add).then_inc(folding, 1)
                dve.wait_ge(folding, 6)
                dve.tensor_tensor(K.edge_bias[:], edge[:, 2:3], abb[:], ALU.add)
                dve.wait_ge(qkv_hi, DT)
                for d in range(DT):
                    dve.scalar_tensor_tensor(K.qkv[1][:, d, :], K.bank[4 + d][:, 0:2 * QK + D], W_SCALE,
                                             K.qkv[0][:, d, :], ALU.mult, ALU.subtract)
                low = slice(32, 33)
                dve.wait_ge(row_hi, 2)
                dve.tensor_tensor(K.b2row[low, :], b2n[low, :], K.b2row[low, :], ALU.subtract)
                dve.tensor_tensor(K.bkrow[low, :], bks[low, 2, :], K.bkrow[low, :], ALU.subtract)


def load_adj(K, sp, g, p):
    sp.dma_start(K.adjn[p][:], K.ad[:, bass.ds(g * GP, GP), :]).then_inc(K.adj_in[p], 16)


def load_x(K, sp, g, p):
    sp.dma_start(K.x[:, xcols(g)].rearrange("p (g d) -> p g d", g=GP),
                 K.xd[:, bass.ds(g * GP, GP), :]).then_inc(K.x_in[p], 16)


def layer0(nc, K):
    ctx = ExitStack()
    with ctx:
        def sb(name, shape, dt=F32):
            return ctx.enter_context(nc.sbuf_tensor(name, shape, dt))

        def sem(name):
            return ctx.enter_context(nc.semaphore(name))

        def halves(name, shape):
            return [sb(f"{name}_{s}", shape, F16) for s in ("hi", "lo")]

        bank = K.bank
        b_adj, b_gram = bank[0], bank[1]
        b_mix, b_hid, b_z = bank[2:4], bank[4:6], bank[6:8]

        adjn = K.adjn
        inc = [sb(f"incT{p}", [128, C], F16) for p in range(2)]
        wcol = halves("wcol", [128, GP])
        cnt, cnt1, rcnt = sb("cnt", [128, GP]), sb("cnt1", [128, GP]), sb("rcnt", [128, GP])
        rcs = halves("rcs", [128, GP])
        incb = [halves(f"incB{p}", [128, C]) for p in range(2)]
        dcl, drc, dpos, dinv = (sb(f"d{i}", [128, GP]) for i in range(4))
        dis = halves("dis", [128, GP])
        dbc, pf = sb("dbc", [128, C]), sb("pf", [128, C])
        ps = [halves(f"P{p}", [128, C]) for p in range(2)]
        xs = [halves(f"x{p}", [128, GP, D]) for p in range(2)]
        px = [halves(f"px{p}", [128, DT, C]) for p in range(2)]
        hf = sb("hf", [128, HT, C])
        hs = halves("h", [128, HT, C])
        hq, hqp, hqs = sb("hq", [128, HT, C]), sb("hq_partial", [128, 2, C]), sb("hqs", [128, C])
        zf, zn = sb("zf", [128, GP, D + 2]), sb("zn", [128, GP, D])
        zs = halves("z", [128, GP, D])
        zm2, zvar, zrs = sb("zm2", [128, GP]), sb("zvar", [128, GP]), sb("zrs", [128, GP])
        L = norm(nc, ctx, "l0", 2)

        adj_in, x_in = K.adj_in, K.x_in
        adjT_ps, adjT_sb, inc_ok, wcol_ok, small, incb_ok = map(
            sem, ("adjT_ps", "adjT_sb", "inc_ok", "wcol_ok", "small", "incb_ok"))
        deg_ps, gram_ps, dinv_ok, dbc_ps, dbc_sb, pf_ok, p_hi, p_lo = map(
            sem, ("deg_ps", "gram_ps", "dinv_ok", "dbc_ps", "dbc_sb", "pf_ok", "p_hi", "p_lo"))
        x_hi, x_lo, px_ps, px_hi, px_lo = map(sem, ("x_hi", "x_lo", "px_ps", "px_hi", "px_lo"))
        hid_ps, hf_ok, h_hi, h_sq, h_lo, hqs_ok = map(
            sem, ("hid_ps", "hf_ok", "h_hi", "h_sq", "h_lo", "hqs_ok"))
        z_ps, zf_ok, zvar_ok, zrs_ok, zn_ok, z_hi, z_lo = map(
            sem, ("z_ps", "zf_ok", "zvar_ok", "zrs_ok", "zn_ok", "z_hi", "z_lo"))
        y_ps = sem("y_ps")
        dchain = sem("dchain")

        with nc.Block() as block:
            @block.sync
            def _(sp):
                def load(g, p, has):
                    if has(0) and reused(g):
                        sp.wait_ge(adjT_ps, upto(g - 2, 1, 1))
                        load_adj(K, sp, g, p)
                        sp.wait_ge(x_lo, upto(g - 2, 1, 1))
                        load_x(K, sp, g, p)
                over_groups(sp, load, 0, 0)

            @block.tensor
            def _(pe):
                def transpose_adj(g, p):
                    pe.wait_ge(adj_in[p], 8 * (g - p) + 16)
                    if reused(g, 1):
                        pe.wait_ge(dbc_sb, upto(g - 1, 1, 1))
                    for j in range(GP):
                        m = pe.transpose(b_adj[:, j * N:(j + 1) * N], adjn[p][:, j, :], K.ident[:])
                    m.then_inc(adjT_ps, 1)

                def hidden(g, p, h):
                    if h == 0:
                        pe.wait_ge(px_lo, upto(g, 2, 2))
                        pe.wait_ge(px_hi, upto(g, 2, 2))
                    if h >= 2 or reused(g, 1):
                        pe.wait_ge(hf_ok, upto(g, HT, h - 1))
                    for d in range(DT):
                        m = triple(nc, b_hid[h % 2][:], [w[:, d, h * 128:(h + 1) * 128] for w in K.w1],
                                   [s[:, d, :] for s in px[p]], start=d == 0, stop=d == DT - 1)
                    m.then_inc(hid_ps, 1)

                def gram(g, p):
                    pe.wait_ge(incb_ok, upto(g, 8, 8))
                    if reused(g, 1):
                        pe.wait_ge(pf_ok, upto(g - 1, 1, 1))
                    for j in range(GP):
                        c = slice(j * N, (j + 1) * N)
                        pe.matmul(b_gram[:, c], inc[p][:, c], incb[p][1][:, c], start=True, stop=False)
                        m = pe.matmul(b_gram[:, c], inc[p][:, c], incb[p][0][:, c], start=False, stop=True)
                    m.then_inc(gram_ps, 1)

                def degree(g, p):
                    pe.wait_ge(wcol_ok, upto(g, 2, 2))
                    pe.wait_ge(inc_ok, upto(g, 1, 1))
                    pe.wait_ge(adjT_sb, upto(g, 1, 1))
                    for j in range(GP):
                        c = slice(j * N, (j + 1) * N)
                        pe.matmul(b_adj[:, j:j + 1], inc[p][:, c], wcol[1][:, j:j + 1], start=True, stop=False)
                        m = pe.matmul(b_adj[:, j:j + 1], inc[p][:, c], wcol[0][:, j:j + 1], start=False, stop=True)
                    m.then_inc(deg_ps, 1)

                def spread_degrees(g, p):
                    pe.wait_ge(dinv_ok, upto(g, 2, 2))
                    for j in range(GP):
                        for i, s in enumerate((1, 0)):
                            m = pe.matmul(b_adj[:, j * N:(j + 1) * N], dis[s][:, j:j + 1].to_broadcast([128, 128]),
                                          K.ident16[:], start=i == 0, stop=i == 1)
                    m.then_inc(dbc_ps, 1)

                def mix_x(g, p, d):
                    if d == 0:
                        pe.wait_ge(x_hi, upto(g, 1, 1))
                        pe.wait_ge(x_lo, upto(g, 1, 1))
                        pe.wait_ge(p_hi, upto(g, 1, 1))
                        pe.wait_ge(p_lo, upto(g, 1, 1))
                    if reused(g, 2):
                        pe.wait_ge(L.pre_ok, upto(g - 2, 2, d + 1))
                    elif g == 1:
                        pe.wait_ge(px_lo, upto(0, 2, d + 1))
                    for j in range(GP):
                        c = slice(j * N, (j + 1) * N)
                        m = triple(nc, b_mix[d][:, c], [s[:, j, d * 128:(d + 1) * 128] for s in xs[p]],
                                   [s[:, c] for s in ps[p]])
                    m.then_inc(px_ps, 1)

                def project(g, j):
                    if j >= 2 or reused(g, 1):
                        pe.wait_ge(zf_ok, upto(g, GP, j - 1))
                    for h in range(HT):
                        if j == 0:
                            pe.wait_ge(h_lo, upto(g, HT, h + 1))
                        triple(nc, b_z[j % 2][:, 0:D + 1], [s[:, h, j * N:(j + 1) * N] for s in hs],
                               [w[:, h, :] for w in K.w2], start=h == 0, stop=h == HT - 1)

                def square_sums(g, j):
                    if j == 0:
                        pe.wait_ge(hqs_ok, upto(g, 3, 3))
                    pe.matmul(b_z[j % 2][:, D + 1:D + 2], hqs[:, j * N:(j + 1) * N], K.ones[:, 0:1],
                              start=True, stop=True).then_inc(z_ps, 1)

                def mix_z(g, p, i):
                    if isinstance(g, int) and g == G - 1:
                        pe.wait_ge(L.pre_ok, upto(g - 1, 2, i + 1))
                    elif i == 0:
                        pe.wait_ge(px_lo, upto(g + 1, 2, 2))
                    for jj in range(2):
                        j = 2 * i + jj
                        pe.wait_ge(z_hi, upto(g, GP, j + 1))
                        pe.wait_ge(z_lo, upto(g, GP, j + 1))
                        o = b_mix[i][:, jj * D:(jj + 1) * D]
                        pe.matmul(o, K.ones16[:], K.b2row[:], start=True, stop=False)
                        m = triple(nc, o, [s[:, j * N:(j + 1) * N] for s in ps[p]],
                                   [s[:, j, :] for s in zs], start=False)
                    m.then_inc(y_ps, 1)

                def step(g, p, has):
                    q = 1 - p
                    if has(-1):
                        hidden(g - 1, q, 3)
                    if has(-2):
                        mix_z(g - 2, p, 0)
                        mix_z(g - 2, p, 1)
                    if has(0):
                        spread_degrees(g, p)
                        gram(g, p)
                    if has(-1):
                        project(g - 1, 0)
                        project(g - 1, 1)
                        square_sums(g - 1, 0)
                    if has(1):
                        transpose_adj(g + 1, q)
                    if has(-1):
                        square_sums(g - 1, 1)
                        project(g - 1, 2)
                        square_sums(g - 1, 2)
                    if has(0):
                        mix_x(g, p, 0)
                        mix_x(g, p, 1)
                    if has(-1):
                        project(g - 1, 3)
                        square_sums(g - 1, 3)
                    if has(0):
                        hidden(g, p, 0)
                        hidden(g, p, 1)
                        hidden(g, p, 2)
                    if has(1):
                        degree(g + 1, q)
                over_groups(pe, step, 1, 2)

            @block.scalar
            def _(act):
                def hidden(g, h):
                    act.wait_ge(hid_ps, upto(g, HT, h + 1))
                    if reused(g, 1):
                        act.wait_ge(h_lo, upto(g - 1, HT, h + 1))
                        act.wait_ge(h_sq, upto(g - 1, HT, h + 1))
                    act.activation(hf[:, h, :], b_hid[h % 2][:], ACT.Relu, bias=K.b1[:, h:h + 1],
                                   scale=1.0 / W_SCALE).then_inc(hf_ok, 1)

                def square(g, h):
                    act.wait_ge(hf_ok, upto(g, HT, h + 1))
                    if reused(g, 1):
                        act.wait_ge(hqs_ok, upto(g - 1, 3, 3))
                    act.activation(hq[:, h, :], hf[:, h, :], ACT.Square).then_inc(h_sq, 1)

                def copy_z(g, j):
                    act.wait_ge(z_ps, upto(g, GP, j + 1))
                    if reused(g, 1):
                        act.wait_ge(zn_ok, upto(g - 1, GP, GP))
                    act.activation(zf[:, j, :], b_z[j % 2][:, 0:D + 2], ACT.Copy,
                                   scale=1.0 / W_SCALE).then_inc(zf_ok, 1)

                def z_high(g, j):
                    act.wait_ge(zn_ok, upto(g, GP, j + 1))
                    if reused(g, 1):
                        act.wait_ge(y_ps, upto(g - 1, 2, 2))
                    act.activation(zs[0][:, j, :], zn[:, j, :], ACT.Copy).then_inc(z_hi, 1)

                def x_high(g, p):
                    act.wait_ge(x_in[p], 8 * (g - p) + 16)
                    if reused(g):
                        act.wait_ge(px_ps, upto(g - 2, 2, 2))
                    act.activation(xs[p][0][:], K.x[:, xcols(g)].rearrange("p (g d) -> p g d", g=GP),
                                   ACT.Copy).then_inc(x_hi, 1)

                def copy_degrees(g):
                    act.wait_ge(dbc_ps, upto(g, 1, 1))
                    if reused(g, 1):
                        act.wait_ge(pf_ok, upto(g - 1, 1, 1))
                    act.activation(dbc[:], b_adj[:], ACT.Copy).then_inc(dbc_sb, 1)

                def operator_high(g, p):
                    act.wait_ge(pf_ok, upto(g, 1, 1))
                    if reused(g):
                        act.wait_ge(y_ps, upto(g - 2, 2, 2))
                    act.activation(ps[p][0][:], pf[:], ACT.Copy).then_inc(p_hi, 1)

                def mixed_high(g, p, d):
                    act.wait_ge(px_ps, upto(g, 2, d + 1))
                    if reused(g):
                        act.wait_ge(hid_ps, upto(g - 2, HT, HT))
                    act.activation(px[p][0][:, d, :], b_mix[d][:], ACT.Copy).then_inc(px_hi, 1)

                def copy_adj(g):
                    act.wait_ge(adjT_ps, upto(g, 1, 1))
                    act.activation(K.at[:, acols(g)], b_adj[:], ACT.Copy).then_inc(adjT_sb, 1)

                def step(g, p, has):
                    q = 1 - p
                    if has(1):
                        copy_adj(g + 1)
                    if has(-1):
                        copy_z(g - 1, 3)
                    if has(1):
                        x_high(g + 1, q)
                    if has(0):
                        hidden(g, 0)
                        hidden(g, 1)
                    if has(-1):
                        z_high(g - 1, 0)
                        z_high(g - 1, 1)
                    if has(0):
                        square(g, 0)
                    if has(-1):
                        z_high(g - 1, 2)
                    if has(0):
                        square(g, 1)
                    if has(-1):
                        z_high(g - 1, 3)
                    if has(0):
                        hidden(g, 2)
                        square(g, 2)
                        hidden(g, 3)
                        square(g, 3)
                    if has(1):
                        copy_degrees(g + 1)
                    if has(-2):
                        norm_apply(K, L, act, g - 2, p, 0)
                        norm_apply(K, L, act, g - 2, p, 1)
                        norm_apply(K, L, act, g - 2, p, 2)
                    if has(1):
                        operator_high(g + 1, q)
                    if has(-2):
                        norm_apply(K, L, act, g - 2, p, 3)
                    if has(0):
                        copy_z(g, 0)
                        copy_z(g, 1)
                        copy_z(g, 2)
                    if has(1):
                        mixed_high(g + 1, q, 0)
                        mixed_high(g + 1, q, 1)
                over_groups(act, step, 1, 2)

            @block.vector
            def _(dve):
                def incidence(g, p):
                    dve.wait_ge(adjT_sb, upto(g, 1, 1))
                    if reused(g):
                        dve.wait_ge(deg_ps, upto(g - 2, 1, 1))
                    dve.tensor_scalar(inc[p][:], K.at[:, acols(g)], 0.0, None, ALU.not_equal).then_inc(inc_ok, 1)

                def edge_weights(g):
                    first = K.at[:, acols(g)].rearrange("p (g n) -> p g n", g=GP)[:, :, 0]
                    if reused(g, 1):
                        dve.wait_ge(deg_ps, upto(g - 1, 1, 1))
                    dve.tensor_scalar(wcol[0][:], first, 1.0, None, ALU.mult).then_inc(wcol_ok, 1)
                    dve.wait_ge(wcol_ok, upto(g, 2, 1))
                    dve.tensor_tensor(wcol[1][:], first, wcol[0][:], ALU.subtract).then_inc(wcol_ok, 1)

                def counts(g, p):
                    dve.wait_ge(inc_ok, upto(g, 1, 1))
                    dve.tensor_reduce(cnt[:], inc[p][:].rearrange("p (g n) -> p g n", g=GP), AX.X,
                                      ALU.add).then_inc(small, 1)
                    dve.wait_ge(small, upto(g, 5, 1))
                    dve.tensor_scalar(cnt1[:], cnt[:], 1.0, 1.0 / CNT_SCALE, ALU.max, ALU.mult).then_inc(small, 1)
                    dve.wait_ge(small, upto(g, 5, 2))
                    dve.reciprocal(rcnt[:], cnt1[:]).then_inc(small, 1)
                    dve.wait_ge(small, upto(g, 5, 3))
                    dve.tensor_copy(rcs[0][:], rcnt[:]).then_inc(small, 1)
                    dve.wait_ge(small, upto(g, 5, 4))
                    dve.tensor_tensor(rcs[1][:], rcnt[:], rcs[0][:], ALU.subtract).then_inc(small, 1)

                def scale_incidence(g, p, s):
                    dve.wait_ge(small, upto(g, 5, 5))
                    if reused(g):
                        dve.wait_ge(gram_ps, upto(g - 2, 1, 1))
                    for j in range(GP):
                        c = slice(j * N, (j + 1) * N)
                        dve.tensor_scalar(incb[p][s][:, c], inc[p][:, c], rcs[s][:, j:j + 1], None,
                                          ALU.mult).then_inc(incb_ok, 1)

                def degrees(g):
                    dve.wait_ge(deg_ps, upto(g, 1, 1))
                    dve.tensor_scalar(dcl[:], b_adj[:, 0:GP], 1e-37, None, ALU.max).then_inc(dchain, 1)
                    dve.tensor_scalar(dpos[:], b_adj[:, 0:GP], 0.0, 1.0 / CNT_SCALE, ALU.is_gt,
                                      ALU.mult).then_inc(dchain, 1)
                    dve.wait_ge(dchain, upto(g, 4, 2))
                    dve.reciprocal(drc[:], dcl[:]).then_inc(dchain, 1)
                    dve.wait_ge(dchain, upto(g, 4, 3))
                    dve.tensor_tensor(dinv[:], drc[:], dpos[:], ALU.mult).then_inc(dchain, 1)
                    dve.wait_ge(dchain, upto(g, 4, 4))
                    if reused(g, 1):
                        dve.wait_ge(dbc_ps, upto(g - 1, 1, 1))
                    dve.tensor_copy(dis[0][:], dinv[:]).then_inc(dinv_ok, 1)
                    dve.wait_ge(dinv_ok, upto(g, 2, 1))
                    dve.tensor_tensor(dis[1][:], dinv[:], dis[0][:], ALU.subtract).then_inc(dinv_ok, 1)

                def hidden_high(g, h):
                    dve.wait_ge(hf_ok, upto(g, HT, h + 1))
                    if reused(g, 1):
                        dve.wait_ge(z_ps, upto(g - 1, GP, GP))
                    dve.tensor_copy(hs[0][:, h, :], hf[:, h, :]).then_inc(h_hi, 1)

                def hidden_low(g, h):
                    dve.wait_ge(h_hi, upto(g, HT, h + 1))
                    dve.tensor_tensor(hs[1][:, h, :], hf[:, h, :], hs[0][:, h, :],
                                      ALU.subtract).then_inc(h_lo, 1)

                def operator(g, p):
                    dve.wait_ge(gram_ps, upto(g, 1, 1))
                    dve.wait_ge(dbc_sb, upto(g, 1, 1))
                    if reused(g, 1):
                        dve.wait_ge(p_hi, upto(g - 1, 1, 1))
                        dve.wait_ge(p_lo, upto(g - 1, 1, 1))
                    dve.tensor_tensor(pf[:], b_gram[:], dbc[:], ALU.mult).then_inc(pf_ok, 1)

                def operator_low(g, p):
                    dve.wait_ge(p_hi, upto(g, 1, 1))
                    dve.wait_ge(pf_ok, upto(g, 1, 1))
                    if reused(g):
                        dve.wait_ge(y_ps, upto(g - 2, 2, 2))
                    dve.tensor_tensor(ps[p][1][:], pf[:], ps[p][0][:], ALU.subtract).then_inc(p_lo, 1)

                def mixed_low(g, p, d):
                    dve.wait_ge(px_hi, upto(g, 2, d + 1))
                    if reused(g):
                        dve.wait_ge(hid_ps, upto(g - 2, HT, HT))
                    dve.tensor_tensor(px[p][1][:, d, :], b_mix[d][:], px[p][0][:, d, :],
                                      ALU.subtract).then_inc(px_lo, 1)

                def layer_out(g, p, i):
                    dve.wait_ge(y_ps, upto(g, 2, i + 1))
                    pre_free(L, dve, g)
                    dve.scalar_tensor_tensor(L.pre[p][:, 2 * i:2 * i + 2, :].rearrange("p a b -> p (a b)"),
                                             b_mix[i][:], 0.5, K.x[:, bass.ds(g * (GP * D) + i * 2 * D, 2 * D)],
                                             ALU.mult, ALU.add).then_inc(L.pre_ok, 1)

                def hidden_norm(g):
                    dve.wait_ge(zf_ok, upto(g, GP, GP))
                    dve.tensor_tensor(zm2[:], zf[:, :, D], zf[:, :, D], ALU.mult).then_inc(zvar_ok, 1)
                    dve.wait_ge(zvar_ok, upto(g, 3, 1))
                    dve.scalar_tensor_tensor(zvar[:], zf[:, :, D + 1], W_SCALE / H, zm2[:], ALU.mult,
                                             ALU.subtract).then_inc(zvar_ok, 1)
                    dve.wait_ge(zvar_ok, upto(g, 3, 2))
                    if reused(g, 1):
                        dve.wait_ge(zrs_ok, upto(g - 1, 1, 1))
                    dve.tensor_scalar(zvar[:], zvar[:], 0.0, EPS, ALU.max, ALU.add).then_inc(zvar_ok, 1)

                def normalise(g, j):
                    if j == 0:
                        dve.wait_ge(zrs_ok, upto(g, 1, 1))
                    if reused(g, 1):
                        dve.wait_ge(z_hi, upto(g - 1, GP, j + 1))
                        dve.wait_ge(z_lo, upto(g - 1, GP, j + 1))
                    dve.scalar_tensor_tensor(zn[:, j, :], zf[:, j, 0:D], zrs[:, j:j + 1], K.w2beta[:],
                                             ALU.mult, ALU.add).then_inc(zn_ok, 1)

                def step(g, p, has):
                    q = 1 - p
                    if has(1):
                        incidence(g + 1, q)
                    if has(-2):
                        norm_shift(L, dve, g - 2, p)
                    if has(-1):
                        hidden_norm(g - 1)
                    if has(1):
                        counts(g + 1, q)
                    if has(-1):
                        normalise(g - 1, 0)
                    if has(1):
                        edge_weights(g + 1)
                    if has(-1):
                        normalise(g - 1, 1)
                        normalise(g - 1, 2)
                    if has(0):
                        hidden_high(g, 0)
                    if has(-1):
                        normalise(g - 1, 3)
                    if has(0):
                        hidden_low(g, 0)
                        hidden_high(g, 1)
                    if has(1):
                        scale_incidence(g + 1, q, 0)
                        degrees(g + 1)
                    if has(0):
                        hidden_low(g, 1)
                        hidden_high(g, 2)
                    if has(1):
                        scale_incidence(g + 1, q, 1)
                    if has(0):
                        hidden_low(g, 2)
                        hidden_high(g, 3)
                        hidden_low(g, 3)
                    if has(1):
                        operator(g + 1, q)
                    if has(-1):
                        layer_out(g - 1, q, 0)
                        norm_row(L, dve, g - 1, q, 0, 2)
                        layer_out(g - 1, q, 1)
                        norm_row(L, dve, g - 1, q, 1, 2)
                        norm_row(L, dve, g - 1, q, 2, 2)
                    if has(1):
                        operator_low(g + 1, q)
                    if has(-1):
                        norm_row(L, dve, g - 1, q, 3, 2)
                        norm_variance(L, dve, g - 1, q, 0.25 * EPS)
                    if has(1):
                        mixed_low(g + 1, q, 0)
                        mixed_low(g + 1, q, 1)
                over_groups(dve, step, 1, 2)

            @block.gpsimd
            def _(pool):
                def hidden_power(g):
                    pool.wait_ge(zvar_ok, upto(g, 3, 3))
                    if reused(g, 1):
                        pool.wait_ge(zn_ok, upto(g - 1, GP, GP))
                    pool.tensor_tensor(zrs[:], zvar[:], K.minus_half[:], ALU.pow).then_inc(zrs_ok, 1)

                def z_low(g, j):
                    pool.wait_ge(z_hi, upto(g, GP, j + 1))
                    if reused(g, 1):
                        pool.wait_ge(y_ps, upto(g - 1, 2, 2))
                    pool.tensor_tensor(zs[1][:, j, :], zn[:, j, :], zs[0][:, j, :], ALU.subtract).then_inc(z_lo, 1)

                def sum_squares(g, h):
                    pool.wait_ge(h_sq, upto(g, HT, h + 1))
                    if h > 1:
                        pool.wait_ge(hqs_ok, upto(g, 3, h - 1))
                    elif reused(g, 1):
                        pool.wait_ge(z_ps, upto(g - 1, GP, GP))
                    pool.tensor_tensor((hqs if h == HT - 1 else hqp[:, h - 1, :])[:],
                                       (hq[:, 0, :] if h == 1 else hqp[:, h - 2, :])[:],
                                       hq[:, h, :], ALU.add).then_inc(hqs_ok, 1)

                def x_low(g, p):
                    pool.wait_ge(x_hi, upto(g, 1, 1))
                    if reused(g):
                        pool.wait_ge(px_ps, upto(g - 2, 2, 2))
                    pool.tensor_tensor(xs[p][1][:], K.x[:, xcols(g)].rearrange("p (g d) -> p g d", g=GP),
                                       xs[p][0][:], ALU.subtract).then_inc(x_lo, 1)

                def step(g, p, has):
                    q = 1 - p
                    if has(-1):
                        norm_power(K, L, pool, g - 1, q)
                    if has(0):
                        hidden_power(g)
                        z_low(g, 0)
                        z_low(g, 1)
                        z_low(g, 2)
                    if has(1):
                        sum_squares(g + 1, 1)
                    if has(0):
                        z_low(g, 3)
                    if has(1):
                        sum_squares(g + 1, 2)
                    if has(2):
                        x_low(g + 2, p)
                    if has(1):
                        sum_squares(g + 1, 3)
                over_groups(pool, step, 2, 1)


def norm(nc, ctx, tag, deep=2, tiles=None):
    L = Parts()
    L.deep = deep
    tiles = tiles or ctx

    def sb(name, shape):
        made = [tiles.enter_context(nc.sbuf_tensor(f"{tag}_{name}{i}", shape, F32)) for i in range(deep)]
        return [made[p % deep] for p in range(2)]

    L.pre, L.st = sb("pre", [128, GP, D]), sb("st", [128, GP, 6])
    L.msum, L.veps, L.rstd, L.nmr = (sb(name, [128, GP]) for name in ("msum", "veps", "rstd", "nmr"))
    L.mdiff, L.m2, L.dd = (tiles.enter_context(nc.sbuf_tensor(f"{tag}_{name}", [128, GP], F32))
                           for name in ("mdiff", "m2", "dd"))
    L.pre_ok, L.st_ok, L.agg, L.rstd_ok, L.nmr_ok, L.x_new = (
        ctx.enter_context(nc.semaphore(f"{tag}_{name}"))
        for name in ("pre_ok", "st_ok", "agg", "rstd_ok", "nmr_ok", "x_new"))
    return L


def pre_free(L, dve, g):
    if reused(g, L.deep):
        dve.wait_ge(L.x_new, upto(g - L.deep, GP, GP))


def norm_row(L, dve, g, p, j, per=GP):
    if j % (GP // per) == 0:
        dve.wait_ge(L.pre_ok, upto(g, per, j // (GP // per) + 1))
    dve.bn_stats(L.st[p][:, j, :], L.pre[p][:, j, :]).then_inc(L.st_ok, 1)


def norm_variance(L, dve, g, p, eps):
    dve.wait_ge(L.st_ok, upto(g, GP, GP))
    st = L.st[p]
    dve.tensor_tensor(L.msum[p][:], st[:, :, 1], st[:, :, 4], ALU.add).then_inc(L.agg, 1)
    dve.tensor_tensor(L.mdiff[:], st[:, :, 1], st[:, :, 4], ALU.subtract).then_inc(L.agg, 1)
    dve.scalar_tensor_tensor(L.m2[:], st[:, :, 2], eps * D, st[:, :, 5], ALU.add, ALU.add).then_inc(L.agg, 1)
    dve.wait_ge(L.agg, upto(g, 5, 2))
    dve.scalar_tensor_tensor(L.dd[:], L.mdiff[:], 0.25, L.mdiff[:], ALU.mult, ALU.mult).then_inc(L.agg, 1)
    dve.wait_ge(L.agg, upto(g, 5, 4))
    if reused(g, L.deep):
        dve.wait_ge(L.rstd_ok, upto(g - L.deep, 1, 1))
    dve.scalar_tensor_tensor(L.veps[p][:], L.m2[:], 1.0 / D, L.dd[:], ALU.mult, ALU.add).then_inc(L.agg, 1)


def norm_power(K, L, pool, g, p):
    pool.wait_ge(L.agg, upto(g, 5, 5))
    if reused(g, L.deep):
        pool.wait_ge(L.x_new, upto(g - L.deep, GP, GP))
    pool.tensor_tensor(L.rstd[p][:], L.veps[p][:], K.minus_half[:], ALU.pow).then_inc(L.rstd_ok, 1)


def norm_shift(L, dve, g, p):
    dve.wait_ge(L.rstd_ok, upto(g, 1, 1))
    if reused(g, L.deep):
        dve.wait_ge(L.x_new, upto(g - L.deep, GP, GP))
    dve.scalar_tensor_tensor(L.nmr[p][:], L.msum[p][:], -0.5, L.rstd[p][:], ALU.mult,
                             ALU.mult).then_inc(L.nmr_ok, 1)


def norm_apply(K, L, act, g, p, j):
    if j == 0:
        act.wait_ge(L.nmr_ok, upto(g, 1, 1))
    act.activation(K.x[:, gcols(g, j)], L.pre[p][:, j, :], ACT.Identity,
                   bias=L.nmr[p][:, j:j + 1], scale=L.rstd[p][:, j:j + 1]).then_inc(L.x_new, 1)


def front(nc, ctx):
    F = Parts()
    F.x_hi, F.x_lo, F.xT_ps, F.xT_sb = (ctx.enter_context(nc.semaphore(f"next_{name}"))
                                        for name in ("x_hi", "x_lo", "xT_ps", "xT_sb"))
    F.xs = [[ctx.enter_context(nc.sbuf_tensor(f"x{p}_{s}_next", [128, GP, D], F16)) for s in ("hi", "lo")]
            for p in range(2)]
    F.xT = [[ctx.enter_context(nc.sbuf_tensor(f"xT{p}_{s}", [128, DT, C], F16)) for s in ("hi", "lo")]
            for p in range(2)]
    return F


def front_of(shared, layer):
    F = Parts()
    F.x_hi, F.x_lo, F.xT_ps, F.xT_sb, F.xs, F.xT = (shared.x_hi, shared.x_lo, shared.xT_ps, shared.xT_sb,
                                                    shared.xs, shared.xT)
    F.base = (layer - 1) * G
    F.made = (2, 1) if layer > 1 else (0, 0)
    F.ahead = (2, 1) if layer < 3 else (0, 0)
    return F


def halves_due(F, g):
    return not isinstance(g, int) or F.made[0] <= g < G + F.ahead[0]


def transpose_due(F, g):
    return not isinstance(g, int) or F.made[1] <= g < G + F.ahead[1]


def x_group(K, g):
    return K.x[:, xcols(g - G if isinstance(g, int) and g >= G else g)].rearrange("p (g d) -> p g d", g=GP)


def x_high(K, F, L, act, g, p):
    if isinstance(g, int) and g >= G:
        act.wait_ge(L.x_new, upto(g - G, GP, GP))
    if reused(F.base + g):
        act.wait_ge(F.xT_ps, upto(F.base + g - 2, 2, 2))
    act.activation(F.xs[p][0][:], x_group(K, g), ACT.Copy).then_inc(F.x_hi, 1)


def x_low(K, F, pool, g, p):
    pool.wait_ge(F.x_hi, upto(F.base + g, 1, 1))
    if reused(F.base + g):
        pool.wait_ge(F.xT_ps, upto(F.base + g - 2, 2, 2))
    pool.tensor_tensor(F.xs[p][1][:], x_group(K, g), F.xs[p][0][:], ALU.subtract).then_inc(F.x_lo, 1)


def transpose_x(K, F, pe, g, p, banks, s):
    pe.wait_ge((F.x_hi, F.x_lo)[s], upto(F.base + g, 1, 1))
    if reused(F.base + g, 1):
        pe.wait_ge(F.xT_sb, upto(F.base + g - 1, 2, s + 1))
    o = banks[s][:].bitcast(F16)
    for d in range(DT):
        for j in range(GP):
            m = pe.transpose(o[:, d * C + j * N:d * C + (j + 1) * N],
                             F.xs[p][s][:, j, d * 128:(d + 1) * 128], K.ident16[:])
    m.then_inc(F.xT_ps, 1)


def copy_xT(K, F, dve, g, p, banks, s, readers):
    dve.wait_ge(F.xT_ps, upto(F.base + g, 2, s + 1))
    if reused(g):
        dve.wait_ge(readers[0], upto(g - 2, readers[1], readers[1]))
    dve.tensor_copy(F.xT[p][s][:].rearrange("p d c -> p (d c)"), banks[s][:].bitcast(F16)).then_inc(F.xT_sb, 1)


def layer1(nc, K, ctx, tiles):
    def sb(name, shape, dt=F32):
        return tiles.enter_context(nc.sbuf_tensor(f"l1_{name}", shape, dt))

    def sem(name):
        return ctx.enter_context(nc.semaphore(f"l1_{name}"))

    bank = K.bank
    b_xT, b_qkv, b_ak, b_sm = bank[0:2], bank[2:6], bank[6], bank[7]
    L = norm(nc, ctx, "l1", tiles=tiles)
    qkv = [sb(f"qkv{p}", [128, GP, 2 * QK + D]) for p in range(2)]
    ks = [sb("k_hi", [128, GP, QK + 1], F16), sb("k_lo", [128, GP, QK + 1], F16)]
    ats = [[sb(f"adjT{p}_{s}", [128, C], F16) for s in ("hi", "lo")] for p in range(2)]
    qa, w = sb("qa", [128, GP, QK]), sb("w", [128, GP])
    wmax, wneg, wexp, wsum = sb("wmax", [GP, 1]), sb("wneg", [GP, 1]), sb("wexp", [GP, N]), sb("wsum", [GP, 1])
    wsc, wrec, wn, wgt = sb("wsc", [GP, 1]), sb("wrec", [GP, 1]), sb("wn", [GP, N]), sb("wgt", [128, GP])
    qkv_ps, qkv_sb, k_hi, k_lo, a_hi, a_lo, k_one, ak_ps = map(
        sem, ("qkv_ps", "qkv_sb", "k_hi", "k_lo", "a_hi", "a_lo", "k_one", "ak_ps"))
    qa_ok, w_ok, asum_ok, wT_ps, wmax_ok, wneg_ok, wexp_ok, wrec_ok, wn_ok, wB_ps, wgt_ok = map(
        sem, ("qa_ok", "w_ok", "asum_ok", "wT_ps", "wmax_ok", "wneg_ok", "wexp_ok", "wrec_ok", "wn_ok",
              "wB_ps", "wgt_ok"))
    SC = 1.0 / (W_SCALE * W_SCALE * QK ** 0.5)
    F = front_of(K.F, 1)
    K.qkv_sb, K.asum_ok, K.qa_ok, K.wgt_ok = qkv_sb, asum_ok, qa_ok, wgt_ok
    K.x_new[1], K.scores_after[2] = L.x_new, [(qkv_sb, G * GP)]

    def sync(sp):
        for g in range(2):
            load_adj(K, sp, g, g)

    def tensor(pe):
        def project(g, p, j):
            if j == 0:
                pe.wait_ge(F.xT_sb, upto(F.base + g, 2, 2))
            if reused(g, 1):
                pe.wait_ge(qkv_sb, upto(g - 1, GP, j + 1))
            c = slice(j * N, (j + 1) * N)
            for d in range(DT):
                m = triple(nc, b_qkv[j][:, 0:2 * QK + D], [s[:, d, c] for s in F.xT[p]],
                           [w[:, d, :] for w in K.qkv], start=d == 0, stop=d == DT - 1)
            m.then_inc(qkv_ps, 1)

        def aggregate(g, p):
            for s in (k_hi, k_lo, a_hi, a_lo):
                pe.wait_ge(s, upto(g, 1, 1))
            if isinstance(g, int) and g == 0:
                pe.wait_ge(k_one, 2)
            if reused(g, 1):
                pe.wait_ge(asum_ok, upto(g - 1, 1, 1))
                pe.wait_ge(qa_ok, upto(g - 1, 1, 1))
            for j in range(GP):
                m = triple(nc, b_ak[:, j * (QK + 1):(j + 1) * (QK + 1)],
                           [s[:, j * N:(j + 1) * N] for s in ats[p]], [s[:, j, :] for s in ks])
            m.then_inc(ak_ps, 1)

        def score_rows(g):
            pe.wait_ge(w_ok, upto(g, 1, 1))
            if reused(g, 1):
                pe.wait_ge(wgt_ok, upto(g - 1, 1, 1))
            pe.transpose(b_sm[0:GP, 0:N], w[:], K.ident[:]).then_inc(wT_ps, 1)

        def weight_columns(g):
            pe.wait_ge(wn_ok, upto(g, 1, 1))
            pe.matmul(b_sm[:, N:N + GP], wn[:], K.ident[0:GP, 0:GP], start=True,
                      stop=True).then_inc(wB_ps, 1)

        def step(g, p, has):
            q = 1 - p
            if transpose_due(F, g + 2):
                transpose_x(K, F, pe, g + 2, p, b_xT, 0)
            if has(1):
                project(g + 1, q, 0)
            if transpose_due(F, g + 2):
                transpose_x(K, F, pe, g + 2, p, b_xT, 1)
            if has(-1):
                weight_columns(g - 1)
            if has(0):
                aggregate(g, p)
            if has(1):
                project(g + 1, q, 1)
                project(g + 1, q, 2)
            if has(0):
                score_rows(g)
            if has(1):
                project(g + 1, q, 3)
        return step, 2, 1

    def scalar(act):
        def adj_high(g, p):
            if reused(g):
                act.wait_ge(ak_ps, upto(g - 2, 1, 1))
            act.activation(ats[p][0][:], K.at[:, acols(g)], ACT.Copy).then_inc(a_hi, 1)

        def copy_qkv(g, p, j):
            act.wait_ge(qkv_ps, upto(g, GP, j + 1))
            if reused(g):
                act.wait_ge(L.pre_ok, upto(g - 2, GP, j + 1))
            act.activation(qkv[p][:, j, :], b_qkv[j][:, 0:2 * QK + D], ACT.Copy).then_inc(qkv_sb, 1)

        def key_high(g, p):
            act.wait_ge(qkv_sb, upto(g, GP, GP))
            if reused(g, 1):
                act.wait_ge(ak_ps, upto(g - 1, 1, 1))
            act.activation(ks[0][:, :, 0:QK], qkv[p][:, :, QK:2 * QK], ACT.Copy).then_inc(k_hi, 1)

        def exponentials(g):
            act.wait_ge(wneg_ok, upto(g, 1, 1))
            if reused(g, 1):
                act.wait_ge(wn_ok, upto(g - 1, 1, 1))
            act.activation(wexp[:], b_sm[0:GP, 0:N], ACT.Exp, bias=wneg[:], scale=SC,
                           accum_out=wsum[:]).then_inc(wexp_ok, 1)

        def step(g, p, has):
            q = 1 - p
            if halves_due(F, g + 2):
                x_high(K, F, L, act, g + 2, p)
            if has(0):
                copy_qkv(g, p, 0)
                copy_qkv(g, p, 1)
                copy_qkv(g, p, 2)
                copy_qkv(g, p, 3)
                key_high(g, p)
            if has(-1):
                exponentials(g - 1)
            if has(1):
                adj_high(g + 1, q)
            if has(-2):
                norm_apply(K, L, act, g - 2, p, 0)
                norm_apply(K, L, act, g - 2, p, 1)
                norm_apply(K, L, act, g - 2, p, 2)
                norm_apply(K, L, act, g - 2, p, 3)
        return step, 2, 2

    def vector(dve):
        def weights(g):
            dve.wait_ge(wB_ps, upto(g, 1, 1))
            if reused(g, 1):
                dve.wait_ge(L.pre_ok, upto(g - 1, GP, GP))
            dve.tensor_copy(wgt[:], b_sm[:, N:N + GP]).then_inc(wgt_ok, 1)

        def residual(g, p, j):
            if j == 0:
                dve.wait_ge(wgt_ok, upto(g, 1, 1))
                pre_free(L, dve, g)
            dve.scalar_tensor_tensor(L.pre[p][:, j, :], qkv[p][:, j, 2 * QK:], wgt[:, j:j + 1],
                                     K.x[:, gcols(g, j)], ALU.mult, ALU.add).then_inc(L.pre_ok, 1)

        def scores(g, p):
            dve.wait_ge(ak_ps, upto(g, 1, 1))
            ak = b_ak[:, 0:GP * (QK + 1)].rearrange("p (g k) -> p g k", g=GP)
            if reused(g, 1):
                dve.wait_ge(w_ok, upto(g - 1, 1, 1))
            dve.tensor_tensor(qa[:], ak[:, :, 0:QK], qkv[p][:, :, 0:QK], ALU.mult).then_inc(qa_ok, 1)
            dve.tensor_scalar(K.asum[:, bass.ds(g * GP, GP)], ak[:, :, QK], 1.0, None,
                              ALU.mult).then_inc(asum_ok, 1)
            dve.wait_ge(qa_ok, upto(g, 1, 1))
            if reused(g, 1):
                dve.wait_ge(wT_ps, upto(g - 1, 1, 1))
            dve.tensor_reduce(w[:], qa[:], AX.X, ALU.add).then_inc(w_ok, 1)

        def maximum(g):
            dve.wait_ge(wT_ps, upto(g, 1, 1))
            dve.tensor_reduce(wmax[:], b_sm[0:GP, 0:N], AX.X, ALU.max).then_inc(wmax_ok, 1)
            dve.wait_ge(wmax_ok, upto(g, 1, 1))
            if reused(g, 1):
                dve.wait_ge(wexp_ok, upto(g - 1, 1, 1))
            dve.tensor_scalar(wneg[:], wmax[:], -SC, None, ALU.mult).then_inc(wneg_ok, 1)

        def softmax(g):
            dve.wait_ge(wexp_ok, upto(g, 1, 1))
            dve.tensor_scalar(wsc[:], wsum[:], W_SCALE, None, ALU.mult).then_inc(wrec_ok, 1)
            dve.wait_ge(wrec_ok, upto(g, 2, 1))
            dve.reciprocal(wrec[:], wsc[:]).then_inc(wrec_ok, 1)
            dve.wait_ge(wrec_ok, upto(g, 2, 2))
            if reused(g, 1):
                dve.wait_ge(wB_ps, upto(g - 1, 1, 1))
            dve.tensor_scalar(wn[:], wexp[:], wrec[:], None, ALU.mult).then_inc(wn_ok, 1)

        dve.memset(ks[0][:, :, QK:QK + 1], 1.0).then_inc(k_one, 1)
        dve.memset(ks[1][:, :, QK:QK + 1], 0.0).then_inc(k_one, 1)

        def step(g, p, has):
            q = 1 - p
            if has(-1):
                scores(g - 1, q)
            if has(-2):
                residual(g - 2, p, 2)
                norm_row(L, dve, g - 2, p, 0)
            if has(-1):
                maximum(g - 1)
            if has(-2):
                residual(g - 2, p, 3)
                norm_row(L, dve, g - 2, p, 1)
                norm_row(L, dve, g - 2, p, 2)
            if transpose_due(F, g + 2):
                copy_xT(K, F, dve, g + 2, p, b_xT, 0, (qkv_ps, GP))
            if has(-2):
                norm_row(L, dve, g - 2, p, 3)
                norm_variance(L, dve, g - 2, p, EPS)
            if has(-1):
                softmax(g - 1)
            if transpose_due(F, g + 2):
                copy_xT(K, F, dve, g + 2, p, b_xT, 1, (qkv_ps, GP))
            if has(-1):
                weights(g - 1)
            if has(-2):
                norm_shift(L, dve, g - 2, p)
            if has(-1):
                residual(g - 1, q, 0)
                residual(g - 1, q, 1)
        return step, 2, 2

    def gpsimd(pool):
        def adj_low(g, p):
            pool.wait_ge(a_hi, upto(g, 1, 1))
            if reused(g):
                pool.wait_ge(ak_ps, upto(g - 2, 1, 1))
            pool.tensor_tensor(ats[p][1][:], K.at[:, acols(g)], ats[p][0][:], ALU.subtract).then_inc(a_lo, 1)

        def key_low(g, p):
            pool.wait_ge(k_hi, upto(g, 1, 1))
            if reused(g, 1):
                pool.wait_ge(ak_ps, upto(g - 1, 1, 1))
            pool.tensor_tensor(ks[1][:, :, 0:QK], qkv[p][:, :, QK:2 * QK], ks[0][:, :, 0:QK],
                               ALU.subtract).then_inc(k_lo, 1)

        def step(g, p, has):
            if has(0):
                adj_low(g, p)
            if halves_due(F, g + 2):
                x_low(K, F, pool, g + 2, p)
            if has(0):
                key_low(g, p)
            if has(-2):
                norm_power(K, L, pool, g - 2, p)
        return step, 2, 2

    return sync, tensor, scalar, vector, gpsimd


def attention_front(nc, K, ctx, layer, width):
    S = Parts()
    S.s_ps, S.s_hi, S.s_lo, S.s_bias, S.sj_ps, S.t_ok, S.e_ok, S.u_ok = (
        ctx.enter_context(nc.semaphore(f"l{layer}_{name}"))
        for name in ("s_ps", "s_hi", "s_lo", "s_bias", "sj_ps", "t_ok", "e_ok", "u_ok"))
    S.s = [ctx.enter_context(nc.sbuf_tensor(f"l{layer}_s_{s}", [128, GP], F16)) for s in ("hi", "lo")]
    S.bias = ctx.enter_context(nc.sbuf_tensor(f"l{layer}_bias", [128, GP], F32))
    S.t = ctx.enter_context(nc.sbuf_tensor(f"l{layer}_t", [128, C], F32))
    S.lr = ctx.enter_context(nc.sbuf_tensor(f"l{layer}_lr", [128, C], F32))
    S.e = ctx.enter_context(nc.sbuf_tensor(f"l{layer}_e", [128, C], F32))
    S.u = ctx.enter_context(nc.sbuf_tensor(f"l{layer}_u", [128, C], F32))
    S.width, S.layer = width, layer
    return S


def node_scores(nc, K, F, S, pe, g, p, b, weights, column):
    if is_first(g):
        for done, count in K.scores_after[S.layer]:
            pe.wait_ge(done, count)
    pe.wait_ge(F.xT_sb, upto(F.base + g, 2, 2))
    if reused(g, 1):
        pe.wait_ge(S.s_lo, upto(g - 1, 1, 1))
        pe.wait_ge(S.s_bias, upto(g - 1, 1, 1))
    for j in range(GP):
        for d in range(DT):
            m = triple(nc, b[:, j * S.width:(j + 1) * S.width], [s[:, d, j * N:(j + 1) * N] for s in F.xT[p]],
                       [w[:, d, column:column + S.width] for w in weights], start=d == 0, stop=d == DT - 1)
    m.then_inc(S.s_ps, 1)


def split_scores(S, dve, g, b):
    dve.wait_ge(S.s_ps, upto(g, 1, 1))
    if reused(g, 1):
        dve.wait_ge(S.sj_ps, upto(g - 1, 1, 1))
    sj = b[:, 0:GP * S.width].rearrange("p (g s) -> p g s", g=GP)[:, :, 0]
    dve.tensor_copy(S.s[0][:], sj).then_inc(S.s_hi, 1)
    dve.wait_ge(S.s_hi, upto(g, 1, 1))
    dve.tensor_tensor(S.s[1][:], sj, S.s[0][:], ALU.subtract).then_inc(S.s_lo, 1)


def spread_scores(nc, K, S, pe, g, b, free, per):
    pe.wait_ge(S.s_lo, upto(g, 1, 1))
    if reused(g, 1):
        pe.wait_ge(free, upto(g - 1, per, per))
    for j in range(GP):
        for s in (1, 0):
            m = pe.matmul(b[:, j * N:(j + 1) * N], S.s[s][:, j:j + 1].to_broadcast([128, 128]),
                          K.ident16[:], start=s == 1, stop=s == 0)
    m.then_inc(S.sj_ps, 1)


def layer2(nc, K, ctx):
    def sb(name, shape, dt=F32):
        return ctx.enter_context(nc.sbuf_tensor(f"l2_{name}", shape, dt))

    def sem(name):
        return ctx.enter_context(nc.semaphore(f"l2_{name}"))

    bank = K.bank
    b_xT, b_far, b_near, b_s, b_t = bank[0:2], bank[4], bank[5:8], bank[2], bank[3]
    L, S = norm(nc, ctx, "l2"), attention_front(nc, K, ctx, 2, 2)
    adjn, adj_in = K.adjn, K.adj_in
    before_l2 = 8 * G
    rsum, reps, rinv = sb("rsum", [128, GP]), sb("reps", [128, GP]), sb("rinv", [128, GP])
    tf = sb("tf", [128, C])
    ts = [sb("T_hi", [128, C], F16), sb("T_lo", [128, C], F16)]
    tT = [sb(f"TT{p}", [128, 2, C], F16) for p in range(2)]
    far = [[sb(f"far{j}_{s}", [128, D], F16) for s in ("hi", "lo")] for j in range(GP)]
    mid = [[sb(f"mid{j}_{s}", [128, D], F16) for s in ("hi", "lo")] for j in range(GP)]
    hr = sb("hr", [128, GP, D])
    rsum_ok, reps_ok, rinv_ok, tf_ok, t_hi, t_lo, tT_ps, tT_sb = map(
        sem, ("rsum_ok", "reps_ok", "rinv_ok", "tf_ok", "t_hi", "t_lo", "tT_ps", "tT_sb"))
    far_ps, far_hi, far_lo, near_ps, mid_ps, mid_hi, mid_lo, out_ps, hr_ok = map(
        sem, ("far_ps", "far_hi", "far_lo", "near_ps", "mid_ps", "mid_hi", "mid_lo", "out_ps", "hr_ok"))
    lr_ok = sem("lr_ok")
    before = (0, -2, -1, 1)
    F = front_of(K.F, 2)
    K.far_lo, K.hr_ok, K.x_new[2] = far_lo, hr_ok, L.x_new
    K.scores_after[3] = [(S.s_lo, G), (S.s_bias, G), (tT_sb, G)]

    def sync(sp):
        def load(g, p, has):
            if has(0) and reused(g):
                sp.wait_ge(S.u_ok, upto(g - 2, 1, 1))
                load_adj(K, sp, g, p)
        over_groups(sp, load, 0, 0)

    def tensor(pe):
        def project_far(g, p, j):
            if j == 0:
                pe.wait_ge(F.xT_sb, upto(F.base + g, 2, 2))
            if j == 0 and is_first(g):
                pe.wait_ge(K.qkv_sb, G * GP)
            if j >= 1 or reused(g, 1):
                pe.wait_ge(far_lo, upto(g, GP, j))
            c = slice(j * N, (j + 1) * N)
            for d in range(DT):
                m = triple(nc, b_far[:, 0:D], [s[:, d, c] for s in F.xT[p]],
                           [w[:, d, 0:D] for w in K.wk], start=d == 0, stop=d == DT - 1)
            m.then_inc(far_ps, 1)

        def project_near(g, p, j, n):
            if j == 0:
                pe.wait_ge(F.xT_sb, upto(F.base + g, 2, 2))
            if j == 1 and is_first(g):
                pe.wait_ge(K.asum_ok, G)
                pe.wait_ge(K.qa_ok, G)
            if j == 2 and is_first(g):
                pe.wait_ge(K.wgt_ok, G)
            c = slice(j * N, (j + 1) * N)
            if j == 3 or reused(g, 1):
                pe.wait_ge(hr_ok, upto(g, GP, before[j]))
            for d in range(DT):
                m = triple(nc, b_near[n][:], [s[:, d, c] for s in F.xT[p]],
                           [w[:, d, D + 2:3 * D + 2] for w in K.wk], start=d == 0, stop=d == DT - 1)
            m.then_inc(near_ps, 1)

        def walk_far(g, p, j, n):
            pe.wait_ge(tT_sb, upto(g, 1, 1))
            pe.wait_ge(far_hi, upto(g, GP, j + 1))
            pe.wait_ge(far_lo, upto(g, GP, j + 1))
            triple(nc, b_near[n][:, 0:D], [tT[p][:, s, j * N:(j + 1) * N] for s in range(2)],
                   [s[:] for s in far[j]], start=False, skip_group_check=True).then_inc(mid_ps, 1)

        def walk_mid(g, p, j, n):
            pe.wait_ge(mid_hi, upto(g, GP, j + 1))
            pe.wait_ge(mid_lo, upto(g, GP, j + 1))
            o = b_near[n][:, D:2 * D]
            pe.matmul(o, K.ones16[:], K.bkrow[:], start=False, stop=False, skip_group_check=True)
            triple(nc, o, [tT[p][:, s, j * N:(j + 1) * N] for s in range(2)], [s[:] for s in mid[j]],
                   start=False, skip_group_check=True).then_inc(out_ps, 1)

        def transpose_T(g):
            pe.wait_ge(t_hi, upto(g, 1, 1))
            pe.wait_ge(t_lo, upto(g, 1, 1))
            pe.wait_ge(S.t_ok, upto(g, GP, GP))
            o = b_t[:].bitcast(F16)
            for s in range(2):
                for j in range(GP):
                    m = pe.transpose(o[:, s * C + j * N:s * C + (j + 1) * N],
                                     ts[s][:, j * N:(j + 1) * N], K.ident16[:])
            m.then_inc(tT_ps, 1)

        def step(g, p, has):
            q = 1 - p
            if has(-1):
                walk_far(g - 1, q, 0, 0)
                project_far(g - 1, q, 2)
                project_near(g - 1, q, 2, 2)
                walk_far(g - 1, q, 1, 1)
                walk_far(g - 1, q, 2, 2)
                walk_mid(g - 1, q, 0, 0)
                walk_mid(g - 1, q, 1, 1)
                project_far(g - 1, q, 3)
                project_near(g - 1, q, 3, 0)
                walk_mid(g - 1, q, 2, 2)
                walk_far(g - 1, q, 3, 0)
            if has(0):
                transpose_T(g)
            if transpose_due(F, g + 1):
                transpose_x(K, F, pe, g + 1, q, b_xT, 0)
            if has(-1):
                walk_mid(g - 1, q, 3, 0)
            if transpose_due(F, g + 1):
                transpose_x(K, F, pe, g + 1, q, b_xT, 1)
            if has(0):
                project_far(g, p, 0)
                project_near(g, p, 0, 0)
            if has(1):
                node_scores(nc, K, F, S, pe, g + 1, q, b_s, K.wk, D)
            if has(0):
                project_far(g, p, 1)
            if has(1):
                spread_scores(nc, K, S, pe, g + 1, b_t, tT_sb, 1)
            if has(0):
                project_near(g, p, 1, 1)
        return step, 1, 1

    def scalar(act):
        def logits(g, j):
            if j == 0:
                act.wait_ge(S.sj_ps, upto(g, 1, 1))
                act.wait_ge(S.s_bias, upto(g, 1, 1))
                if reused(g, 1):
                    act.wait_ge(lr_ok, upto(g - 1, 1, 1))
            act.activation(S.t[:, j * N:(j + 1) * N], b_t[:, j * N:(j + 1) * N], ACT.Identity,
                           bias=S.bias[:, j:j + 1], scale=1.0 / WK_SCALE).then_inc(S.t_ok, 1)

        def far_high(g, j):
            act.wait_ge(far_ps, upto(g, GP, j + 1))
            if reused(g, 1):
                act.wait_ge(mid_ps, upto(g - 1, GP, j + 1))
            act.activation(far[j][0][:], b_far[:, 0:D], ACT.Copy).then_inc(far_hi, 1)

        def mid_high(g, j, n):
            act.wait_ge(mid_ps, upto(g, GP, j + 1))
            if reused(g, 1):
                act.wait_ge(out_ps, upto(g - 1, GP, j + 1))
            act.activation(mid[j][0][:], b_near[n][:, 0:D], ACT.Copy).then_inc(mid_hi, 1)

        def relu(g, j, n):
            act.wait_ge(out_ps, upto(g, GP, j + 1))
            if reused(g, 1):
                act.wait_ge(L.pre_ok, upto(g - 1, GP, j + 1))
            act.activation(hr[:, j, :], b_near[n][:, D:2 * D], ACT.Relu,
                           scale=1.0 / WK_SCALE).then_inc(hr_ok, 1)

        def exponentials(g):
            act.wait_ge(lr_ok, upto(g, 1, 1))
            if reused(g, 1):
                act.wait_ge(S.u_ok, upto(g - 1, 1, 1))
            act.activation(S.e[:], S.lr[:], ACT.Exp).then_inc(S.e_ok, 1)

        def transition_high(g):
            act.wait_ge(tf_ok, upto(g, 1, 1))
            if reused(g, 1):
                act.wait_ge(tT_ps, upto(g - 1, 1, 1))
            act.activation(ts[0][:], tf[:], ACT.Copy).then_inc(t_hi, 1)

        def step(g, p, has):
            q = 1 - p
            if has(-1):
                mid_high(g - 1, 3, 0)
                relu(g - 1, 2, 2)
                relu(g - 1, 3, 0)
            if halves_due(F, g + 2):
                x_high(K, F, L, act, g + 2, p)
            if has(0):
                far_high(g, 0)
            if has(-2):
                norm_apply(K, L, act, g - 2, p, 3)
            if has(0):
                far_high(g, 1)
            if has(1):
                logits(g + 1, 0)
                logits(g + 1, 1)
                logits(g + 1, 2)
                logits(g + 1, 3)
            if has(0):
                mid_high(g, 0, 0)
                far_high(g, 2)
            if has(1):
                exponentials(g + 1)
            if has(0):
                mid_high(g, 1, 1)
            if has(-1):
                norm_apply(K, L, act, g - 1, q, 0)
            if has(0):
                mid_high(g, 2, 2)
            if has(-1):
                norm_apply(K, L, act, g - 1, q, 1)
            if has(0):
                relu(g, 0, 0)
            if has(-1):
                norm_apply(K, L, act, g - 1, q, 2)
            if has(0):
                relu(g, 1, 1)
                far_high(g, 3)
            if has(1):
                transition_high(g + 1)
        return step, 2, 2

    def vector(dve):
        def far_low(g, j):
            dve.wait_ge(far_hi, upto(g, GP, j + 1))
            if reused(g, 1):
                dve.wait_ge(mid_ps, upto(g - 1, GP, j + 1))
            dve.tensor_tensor(far[j][1][:], b_far[:, 0:D], far[j][0][:], ALU.subtract).then_inc(far_lo, 1)

        def mid_low(g, j, n):
            dve.wait_ge(mid_hi, upto(g, GP, j + 1))
            if reused(g, 1):
                dve.wait_ge(out_ps, upto(g - 1, GP, j + 1))
            dve.tensor_tensor(mid[j][1][:], b_near[n][:, 0:D], mid[j][0][:],
                              ALU.subtract).then_inc(mid_lo, 1)

        def residual(g, p, j):
            if j == 0 and is_first(g):
                dve.wait_ge(K.x_new[1], G * GP)
            dve.wait_ge(hr_ok, upto(g, GP, j + 1))
            pre_free(L, dve, g)
            dve.tensor_tensor(L.pre[p][:, j, :], hr[:, j, :], K.x[:, gcols(g, j)],
                              ALU.add).then_inc(L.pre_ok, 1)

        def scores(g):
            split_scores(S, dve, g, b_s)
            if reused(g, 1):
                dve.wait_ge(S.t_ok, upto(g - 1, GP, GP))
            si = b_s[:, 0:2 * GP].rearrange("p (g s) -> p g s", g=GP)[:, :, 1]
            dve.tensor_scalar(S.bias[:], si, 1.0 / WK_SCALE, K.edge_bias[:], ALU.mult,
                              ALU.add).then_inc(S.s_bias, 1)

        def leaky(g):
            dve.wait_ge(S.t_ok, upto(g, GP, GP))
            if reused(g, 1):
                dve.wait_ge(S.e_ok, upto(g - 1, 1, 1))
            dve.scalar_tensor_tensor(S.lr[:], S.t[:], 0.2, S.t[:], ALU.mult, ALU.max).then_inc(lr_ok, 1)

        def transition(g, p):
            dve.wait_ge(S.e_ok, upto(g, 1, 1))
            dve.wait_ge(adj_in[p], before_l2 + 8 * (g - p) + 16)
            if reused(g, 1):
                dve.wait_ge(tf_ok, upto(g - 1, 1, 1))
            dve.tensor_tensor(S.u[:], S.e[:], adjn[p][:].rearrange("p g n -> p (g n)"),
                              ALU.mult).then_inc(S.u_ok, 1)

        def row_sums(g):
            dve.wait_ge(S.u_ok, upto(g, 1, 1))
            u = S.u[:].rearrange("p (g n) -> p g n", g=GP)
            dve.tensor_reduce(rsum[:], u, AX.X, ALU.add).then_inc(rsum_ok, 1)
            dve.wait_ge(rsum_ok, upto(g, 1, 1))
            dve.tensor_scalar(reps[:], rsum[:], 1e-12, None, ALU.add).then_inc(reps_ok, 1)
            dve.wait_ge(reps_ok, upto(g, 1, 1))
            dve.reciprocal(rinv[:], reps[:]).then_inc(rinv_ok, 1)

        def normalised(g):
            u = S.u[:].rearrange("p (g n) -> p g n", g=GP)
            dve.wait_ge(rinv_ok, upto(g, 1, 1))
            if reused(g, 1):
                dve.wait_ge(t_hi, upto(g - 1, 1, 1))
                dve.wait_ge(t_lo, upto(g - 1, 1, 1))
            dve.tensor_tensor(tf[:].rearrange("p (g n) -> p g n", g=GP), u,
                              rinv[:, :, None].to_broadcast([128, GP, N]), ALU.mult).then_inc(tf_ok, 1)

        def copy_tT(g, p):
            dve.wait_ge(tT_ps, upto(g, 1, 1))
            if reused(g):
                dve.wait_ge(out_ps, upto(g - 2, GP, GP))
            dve.tensor_copy(tT[p][:].rearrange("p s c -> p (s c)"), b_t[:].bitcast(F16)).then_inc(tT_sb, 1)

        def step(g, p, has):
            q = 1 - p
            if has(-1):
                mid_low(g - 1, 2, 2)
                far_low(g - 1, 3)
                residual(g - 1, q, 0)
                residual(g - 1, q, 1)
                mid_low(g - 1, 3, 0)
                residual(g - 1, q, 2)
                norm_row(L, dve, g - 1, q, 0)
            if has(0):
                copy_tT(g, p)
            if has(-1):
                norm_row(L, dve, g - 1, q, 1)
            if transpose_due(F, g + 1):
                copy_xT(K, F, dve, g + 1, q, b_xT, 0, (near_ps, GP))
            if has(-1):
                norm_row(L, dve, g - 1, q, 2)
            if transpose_due(F, g + 1):
                copy_xT(K, F, dve, g + 1, q, b_xT, 1, (near_ps, GP))
            if has(0):
                far_low(g, 0)
            if has(1):
                scores(g + 1)
            if has(-1):
                residual(g - 1, q, 3)
            if has(0):
                far_low(g, 1)
            if has(-1):
                norm_row(L, dve, g - 1, q, 3)
                norm_variance(L, dve, g - 1, q, EPS)
            if has(1):
                leaky(g + 1)
            if has(0):
                mid_low(g, 0, 0)
                far_low(g, 2)
            if has(-1):
                norm_shift(L, dve, g - 1, q)
            if has(1):
                transition(g + 1, q)
            if has(0):
                mid_low(g, 1, 1)
            if has(1):
                row_sums(g + 1)
                normalised(g + 1)
        return step, 1, 1

    def gpsimd(pool):
        def transition_low(g):
            pool.wait_ge(t_hi, upto(g, 1, 1))
            if reused(g, 1):
                pool.wait_ge(tT_ps, upto(g - 1, 1, 1))
            pool.tensor_tensor(ts[1][:], tf[:], ts[0][:], ALU.subtract).then_inc(t_lo, 1)

        def step(g, p, has):
            q = 1 - p
            if halves_due(F, g + 2):
                x_low(K, F, pool, g + 2, p)
            if has(-1):
                norm_power(K, L, pool, g - 1, q)
            if has(1):
                transition_low(g + 1)
        return step, 2, 1

    return sync, tensor, scalar, vector, gpsimd


def layer3(nc, K, ctx):
    def sb(name, shape, dt=F32):
        return ctx.enter_context(nc.sbuf_tensor(f"l3_{name}", shape, dt))

    def sem(name):
        return ctx.enter_context(nc.semaphore(f"l3_{name}"))

    bank = K.bank
    b_xT, b_s, b_t, b_xw, b_out = bank[0:2], bank[2], bank[3], (bank[4], bank[6]), (bank[7], bank[5])
    L, S = norm(nc, ctx, "l3"), attention_front(nc, K, ctx, 3, 1)
    us = [[sb(f"U{p}_{s}", [128, C], F16) for s in ("hi", "lo")] for p in range(2)]
    xw = [[sb(f"xw{p}_{s}", [128, GP, D], F16) for s in ("hi", "lo")] for p in range(2)]
    rrec, rfac = sb("rrec", [128, GP]), [sb(f"rfac{p}", [128, GP]) for p in range(2)]
    lr_ok, u_hi, u_lo, xw_ps, xw_hi, xw_lo, out_ps, rrec_ok, rfac_ok = map(
        sem, ("lr_ok", "u_hi", "u_lo", "xw_ps", "xw_hi", "xw_lo", "out_ps", "rrec_ok", "rfac_ok"))
    stored = sem("stored")
    F = front_of(K.F, 3)

    def sync(sp):
        def store(g, p, has):
            if isinstance(g, int) and g == G - 1:
                for j in range(GP):
                    sp.wait_ge(L.x_new, upto(g, GP, j + 1))
                    sp.dma_start(K.od[:, bass.ds(g * GP + j, 1), :],
                                 K.x[:, gcols(g, j)].rearrange("p (g d) -> p g d", g=1)).then_inc(stored, 16)
            elif has(0):
                sp.wait_ge(L.x_new, upto(g, GP, GP))
                sp.dma_start(K.od[:, bass.ds(g * GP, GP), :], x_group(K, g)).then_inc(stored, 16)
        over_groups(sp, store, 0, 0)
        sp.wait_ge(stored, 16 * (G - 1 + GP))

    def tensor(pe):
        def project(g, p, j):
            if j == 0 and is_first(g):
                pe.wait_ge(K.far_lo, G * GP)
            if j == 1 and is_first(g):
                pe.wait_ge(K.hr_ok, G * GP)
            if j >= 2 or reused(g, 1):
                pe.wait_ge(xw_lo, upto(g, GP, j - 1))
            c = slice(j * N, (j + 1) * N)
            for d in range(DT):
                m = triple(nc, b_xw[j % 2][:, 0:D], [s[:, d, c] for s in F.xT[p]],
                           [w[:, d, 0:D] for w in K.w3], start=d == 0, stop=d == DT - 1)
            m.then_inc(xw_ps, 1)

        def aggregate(g, p, j):
            if j == 0:
                pe.wait_ge(u_hi, upto(g, 1, 1))
                pe.wait_ge(u_lo, upto(g, 1, 1))
            pe.wait_ge(xw_hi, upto(g, GP, j + 1))
            pe.wait_ge(xw_lo, upto(g, GP, j + 1))
            if j >= 2 or reused(g, 1):
                pe.wait_ge(L.pre_ok, upto(g, GP, j - 1))
            if j == 0:
                for i in range(GP):
                    for s in (1, 0):
                        pe.matmul(b_out[0][:, D + i:D + i + 1], us[p][s][:, i * N:(i + 1) * N],
                                  K.ones16[:, 0:1], start=s == 1, stop=s == 0)
            triple(nc, b_out[j % 2][:, 0:D], [s[:, j * N:(j + 1) * N] for s in us[p]],
                   [s[:, j, :] for s in xw[p]]).then_inc(out_ps, 1)

        def step(g, p, has):
            q = 1 - p
            if has(0):
                node_scores(nc, K, F, S, pe, g, p, b_s, K.w3, D)
            if has(-1):
                project(g - 1, q, 1)
                project(g - 1, q, 2)
                aggregate(g - 1, q, 0)
            if has(0):
                spread_scores(nc, K, S, pe, g, b_t, S.t_ok, GP)
            if has(-1):
                project(g - 1, q, 3)
            if transpose_due(F, g + 1):
                transpose_x(K, F, pe, g + 1, q, b_xT, 0)
                transpose_x(K, F, pe, g + 1, q, b_xT, 1)
            if has(-1):
                aggregate(g - 1, q, 1)
                aggregate(g - 1, q, 2)
            if has(0):
                project(g, p, 0)
            if has(-1):
                aggregate(g - 1, q, 3)
        return step, 1, 1

    def scalar(act):
        def xw_high(g, p, j):
            act.wait_ge(xw_ps, upto(g, GP, j + 1))
            if reused(g):
                act.wait_ge(out_ps, upto(g - 2, GP, j + 1))
            act.activation(xw[p][0][:, j, :], b_xw[j % 2][:, 0:D], ACT.Copy).then_inc(xw_hi, 1)

        def tanh(g, j):
            if j == 0:
                act.wait_ge(S.sj_ps, upto(g, 1, 1))
                act.wait_ge(S.s_bias, upto(g, 1, 1))
                if reused(g, 1):
                    act.wait_ge(lr_ok, upto(g - 1, 1, 1))
            act.activation(S.t[:, j * N:(j + 1) * N], b_t[:, j * N:(j + 1) * N], ACT.Tanh,
                           bias=S.bias[:, j:j + 1], scale=0.125).then_inc(S.t_ok, 1)

        def exponentials(g):
            act.wait_ge(lr_ok, upto(g, 1, 1))
            if reused(g, 1):
                act.wait_ge(S.u_ok, upto(g - 1, 1, 1))
            act.activation(S.e[:], S.lr[:], ACT.Exp, scale=8.0).then_inc(S.e_ok, 1)

        def attention_high(g, p):
            act.wait_ge(S.u_ok, upto(g, 1, 1))
            if reused(g):
                act.wait_ge(out_ps, upto(g - 2, GP, GP))
            act.activation(us[p][0][:], S.u[:], ACT.Copy).then_inc(u_hi, 1)

        def step(g, p, has):
            q = 1 - p
            if has(-2):
                norm_apply(K, L, act, g - 2, p, 0)
            if has(0):
                tanh(g, 0)
                tanh(g, 1)
            if has(-1):
                xw_high(g - 1, q, 3)
            if has(0):
                tanh(g, 2)
                tanh(g, 3)
            if has(-2):
                norm_apply(K, L, act, g - 2, p, 1)
            if halves_due(F, g + 2):
                x_high(K, F, L, act, g + 2, p)
            if has(-2):
                norm_apply(K, L, act, g - 2, p, 2)
            if has(0):
                exponentials(g)
                xw_high(g, p, 0)
                attention_high(g, p)
                xw_high(g, p, 1)
            if has(-2):
                norm_apply(K, L, act, g - 2, p, 3)
            if has(0):
                xw_high(g, p, 2)
        return step, 2, 2

    def vector(dve):
        def xw_low(g, p, j):
            dve.wait_ge(xw_hi, upto(g, GP, j + 1))
            if reused(g):
                dve.wait_ge(out_ps, upto(g - 2, GP, j + 1))
            dve.tensor_tensor(xw[p][1][:, j, :], b_xw[j % 2][:, 0:D], xw[p][0][:, j, :],
                              ALU.subtract).then_inc(xw_lo, 1)

        def scores(g):
            split_scores(S, dve, g, b_s)
            if reused(g, 1):
                dve.wait_ge(S.t_ok, upto(g - 1, GP, GP))
            dve.tensor_scalar(S.bias[:], b_s[:, 0:GP], 0.125, None, ALU.mult).then_inc(S.s_bias, 1)

        def leaky(g):
            dve.wait_ge(S.t_ok, upto(g, GP, GP))
            if reused(g, 1):
                dve.wait_ge(S.e_ok, upto(g - 1, 1, 1))
            dve.scalar_tensor_tensor(S.lr[:], S.t[:], 0.1, S.t[:], ALU.mult, ALU.max).then_inc(lr_ok, 1)

        def row_factors(g, p):
            dve.wait_ge(out_ps, upto(g, GP, 1))
            dve.reciprocal(rrec[:], b_out[0][:, D:D + GP]).then_inc(rrec_ok, 1)
            dve.wait_ge(rrec_ok, upto(g, 1, 1))
            dve.scalar_tensor_tensor(rfac[p][:], rrec[:], 1.0 / W3_SCALE, K.asum[:, bass.ds(g * GP, GP)],
                                     ALU.mult, ALU.mult).then_inc(rfac_ok, 1)

        def residual(g, p, j):
            if j == 0 and is_first(g):
                dve.wait_ge(K.x_new[2], G * GP)
            dve.wait_ge(out_ps, upto(g, GP, j + 1))
            dve.wait_ge(rfac_ok, upto(g, 1, 1))
            pre_free(L, dve, g)
            dve.scalar_tensor_tensor(L.pre[p][:, j, :], b_out[j % 2][:, 0:D], rfac[p][:, j:j + 1],
                                     K.x[:, gcols(g, j)], ALU.mult, ALU.add).then_inc(L.pre_ok, 1)

        def step(g, p, has):
            q = 1 - p
            if has(-1):
                residual(g - 1, q, 3)
                norm_row(L, dve, g - 1, q, 2)
                norm_row(L, dve, g - 1, q, 3)
            if has(0):
                xw_low(g, p, 0)
            if has(-1):
                norm_variance(L, dve, g - 1, q, EPS)
            if has(1):
                scores(g + 1)
            if has(0):
                xw_low(g, p, 1)
            if has(-1):
                norm_shift(L, dve, g - 1, q)
            if has(0):
                row_factors(g, p)
                xw_low(g, p, 2)
            if transpose_due(F, g + 2):
                copy_xT(K, F, dve, g + 2, p, b_xT, 0, (xw_ps, GP))
            if has(0):
                xw_low(g, p, 3)
            if has(1):
                leaky(g + 1)
            if has(0):
                residual(g, p, 0)
                residual(g, p, 1)
            if transpose_due(F, g + 2):
                copy_xT(K, F, dve, g + 2, p, b_xT, 1, (xw_ps, GP))
            if has(0):
                norm_row(L, dve, g, p, 0)
                norm_row(L, dve, g, p, 1)
                residual(g, p, 2)
        return step, 2, 1

    def gpsimd(pool):
        def attention(g):
            pool.wait_ge(S.e_ok, upto(g, 1, 1))
            if reused(g, 1):
                pool.wait_ge(u_hi, upto(g - 1, 1, 1))
            pool.tensor_tensor(S.u[:], S.e[:], K.at[:, acols(g)], ALU.mult).then_inc(S.u_ok, 1)

        def attention_low(g, p):
            pool.wait_ge(u_hi, upto(g, 1, 1))
            if reused(g):
                pool.wait_ge(out_ps, upto(g - 2, GP, GP))
            pool.tensor_tensor(us[p][1][:], S.u[:], us[p][0][:], ALU.subtract).then_inc(u_lo, 1)

        def step(g, p, has):
            q = 1 - p
            if has(0):
                attention_low(g, p)
            if has(-1):
                norm_power(K, L, pool, g - 1, q)
            if halves_due(F, g + 2):
                x_low(K, F, pool, g + 2, p)
            if has(1):
                attention(g + 1)
        return step, 2, 1

    return sync, tensor, scalar, vector, gpsimd


_INS = ['x', 'adj', 'L0_gnn_W1', 'L0_gnn_b1', 'L0_gnn_gamma', 'L0_gnn_beta', 'L0_gnn_W2', 'L0_gnn_b2',
        'L1_gnn_W_qk', 'L1_gnn_W_v', 'L2_gnn_Wv', 'L2_gnn_bv', 'L2_gnn_aw', 'L2_gnn_ab', 'L2_gnn_Wk',
        'L2_gnn_bk', 'L3_gnn_w', 'L3_gnn_a']


def kernel(**inputs):
    import concourse.bacc as bacc
    from concourse.bass_utils import run_bass_kernel_spmd

    nc = bacc.Bacc("TRN2", target_bir_lowering=False, num_devices=1)
    arrays, args = {}, []
    for name in _INS:
        a = np.ascontiguousarray(inputs[name])
        arrays[f"in_{name}"] = a
        args.append(nc.dram_tensor(f"in_{name}", a.shape, mybir.dt.from_np(a.dtype), kind="ExternalInput").ap())
    out = nc.dram_tensor("out", (GRAPHS, N, D), F32, kind="ExternalOutput").ap()
    build(nc, *args, out)
    r = run_bass_kernel_spmd(nc, [arrays], core_ids=[0])
    return r.results[0]["out"]
```
